# Optimizing a Trainium2 kernel written in Bass

```python
import numpy as np
import jax
import jax.numpy as jnp

def _softmax(x, axis=-1):
    return jax.nn.softmax(x, axis=axis)

def _gelu(x):
    return jax.nn.gelu(x, approximate=True)

def _silu(x):
    return jax.nn.silu(x)

def _sigmoid(x):
    return jax.nn.sigmoid(x)

def _layernorm(x, axis=-1, eps=1e-05):
    m = jnp.mean(x, axis=axis, keepdims=True)
    v = jnp.var(x, axis=axis, keepdims=True)
    return (x - m) / jnp.sqrt(v + eps)

def _scatter_add(tgt, idx, src, axis=0):
    return tgt.at[idx].add(src)

def _segment_sum(src, seg, n):
    return jax.ops.segment_sum(src, seg, n)
kernel_name = 'mk_xattn_seq_d4_seqx_r8_76f3bd'

def setup_inputs(seed: int=0):
    np.random.seed(seed)
    _w = jnp.asarray

    def _rec_inputs():
        import jax
        import jax.numpy as jnp
        _rk = jax.random.key(seed)
        x = -0.0005146 + 1 * jax.random.normal(jax.random.fold_in(_rk, 1), (64, 64, 256), jnp.float32)
        _lenS = 64 - jax.random.randint(jax.random.fold_in(_rk, 7), (64,), 0, max(1, 64 // 4) + 1, jnp.int32)
        _lenS2 = 64 - jax.random.randint(jax.random.fold_in(_rk, 8), (64,), 0, max(1, 64 // 4) + 1, jnp.int32)
        _ctx_2048P = jax.random.normal(jax.random.fold_in(_rk, 11), (64, 16, 256), jnp.float32)
        _ctx_2048c = jax.random.dirichlet(jax.random.fold_in(_rk, 511), 0.3 * jnp.ones((16,), jnp.float32), (64, 64))
        _ctx_2048t = jnp.einsum('bsk,bkd->bsd', _ctx_2048c, _ctx_2048P)
        _ctx_2048t = _ctx_2048t * jax.lax.rsqrt(jnp.mean(jnp.square(_ctx_2048t)) + 1e-12) * 0.953939
        ctx_2048 = -0.000392918 + 0.999932 * (_ctx_2048t + 0.3 * jax.random.normal(jax.random.fold_in(_rk, 611), (64, 64, 256), jnp.float32))
        _validS = jnp.arange(64)[None, :] < _lenS[:, None]
        _validS2 = jnp.arange(64)[None, :] < _lenS2[:, None]
        _causal = jnp.tril(jnp.ones((64, 64), dtype=bool))
        mask_BxS2_ik0 = jnp.where(jnp.broadcast_to(_validS2[:, :], (64, 64)), 0, 1).astype(jnp.int32)
        mask_Bx1xSxS2_ff0 = jnp.where(jnp.ones((64, 1, 64, 64), dtype=bool), 0.0, -1000000000.0).astype(jnp.float32)
        return (x, ctx_2048, mask_BxS2_ik0, mask_Bx1xSxS2_ff0)
    x, ctx_2048, mask_BxS2_ik0, mask_Bx1xSxS2_ff0 = _rec_inputs()

    def _L0_xattn_setup():
        import jax, jax.numpy as jnp
        import numpy as np
        B, P, K, H, NH = (4, 256, 32, 256, 16)
        DH = H // NH
        EPS = 1e-06

        def rmsnorm(x, w):
            var = jnp.mean(jnp.square(x), axis=-1, keepdims=True)
            return x * jax.lax.rsqrt(var + EPS) * w
        key = jax.random.key(seed)
        ks = jax.random.split(key, 12)
        s = 0.02
        return {'x': jax.random.normal(ks[0], (B, P, H), jnp.float32), 'latents': jax.random.normal(ks[1], (B, K, H), jnp.float32), 'attention_mask': jax.random.randint(ks[2], (B, P), 0, 2, jnp.int32), 'q_w': s * jax.random.normal(ks[3], (H, H), jnp.float32), 'q_b': jnp.zeros((H,), jnp.float32), 'kv_w': s * jax.random.normal(ks[4], (H, 2 * H), jnp.float32), 'kv_b': jnp.zeros((2 * H,), jnp.float32), 'out_w': s * jax.random.normal(ks[5], (H, H), jnp.float32), 'out_b': jnp.zeros((H,), jnp.float32), 'postnorm_w': jnp.ones((H,), jnp.float32), 'mlp_w1': s * jax.random.normal(ks[6], (H, 4 * H), jnp.float32), 'mlp_b1': jnp.zeros((4 * H,), jnp.float32), 'mlp_w2': s * jax.random.normal(ks[7], (4 * H, H), jnp.float32), 'mlp_b2': jnp.zeros((H,), jnp.float32)}
    _L0_xattn_all = _L0_xattn_setup()
    _L0_xattn_in = {k: v for k, v in _L0_xattn_all.items() if k in ('q_w', 'q_b', 'kv_w', 'kv_b', 'out_w', 'out_b', 'postnorm_w', 'mlp_w1', 'mlp_b1', 'mlp_w2', 'mlp_b2')}
    del _L0_xattn_all

    def _L1_xattn_setup():
        import jax, jax.numpy as jnp
        import numpy as np
        E, H, L, B = (256, 32, 128, 4)
        S = E // H
        DM, DD = (32, 64)

        def _ln(x, w, b, eps=1e-05):
            m = x.mean(-1, keepdims=True)
            v = ((x - m) ** 2).mean(-1, keepdims=True)
            return (x - m) / jnp.sqrt(v + eps) * w + b

        def _block(x, state, ln1_w, ln1_b, ln2_w, ln2_b, maa_x, maa_w1, maa_w2, maa_stack, time_decay, td_w1, td_w2, u, Wr, Wk, Wv, Wg, Wo, gn_w, gn_b, ffn_maa_k, ffn_maa_r, Wfk, Wfr, Wfv):
            b, l, e = x.shape
            h = u.shape[0]
            s_ = e // h
            xa = _ln(x, ln1_w, ln1_b)
            sx = jnp.concatenate([state[:, 1:2] - xa[:, :1], xa[:, :-1] - xa[:, 1:]], axis=1)
            xxx = jnp.tanh((xa + sx * maa_x) @ maa_w1).reshape(b, l, 5, DM)
            xxx = jnp.einsum('blfd,fde->blfe', xxx, maa_w2)
            xm = xa[:, :, None] + sx[:, :, None] * (maa_stack + xxx)
            xk, xw, xv, xr, xg = (xm[:, :, j] for j in range(5))
            w = jnp.exp(-jnp.exp(time_decay + jnp.tanh(xw @ td_w1) @ td_w2)).reshape(b, l, h, s_)
            r = (xr @ Wr.T).reshape(b, l, h, s_)
            k = (xk @ Wk.T).reshape(b, l, h, s_)
            v = (xv @ Wv.T).reshape(b, l, h, s_)
            g = jax.nn.silu(xg @ Wg.T)
            s0 = state[:, 2:2 + s_].reshape(b, h, s_, s_)

            def step(s, rkvw):
                r_t, k_t, v_t, w_t = rkvw
                a = k_t[..., :, None] * v_t[..., None, :]
                out = jnp.einsum('bhi,bhij->bhj', r_t, u * a + s)
                s = a + w_t[..., :, None] * s
                return (s, out)
            rkvw = tuple((jnp.moveaxis(t, 1, 0) for t in (r, k, v, w)))
            _, out = jax.lax.scan(step, s0, rkvw)
            out = jnp.moveaxis(out, 0, 1).reshape(b, l, e)
            og = out.reshape(b, l, h, s_)
            m = og.mean(-1, keepdims=True)
            va = ((og - m) ** 2).mean(-1, keepdims=True)
            og = ((og - m) / jnp.sqrt(va + 1e-05)).reshape(b, l, e) * gn_w + gn_b
            x1 = x + og * g @ Wo.T
            xc = _ln(x1, ln2_w, ln2_b)
            sx2 = jnp.concatenate([state[:, 0:1] - xc[:, :1], xc[:, :-1] - xc[:, 1:]], axis=1)
            xk2 = xc + sx2 * ffn_maa_k
            xr2 = xc + sx2 * ffn_maa_r
            rr = jax.nn.sigmoid(xr2 @ Wfr.T)
            kk = jnp.square(jax.nn.relu(xk2 @ Wfk.T))
            return x1 + rr * (kk @ Wfv.T)
        key = jax.random.key(seed)
        ks = jax.random.split(key, 24)
        sc = 0.02
        d = {'x': jax.random.normal(ks[0], (B, L, E), jnp.float32), 'state': jax.random.normal(ks[1], (B, 2 + S, E), jnp.float32) * 0.1, 'ln1_w': jnp.ones((E,), jnp.float32), 'ln1_b': jnp.zeros((E,), jnp.float32), 'ln2_w': jnp.ones((E,), jnp.float32), 'ln2_b': jnp.zeros((E,), jnp.float32), 'maa_x': jax.random.normal(ks[2], (E,), jnp.float32) * 0.1, 'maa_w1': jax.random.normal(ks[3], (E, 5 * DM), jnp.float32) * sc, 'maa_w2': jax.random.normal(ks[4], (5, DM, E), jnp.float32) * sc, 'maa_stack': jax.random.normal(ks[5], (1, 5, E), jnp.float32) * 0.1, 'time_decay': jax.random.normal(ks[6], (E,), jnp.float32) * 0.5, 'td_w1': jax.random.normal(ks[7], (E, DD), jnp.float32) * sc, 'td_w2': jax.random.normal(ks[8], (DD, E), jnp.float32) * sc, 'u': jax.random.normal(ks[9], (H, S, 1), jnp.float32) * 0.1, 'Wr': jax.random.normal(ks[10], (E, E), jnp.float32) * sc, 'Wk': jax.random.normal(ks[11], (E, E), jnp.float32) * sc, 'Wv': jax.random.normal(ks[12], (E, E), jnp.float32) * sc, 'Wg': jax.random.normal(ks[13], (E, E), jnp.float32) * sc, 'Wo': jax.random.normal(ks[14], (E, E), jnp.float32) * sc, 'gn_w': jnp.ones((E,), jnp.float32), 'gn_b': jnp.zeros((E,), jnp.float32), 'ffn_maa_k': jax.random.normal(ks[15], (E,), jnp.float32) * 0.1, 'ffn_maa_r': jax.random.normal(ks[16], (E,), jnp.float32) * 0.1, 'Wfk': jax.random.normal(ks[17], (E, E), jnp.float32) * sc, 'Wfr': jax.random.normal(ks[18], (E, E), jnp.float32) * sc, 'Wfv': jax.random.normal(ks[19], (E, E), jnp.float32) * sc}
        return d
    _L1_xattn_all = _L1_xattn_setup()
    _L1_xattn_in = {k: v for k, v in _L1_xattn_all.items() if k in ('ln1_w', 'ln1_b', 'ln2_w', 'ln2_b', 'maa_x', 'maa_w1', 'maa_w2', 'maa_stack', 'time_decay', 'td_w1', 'td_w2', 'u', 'Wr', 'Wk', 'Wv', 'Wg', 'Wo', 'gn_w', 'gn_b', 'ffn_maa_k', 'ffn_maa_r', 'Wfk', 'Wfr', 'Wfv')}
    del _L1_xattn_all

    def _L2_xattn_setup():
        import jax, jax.numpy as jnp
        import numpy as np
        H = 256
        B, L, S = (4, 512, 10)
        key = jax.random.key(seed)
        k1, k2, k3, k4, k5, k6 = jax.random.split(key, 6)
        scale = 1.0 / np.sqrt(H)
        return {'h_english': jax.random.normal(k1, (B, L, H), dtype=jnp.float32), 'h_lojban': jax.random.normal(k2, (B, S, H), dtype=jnp.float32), 'w_q': jax.random.normal(k3, (H, H), dtype=jnp.float32) * scale, 'w_k': jax.random.normal(k4, (H, H), dtype=jnp.float32) * scale, 'w_v': jax.random.normal(k5, (H, H), dtype=jnp.float32) * scale, 'w_o': jax.random.normal(k6, (H, H), dtype=jnp.float32) * scale, 'alpha': jnp.float32(0.1)}
    _L2_xattn_all = _L2_xattn_setup()
    _L2_xattn_in = {k: v for k, v in _L2_xattn_all.items() if k in ('w_q', 'w_k', 'w_v', 'w_o', 'alpha')}
    del _L2_xattn_all

    def _L3_xattn_setup():
        import jax, jax.numpy as jnp
        import numpy as np
        H = 256
        NH = 32
        KVH = 8
        HD = H // NH
        GROUPS = NH // KVH
        EPS = 1e-06
        B, L, S = (4, 128, 128)

        def _gqa_forward(hidden_state, encoder_hidden_state, encoder_attention_mask, Wq, bq, Wk, bk, Wv, bv, Wo, bo, gamma, beta):
            b, l, _ = hidden_state.shape
            s = encoder_hidden_state.shape[1]
            q = hidden_state @ Wq + bq
            k = encoder_hidden_state @ Wk + bk
            v = encoder_hidden_state @ Wv + bv
            q = q.reshape(b, l, KVH, GROUPS, HD).transpose(0, 2, 3, 1, 4)
            k = k.reshape(b, s, KVH, HD).transpose(0, 2, 1, 3)
            v = v.reshape(b, s, KVH, HD).transpose(0, 2, 1, 3)
            scale = 1.0 / jnp.sqrt(jnp.asarray(HD, q.dtype))
            scores = jnp.einsum('bkgld,bksd->bkgls', q, k) * scale
            scores = scores + encoder_attention_mask[:, :, None, :, :]
            attn = jax.nn.softmax(scores, axis=-1)
            out = jnp.einsum('bkgls,bksd->bkgld', attn, v)
            out = out.transpose(0, 3, 1, 2, 4).reshape(b, l, H)
            out = out @ Wo + bo
            x = out + hidden_state
            mu = jnp.mean(x, axis=-1, keepdims=True)
            var = jnp.var(x, axis=-1, keepdims=True)
            return (x - mu) * jax.lax.rsqrt(var + EPS) * gamma + beta
        key = jax.random.key(seed)
        ks = jax.random.split(key, 12)
        sd = 0.02
        return {'hidden_state': jax.random.normal(ks[0], (B, L, H), jnp.float32), 'encoder_hidden_state': jax.random.normal(ks[1], (B, S, H), jnp.float32), 'encoder_attention_mask': jnp.zeros((B, 1, L, S), jnp.float32), 'Wq': jax.random.normal(ks[2], (H, H), jnp.float32) * sd, 'bq': jnp.zeros((H,), jnp.float32), 'Wk': jax.random.normal(ks[3], (H, KVH * HD), jnp.float32) * sd, 'bk': jnp.zeros((KVH * HD,), jnp.float32), 'Wv': jax.random.normal(ks[4], (H, KVH * HD), jnp.float32) * sd, 'bv': jnp.zeros((KVH * HD,), jnp.float32), 'Wo': jax.random.normal(ks[5], (H, H), jnp.float32) * sd, 'bo': jnp.zeros((H,), jnp.float32), 'gamma': jnp.ones((H,), jnp.float32), 'beta': jnp.zeros((H,), jnp.float32)}
    _L3_xattn_all = _L3_xattn_setup()
    _L3_xattn_in = {k: v for k, v in _L3_xattn_all.items() if k in ('Wq', 'bq', 'Wk', 'bk', 'Wv', 'bv', 'Wo', 'bo', 'gamma', 'beta')}
    del _L3_xattn_all
    return {'x': x, 'ctx_2048': ctx_2048, 'mask_BxS2_ik0': mask_BxS2_ik0, 'mask_Bx1xSxS2_ff0': mask_Bx1xSxS2_ff0, 'L0_xattn_q_w': _L0_xattn_in['q_w'], 'L0_xattn_q_b': _L0_xattn_in['q_b'], 'L0_xattn_kv_w': _L0_xattn_in['kv_w'], 'L0_xattn_kv_b': _L0_xattn_in['kv_b'], 'L0_xattn_out_w': _L0_xattn_in['out_w'], 'L0_xattn_out_b': _L0_xattn_in['out_b'], 'L0_xattn_postnorm_w': _L0_xattn_in['postnorm_w'], 'L0_xattn_mlp_w1': _L0_xattn_in['mlp_w1'], 'L0_xattn_mlp_b1': _L0_xattn_in['mlp_b1'], 'L0_xattn_mlp_w2': _L0_xattn_in['mlp_w2'], 'L0_xattn_mlp_b2': _L0_xattn_in['mlp_b2'], 'L1_xattn_ln1_w': _L1_xattn_in['ln1_w'], 'L1_xattn_ln1_b': _L1_xattn_in['ln1_b'], 'L1_xattn_ln2_w': _L1_xattn_in['ln2_w'], 'L1_xattn_ln2_b': _L1_xattn_in['ln2_b'], 'L1_xattn_maa_x': _L1_xattn_in['maa_x'], 'L1_xattn_maa_w1': _L1_xattn_in['maa_w1'], 'L1_xattn_maa_w2': _L1_xattn_in['maa_w2'], 'L1_xattn_maa_stack': _L1_xattn_in['maa_stack'], 'L1_xattn_time_decay': _L1_xattn_in['time_decay'], 'L1_xattn_td_w1': _L1_xattn_in['td_w1'], 'L1_xattn_td_w2': _L1_xattn_in['td_w2'], 'L1_xattn_u': _L1_xattn_in['u'], 'L1_xattn_Wr': _L1_xattn_in['Wr'], 'L1_xattn_Wk': _L1_xattn_in['Wk'], 'L1_xattn_Wv': _L1_xattn_in['Wv'], 'L1_xattn_Wg': _L1_xattn_in['Wg'], 'L1_xattn_Wo': _L1_xattn_in['Wo'], 'L1_xattn_gn_w': _L1_xattn_in['gn_w'], 'L1_xattn_gn_b': _L1_xattn_in['gn_b'], 'L1_xattn_ffn_maa_k': _L1_xattn_in['ffn_maa_k'], 'L1_xattn_ffn_maa_r': _L1_xattn_in['ffn_maa_r'], 'L1_xattn_Wfk': _L1_xattn_in['Wfk'], 'L1_xattn_Wfr': _L1_xattn_in['Wfr'], 'L1_xattn_Wfv': _L1_xattn_in['Wfv'], 'L2_xattn_w_q': _L2_xattn_in['w_q'], 'L2_xattn_w_k': _L2_xattn_in['w_k'], 'L2_xattn_w_v': _L2_xattn_in['w_v'], 'L2_xattn_w_o': _L2_xattn_in['w_o'], 'L2_xattn_alpha': _L2_xattn_in['alpha'], 'L3_xattn_Wq': _L3_xattn_in['Wq'], 'L3_xattn_bq': _L3_xattn_in['bq'], 'L3_xattn_Wk': _L3_xattn_in['Wk'], 'L3_xattn_bk': _L3_xattn_in['bk'], 'L3_xattn_Wv': _L3_xattn_in['Wv'], 'L3_xattn_bv': _L3_xattn_in['bv'], 'L3_xattn_Wo': _L3_xattn_in['Wo'], 'L3_xattn_bo': _L3_xattn_in['bo'], 'L3_xattn_gamma': _L3_xattn_in['gamma'], 'L3_xattn_beta': _L3_xattn_in['beta']}

def reference(x, ctx_2048, mask_BxS2_ik0, mask_Bx1xSxS2_ff0, L0_xattn_q_w, L0_xattn_q_b, L0_xattn_kv_w, L0_xattn_kv_b, L0_xattn_out_w, L0_xattn_out_b, L0_xattn_postnorm_w, L0_xattn_mlp_w1, L0_xattn_mlp_b1, L0_xattn_mlp_w2, L0_xattn_mlp_b2, L1_xattn_ln1_w, L1_xattn_ln1_b, L1_xattn_ln2_w, L1_xattn_ln2_b, L1_xattn_maa_x, L1_xattn_maa_w1, L1_xattn_maa_w2, L1_xattn_maa_stack, L1_xattn_time_decay, L1_xattn_td_w1, L1_xattn_td_w2, L1_xattn_u, L1_xattn_Wr, L1_xattn_Wk, L1_xattn_Wv, L1_xattn_Wg, L1_xattn_Wo, L1_xattn_gn_w, L1_xattn_gn_b, L1_xattn_ffn_maa_k, L1_xattn_ffn_maa_r, L1_xattn_Wfk, L1_xattn_Wfr, L1_xattn_Wfv, L2_xattn_w_q, L2_xattn_w_k, L2_xattn_w_v, L2_xattn_w_o, L2_xattn_alpha, L3_xattn_Wq, L3_xattn_bq, L3_xattn_Wk, L3_xattn_bk, L3_xattn_Wv, L3_xattn_bv, L3_xattn_Wo, L3_xattn_bo, L3_xattn_gamma, L3_xattn_beta):
    import jax
    import jax.numpy as jnp

    def _L0_xattn_ref(x, latents, attention_mask, q_w, q_b, kv_w, kv_b, out_w, out_b, postnorm_w, mlp_w1, mlp_b1, mlp_w2, mlp_b2):
        import jax, jax.numpy as jnp
        import numpy as np
        B, P, K, H, NH = (4, 256, 32, 256, 16)
        DH = H // NH
        EPS = 1e-06

        def rmsnorm(x, w):
            var = jnp.mean(jnp.square(x), axis=-1, keepdims=True)
            return x * jax.lax.rsqrt(var + EPS) * w
        b, p, _ = x.shape
        k_len = latents.shape[1]
        residual = latents
        h = jnp.concatenate([x, latents], axis=1)
        q = (latents @ q_w + q_b).reshape(b, k_len, NH, DH)
        kv = (h @ kv_w + kv_b).reshape(b, p + k_len, NH, DH, 2)
        kmat, v = (kv[..., 0], kv[..., 1])
        attn = jnp.einsum('bkhd,bnhd->bhkn', q, kmat) / DH
        full_mask = jnp.concatenate([attention_mask.astype(bool), jnp.ones((b, k_len), bool)], axis=-1)
        attn = jnp.where(full_mask[:, None, None, :], attn, -jnp.inf)
        attn = jax.nn.softmax(attn.astype(jnp.float32), axis=-1).astype(q.dtype)
        attn_out = jnp.einsum('bhkn,bnhd->bkhd', attn, v).reshape(b, k_len, H)
        attn_out = attn_out @ out_w + out_b + residual
        out = rmsnorm(attn_out, postnorm_w)
        out = jax.nn.gelu(out @ mlp_w1 + mlp_b1) @ mlp_w2 + mlp_b2
        return out + residual

    def _L1_xattn_ref(x, state, ln1_w, ln1_b, ln2_w, ln2_b, maa_x, maa_w1, maa_w2, maa_stack, time_decay, td_w1, td_w2, u, Wr, Wk, Wv, Wg, Wo, gn_w, gn_b, ffn_maa_k, ffn_maa_r, Wfk, Wfr, Wfv):
        import jax, jax.numpy as jnp
        import numpy as np
        E, H, L, B = (256, 32, 128, 4)
        S = E // H
        DM, DD = (32, 64)

        def _ln(x, w, b, eps=1e-05):
            m = x.mean(-1, keepdims=True)
            v = ((x - m) ** 2).mean(-1, keepdims=True)
            return (x - m) / jnp.sqrt(v + eps) * w + b

        def _block(x, state, ln1_w, ln1_b, ln2_w, ln2_b, maa_x, maa_w1, maa_w2, maa_stack, time_decay, td_w1, td_w2, u, Wr, Wk, Wv, Wg, Wo, gn_w, gn_b, ffn_maa_k, ffn_maa_r, Wfk, Wfr, Wfv):
            b, l, e = x.shape
            h = u.shape[0]
            s_ = e // h
            xa = _ln(x, ln1_w, ln1_b)
            sx = jnp.concatenate([state[:, 1:2] - xa[:, :1], xa[:, :-1] - xa[:, 1:]], axis=1)
            xxx = jnp.tanh((xa + sx * maa_x) @ maa_w1).reshape(b, l, 5, DM)
            xxx = jnp.einsum('blfd,fde->blfe', xxx, maa_w2)
            xm = xa[:, :, None] + sx[:, :, None] * (maa_stack + xxx)
            xk, xw, xv, xr, xg = (xm[:, :, j] for j in range(5))
            w = jnp.exp(-jnp.exp(time_decay + jnp.tanh(xw @ td_w1) @ td_w2)).reshape(b, l, h, s_)
            r = (xr @ Wr.T).reshape(b, l, h, s_)
            k = (xk @ Wk.T).reshape(b, l, h, s_)
            v = (xv @ Wv.T).reshape(b, l, h, s_)
            g = jax.nn.silu(xg @ Wg.T)
            s0 = state[:, 2:2 + s_].reshape(b, h, s_, s_)

            def step(s, rkvw):
                r_t, k_t, v_t, w_t = rkvw
                a = k_t[..., :, None] * v_t[..., None, :]
                out = jnp.einsum('bhi,bhij->bhj', r_t, u * a + s)
                s = a + w_t[..., :, None] * s
                return (s, out)
            rkvw = tuple((jnp.moveaxis(t, 1, 0) for t in (r, k, v, w)))
            _, out = jax.lax.scan(step, s0, rkvw)
            out = jnp.moveaxis(out, 0, 1).reshape(b, l, e)
            og = out.reshape(b, l, h, s_)
            m = og.mean(-1, keepdims=True)
            va = ((og - m) ** 2).mean(-1, keepdims=True)
            og = ((og - m) / jnp.sqrt(va + 1e-05)).reshape(b, l, e) * gn_w + gn_b
            x1 = x + og * g @ Wo.T
            xc = _ln(x1, ln2_w, ln2_b)
            sx2 = jnp.concatenate([state[:, 0:1] - xc[:, :1], xc[:, :-1] - xc[:, 1:]], axis=1)
            xk2 = xc + sx2 * ffn_maa_k
            xr2 = xc + sx2 * ffn_maa_r
            rr = jax.nn.sigmoid(xr2 @ Wfr.T)
            kk = jnp.square(jax.nn.relu(xk2 @ Wfk.T))
            return x1 + rr * (kk @ Wfv.T)
        return _block(x, state, ln1_w, ln1_b, ln2_w, ln2_b, maa_x, maa_w1, maa_w2, maa_stack, time_decay, td_w1, td_w2, u, Wr, Wk, Wv, Wg, Wo, gn_w, gn_b, ffn_maa_k, ffn_maa_r, Wfk, Wfr, Wfv)

    def _L2_xattn_ref(h_english, h_lojban, w_q, w_k, w_v, w_o, alpha):
        import jax, jax.numpy as jnp
        import numpy as np
        H = 256
        B, L, S = (4, 512, 10)
        h = h_english.shape[-1]
        q = jnp.einsum('blh,oh->blo', h_english, w_q)
        k = jnp.einsum('bsh,oh->bso', h_lojban, w_k)
        v = jnp.einsum('bsh,oh->bso', h_lojban, w_v)
        scores = jnp.einsum('blh,bsh->bls', q, k) / jnp.sqrt(jnp.float32(h))
        probs = jax.nn.softmax(scores, axis=-1)
        context = jnp.einsum('bls,bsh->blh', probs, v)
        delta = jnp.einsum('blh,oh->blo', context, w_o)
        return h_english + alpha * delta

    def _L3_xattn_ref(hidden_state, encoder_hidden_state, encoder_attention_mask, Wq, bq, Wk, bk, Wv, bv, Wo, bo, gamma, beta):
        import jax, jax.numpy as jnp
        import numpy as np
        H = 256
        NH = 32
        KVH = 8
        HD = H // NH
        GROUPS = NH // KVH
        EPS = 1e-06
        B, L, S = (4, 128, 128)

        def _gqa_forward(hidden_state, encoder_hidden_state, encoder_attention_mask, Wq, bq, Wk, bk, Wv, bv, Wo, bo, gamma, beta):
            b, l, _ = hidden_state.shape
            s = encoder_hidden_state.shape[1]
            q = hidden_state @ Wq + bq
            k = encoder_hidden_state @ Wk + bk
            v = encoder_hidden_state @ Wv + bv
            q = q.reshape(b, l, KVH, GROUPS, HD).transpose(0, 2, 3, 1, 4)
            k = k.reshape(b, s, KVH, HD).transpose(0, 2, 1, 3)
            v = v.reshape(b, s, KVH, HD).transpose(0, 2, 1, 3)
            scale = 1.0 / jnp.sqrt(jnp.asarray(HD, q.dtype))
            scores = jnp.einsum('bkgld,bksd->bkgls', q, k) * scale
            scores = scores + encoder_attention_mask[:, :, None, :, :]
            attn = jax.nn.softmax(scores, axis=-1)
            out = jnp.einsum('bkgls,bksd->bkgld', attn, v)
            out = out.transpose(0, 3, 1, 2, 4).reshape(b, l, H)
            out = out @ Wo + bo
            x = out + hidden_state
            mu = jnp.mean(x, axis=-1, keepdims=True)
            var = jnp.var(x, axis=-1, keepdims=True)
            return (x - mu) * jax.lax.rsqrt(var + EPS) * gamma + beta
        return _gqa_forward(hidden_state, encoder_hidden_state, encoder_attention_mask, Wq, bq, Wk, bk, Wv, bv, Wo, bo, gamma, beta)
    x = _L0_xattn_ref(ctx_2048, x, mask_BxS2_ik0, L0_xattn_q_w, L0_xattn_q_b, L0_xattn_kv_w, L0_xattn_kv_b, L0_xattn_out_w, L0_xattn_out_b, L0_xattn_postnorm_w, L0_xattn_mlp_w1, L0_xattn_mlp_b1, L0_xattn_mlp_w2, L0_xattn_mlp_b2)
    x = _L1_xattn_ref(x, ctx_2048, L1_xattn_ln1_w, L1_xattn_ln1_b, L1_xattn_ln2_w, L1_xattn_ln2_b, L1_xattn_maa_x, L1_xattn_maa_w1, L1_xattn_maa_w2, L1_xattn_maa_stack, L1_xattn_time_decay, L1_xattn_td_w1, L1_xattn_td_w2, L1_xattn_u, L1_xattn_Wr, L1_xattn_Wk, L1_xattn_Wv, L1_xattn_Wg, L1_xattn_Wo, L1_xattn_gn_w, L1_xattn_gn_b, L1_xattn_ffn_maa_k, L1_xattn_ffn_maa_r, L1_xattn_Wfk, L1_xattn_Wfr, L1_xattn_Wfv)
    x = _L2_xattn_ref(x, ctx_2048, L2_xattn_w_q, L2_xattn_w_k, L2_xattn_w_v, L2_xattn_w_o, L2_xattn_alpha)
    x = _L3_xattn_ref(x, ctx_2048, mask_Bx1xSxS2_ff0, L3_xattn_Wq, L3_xattn_bq, L3_xattn_Wk, L3_xattn_bk, L3_xattn_Wv, L3_xattn_bv, L3_xattn_Wo, L3_xattn_bo, L3_xattn_gamma, L3_xattn_beta)
    return x

_drawn_inputs = setup_inputs


def setup_inputs(seed=0):
    import zlib

    import numpy as np

    out = dict(_drawn_inputs(seed))
    spreads = {'L0_xattn_q_b': (0.0, 0.8),
     'L0_xattn_kv_b': (0.0, 0.8),
     'L0_xattn_out_b': (0.0, 0.666),
     'L0_xattn_postnorm_w': (1.0, 0.6),
     'L0_xattn_mlp_b1': (0.0, 0.1),
     'L0_xattn_mlp_b2': (0.0, 0.1),
     'L1_xattn_ln1_w': (1.0, 0.6),
     'L1_xattn_ln1_b': (0.0, 0.58),
     'L1_xattn_ln2_w': (1.0, 0.6),
     'L1_xattn_ln2_b': (0.0, 0.8),
     'L1_xattn_gn_w': (1.0, 0.6),
     'L1_xattn_gn_b': (0.0, 0.8),
     'L3_xattn_bq': (0.0, 2.0),
     'L3_xattn_bk': (0.0, 2.0),
     'L3_xattn_bv': (0.0, 0.272),
     'L3_xattn_bo': (0.0, 0.1),
     'L3_xattn_gamma': (1.0, 0.2),
     'L3_xattn_beta': (0.0, 0.1)}
    factors = {'L0_xattn_q_w': 8.0,
     'L0_xattn_kv_w': 8.0,
     'L0_xattn_out_w': 8.0,
     'L1_xattn_maa_x': 8.0,
     'L1_xattn_maa_w1': 7.989,
     'L1_xattn_maa_w2': 7.897,
     'L1_xattn_maa_stack': 2.906,
     'L1_xattn_time_decay': 2.826,
     'L1_xattn_td_w1': 8.0,
     'L1_xattn_td_w2': 8.0,
     'L1_xattn_u': 6.034,
     'L1_xattn_ffn_maa_k': 8.0,
     'L1_xattn_ffn_maa_r': 8.0,
     'L1_xattn_Wfk': 2.844,
     'L1_xattn_Wfr': 8.0,
     'L3_xattn_Wq': 8.0,
     'L3_xattn_Wk': 8.0}
    for name, (base, spread) in spreads.items():
        noise = np.random.default_rng([zlib.crc32(name.encode()), seed]).standard_normal(out[name].shape)
        drawn = base * np.exp(spread * noise) if base else spread * noise
        out[name] = jnp.asarray(drawn.astype(out[name].dtype))
    for name, factor in factors.items():
        out[name] = (out[name] * factor).astype(out[name].dtype)
    return out
```

```python
import numpy as np
import concourse.bass as bass
from concourse import mybir
from concourse.alu_op_type import AluOpType as ALU
from contextlib import ExitStack

F32 = mybir.dt.float32
I32 = mybir.dt.int32
ACT = mybir.ActivationFunctionType
AXX = mybir.AxisListType.X

B, S, C = 64, 64, 256
P = 128
KT = C // P
NB = 4
NT = NB * S
TT = NT // P
STEPS = B // (2 * NB)
NCH = 8
J = 8
HT = P // J
HID = 4 * C
W0 = 16
W3 = 8
MASKED = -1.0e30

WEIGHTS_A = [("ident", P), ("q0", 2 * C), ("k0", 2 * C), ("v0", 2 * C), ("o0", 2 * C), ("vec", 64), ("fv", 2 * C)]
WEIGHTS_B = [("w1", 2 * HID), ("w2", 8 * C),
             ("m1", 2 * 160), ("m2", 2 * C), ("td1", 2 * 64), ("td2", C),
             ("wk", 2 * C), ("wv", 2 * C), ("wr", 2 * C), ("wg", 2 * C), ("wo", 2 * C),
             ("fk", 2 * C), ("fr", 2 * C),
             ("q3", 2 * C), ("k3", 2 * P), ("v3", 2 * 64), ("o3", 2 * C),
             ("sumh", HT), ("blk", P), ("spread", J * P), ("perm", P)]
NAT = [("l2q", 2 * C), ("l2k", 2 * C), ("l2v", 2 * C), ("l2o", 2 * C)]
VEC = {}
for _n, _w in [("qb0", 2), ("kb0", 2), ("vb0", 2), ("pn", 2), ("b1", 8), ("ln1w", 2), ("ln1b", 2),
               ("ln2w", 2), ("ln2b", 2), ("maax", 2), ("stack", 10), ("td", 2), ("u", 2),
               ("gnw", 2), ("gnb", 2), ("fmk", 2), ("fmr", 2), ("qb3", 2), ("kb3", 1), ("vb3", 2),
               ("par", 2), ("sub", 4), ("alpha", 1)]:
    VEC[_n] = (sum(w for _, w in VEC.values()), _w)
ROWS = ["out_b", "mlp_b2", "bo", "gamma", "beta"]


def columns(table):
    at, out = 0, {}
    for name, width in table:
        out[name] = (at, width)
        at += width
    return out, at


def build(nc, h_d, x_d, mask_d, amask_d, s0_d, wa_d, wb_d, nat_d, rows_d, out_d):
    ca, na = columns(WEIGHTS_A)
    cb, nb = columns(WEIGHTS_B)
    cn, nn = columns(NAT)


    with ExitStack() as ctx:
        def sb(name, shape, dt=F32):
            return ctx.enter_context(nc.sbuf_tensor(name, shape, dt))

        def sem(name):
            return ctx.enter_context(nc.semaphore(name))

        def sems(name):
            return [sem(f"{name}_{h}") for h in range(2)]

        def sbs(name, shape, dt=F32):
            return [sb(f"{name}_{h}", shape, dt) for h in range(2)]

        wa = sb("wa", [P, na])
        wb = sb("wb", [P, nb])

        def w(name, k=None):
            t, (at, n) = (wa, ca[name]) if name in ca else (wb, cb[name])
            v = t[:, at:at + n]
            return v if k is None else v.rearrange("p (k n) -> p k n", k=2)[:, k, :]

        ident = w("ident")
        vec0 = ca["vec"][0]

        def vec(name, k=0):
            c = vec0 + VEC[name][0] + k
            return wa[:, c:c + 1]

        w2 = w("w2").rearrange("p (m n) -> p m n", m=8)
        rows = sb("rows", [P, len(ROWS), C])

        def row(name, n):
            return rows[:, ROWS.index(name), :].unsqueeze(1).broadcast_to([P, n, C])

        m_qk = sb("m_qk", [P, 2, C])
        m_vo = sb("m_vo", [P, 2, C])
        qb0m = sb("qb0m", [P, 2, 2])
        qb3m = sb("qb3m", [P, 2, 4])
        eps = sb("eps", [P, 68])
        power = sb("power", [P, 64])

        hT = sbs("hT", [P, KT, NB, 2 * S])
        xN = sbs("xN", [P, TT, C])
        mint = sbs("mint", [P, NB, S], I32)
        m0 = sbs("m0", [P, NB, 2 * S])
        m3 = sbs("m3", [P, NB, S])
        s0 = sbs("s0", [P, KT, NB, J])
        big = sbs("big", [P, 2560])
        att = sbs("att", [P, 3584])
        v0 = sbs("v0s", [P, NB, 8, 33])
        v3 = sbs("v3s", [P, NB, 2, 48])
        xaT = sbs("xaT", [P, KT, NB, S + 1])
        sx = sbs("sx", [P, KT, NB, S])
        tA = sbs("tA", [P, KT, NT])
        th = sbs("th", [P, 2, NT])
        kS = sbs("kS", [P, KT, NT])
        vS = sbs("vS", [P, KT, NT])
        rS = sbs("rS", [P, KT, NT])
        gs = sbs("gs", [P, KT, NT])
        wS = sbs("wS", [P, KT, NB, S + 1])
        n1 = sbs("n1", [P, TT, C])
        n2 = sbs("n2", [P, TT, C])
        n3 = sbs("n3", [P, TT, C])
        n4 = sbs("n4", [P, TT, C])
        n5 = sbs("n5", [P, TT, C])
        bns = sbs("bns", [P, TT, 6])
        mv = sbs("mv", [P, TT, 2])
        rstd = sbs("rstd", [P, TT])
        vtmp = sbs("vtmp", [P, TT])
        ssq = sbs("ssq", [P, TT])
        mx = sbs("mx", [P, 2, 8])
        rc = sbs("rc", [P, 64])
        g1 = sbs("g1", [P, 64])
        g2 = sbs("g2", [P, 64])
        g3 = sbs("g3", [P, 64])
        ps = [[ctx.enter_context(nc.psum_tensor(f"ps{h}{k}", [P, 512], F32)) for k in range(4)] for h in range(2)]

        sc = [[a[:, 512 * i:512 * (i + 1)] for i in range(2)] for a in att]
        pt = [a[:, 1024:1536] for a in att]
        ao = [a[:, 1536:2560].rearrange("p (b k c) -> p b k c", b=NB, k=2) for a in att]
        kT = [a[:, 2560:3584].rearrange("p (k b s) -> p k b s", k=2, b=NB) for a in att]
        kT3 = [a[:, 2560:2816].rearrange("p (b s) -> p b s", b=NB) for a in att]
        aB = [[a[:, 520 * i:520 * (i + 1)].rearrange("p (j b s) -> p j b s", j=2, b=NB) for i in range(2)] for a in att]
        st = [[a[:, 1040 + 520 * i:1560 + 520 * i].rearrange("p (j b s) -> p j b s", j=2, b=NB) for i in range(2)] for a in att]
        pd = [[a[:, 2080 + 512 * i:2592 + 512 * i].rearrange("p (j n) -> p j n", j=2) for i in range(2)] for a in att]
        qz = [a[:, 0:1024].rearrange("p (k b v s) -> p k b v s", k=2, v=2, b=NB) for a in big]
        qz3 = [a[:, 0:2048].rearrange("p (k b v s) -> p k b v s", k=2, v=4, b=NB) for a in big]
        hid = [a[:, 0:2048].rearrange("p (m n) -> p m n", m=8) for a in big]
        xm = [[a[:, 512 * j:512 * (j + 1)].rearrange("p (k n) -> p k n", k=2) for j in range(5)] for a in big]
        ruk = [x[0] for x in xm]
        cv = [x[1] for x in xm]
        tS = [x[0] for x in xm]
        uS = [x[1] for x in xm]
        pbd = [x[2].rearrange("p k n -> p (k n)")[:, 0:256].rearrange("p (t n) -> p t n", t=2) for x in xm]
        ptb = [x[3].rearrange("p k n -> p (k n)")[:, 0:256].rearrange("p (t n) -> p t n", t=2) for x in xm]

        def flat(t):
            return t.rearrange("p k n -> p (k n)")

        def kn(bank):
            return bank[:, :].rearrange("p (k n) -> p k n", k=2)

        ld_w, ld_wb, ld_nat, ld_rows = sem("ld_w"), sem("ld_wb"), sem("ld_nat"), sem("ld_rows")
        set_pool, set_dve, set_pe, set_m = sem("set_pool"), sem("set_dve"), sem("set_pe"), sem("set_m")
        ld_h, ld_x, ld_m, ld_3, ld_s = sems("ld_h"), sems("ld_x"), sems("ld_m"), sems("ld_3"), sems("ld_s")
        st_out = sems("st_out")
        free_ps = sems("free_ps")
        q0_ps, k0_ps, v0_ps = sems("q0_ps"), sems("k0_ps"), sems("v0_ps")
        q0_sb, k0_sb, v0_sb = sems("q0_sb"), sems("k0_sb"), sems("v0_sb")
        s_ps, s_sb, s_mx, s_sub, s_exp = sems("s_ps"), sems("s_sb"), sems("s_mx"), sems("s_sub"), sems("s_exp")
        t_ps, t_sb, o_ps, o_rc, o_sb = sems("t_ps"), sems("t_sb"), sems("o_ps"), sems("o_rc"), sems("o_sb")
        mg_ps, mg_sb = sems("mg_ps"), sems("mg_sb")
        res = sems("res")
        pr_ps, pr_sb = sems("pr_ps"), sems("pr_sb")
        sq_ok, rs_a, rs_b = sems("sq_ok"), sems("rs_a"), sems("rs_b")
        bn_a, bn_b = sems("bn_a"), sems("bn_b")
        xh_ok = sems("xh_ok")
        xt_ps, xt_sb = sems("xt_ps"), sems("xt_sb")
        h_ps, h_sb = sems("h_ps"), sems("h_sb")
        sh_ok, sx_ok, xin_ok = sems("sh_ok"), sems("sx_ok"), sems("xin_ok")
        m1_ps, m1_sb, m2_ps, m2_mx, xm_ok = sems("m1_ps"), sems("m1_sb"), sems("m2_ps"), sems("m2_mx"), sems("xm_ok")
        pk_ps, pk_sb = sems("pk_ps"), sems("pk_sb")
        e1_ok, tg_ok = sems("e1_ok"), sems("tg_ok")
        ruk_ok, cb_ps, cv_ok = sems("ruk_ok"), sems("cb_ps"), sems("cv_ok")
        a0_ok, vx_ps, a_ok, sc_ok, pd_ok, rd_ps = sems("a0_ok"), sems("vx_ps"), sems("a_ok"), sems("sc_ok"), sems("pd_ok"), sems("rd_ps")
        gn_d, gn_p, og_ok = sems("gn_d"), sems("gn_p"), sems("og_ok")
        ff_ps, ff_a, kk_ok, ff_d = sems("ff_ps"), sems("ff_a"), sems("kk_ok"), sems("ff_d")
        x2_ok = sems("x2_ok")
        l2_ps, l2_sb = sems("l2_ps"), sems("l2_sb")
        l2_mx = sems("l2_mx")
        kv3_ps, kv3_a, kv3_d = sems("kv3_ps"), sems("kv3_a"), sems("kv3_d")
        fin_ok = sems("fin_ok")

        block = ctx.enter_context(nc.Block())
        halves = range(2)

        @block.sync
        def _(sp):
            sp.dma_start(wa[:, :], wa_d).then_inc(ld_w, 16)

            def load(it, h, skip_free=False):
                b0 = it * (2 * NB) + h * NB
                sp.dma_start(hT[h][:, :, :, :], h_d[:, :, bass.ds(b0, NB), :]).then_inc(ld_h[h], 16)
                sp.dma_start(xN[h][:, :, :], x_d[:, bass.ds(it * (2 * TT) + h * TT, TT), :]).then_inc(ld_x[h], 16)
                sp.dma_start(mint[h][:, :, :], mask_d[bass.ds(b0, NB), :].unsqueeze(0).broadcast_to([P, NB, S])).then_inc(ld_m[h], 16)
                sp.dma_start(s0[h][:, :, :, :], s0_d[:, :, bass.ds(b0, NB), :]).then_inc(ld_s[h], 16)

            def load3(it, h):
                b0 = it * (2 * NB) + h * NB
                for d in range(2):
                    sp.dma_start(m3[h][64 * d:64 * d + 64, :, :],
                                 amask_d[bass.ds(b0, NB), :, :].rearrange("b q k -> q b k")).then_inc(ld_3[h], 16)

            for h in halves:
                load(0, h)
            sp.dma_start(att[0][:, 0:nn], nat_d).then_inc(ld_nat, 16)
            sp.dma_start(rows[:, :, :], rows_d.unsqueeze(0).broadcast_to([P, len(ROWS), C])).then_inc(ld_rows, 16)
            sp.dma_start(wb[:, :], wb_d).then_inc(ld_wb, 16)
            for h in halves:
                load3(0, h)
            with sp.Fori(0, STEPS - 1) as it:
                for h in halves:
                    sp.wait_ge(kv3_ps[h], it * 2 + 2)
                    load(it + 1, h)
                for h in halves:
                    sp.wait_ge(s_sb[h], it * 16 + 16)
                    load3(it + 1, h)
                for h in halves:
                    sp.wait_ge(fin_ok[h], it * 4 + 4)
                    sp.dma_start(out_d[:, bass.ds(it * (2 * TT) + h * TT, TT), :], n5[h][:, :, :]).then_inc(st_out[h], 16)
            for h in halves:
                sp.wait_ge(fin_ok[h], STEPS * 4)
                sp.dma_start(out_d[:, (STEPS - 1) * 2 * TT + h * TT:(STEPS - 1) * 2 * TT + (h + 1) * TT, :],
                             n5[h][:, :, :]).then_inc(st_out[h], 16)
            for h in halves:
                sp.wait_ge(st_out[h], 16 * STEPS + 16)

        @block.tensor
        def _(pe):
            mm = nc.tensor.matmul

            def chunk_scores(it, h, layer, c):
                at, pair, r = layer * NCH + c, c // 4, c % 4
                g = slice(32 * r, 32 * r + 32)
                out = ps[h][c % 2]
                if c >= 2:
                    pe.wait_ge(s_sb[h], it * 16 + at - 1)
                for i in range(2):
                    b = 2 * pair + i
                    for k in range(2):
                        if layer == 0:
                            last = mm(out[:, (2 * i + k) * P:(2 * i + k + 1) * P], qz[h][g, k, b, :, :].rearrange("p v s -> p (v s)"),
                                      kT[h][g, k, b, :], start=True, stop=True)
                        else:
                            for v in range(2):
                                o = ((2 * i + k) * 2 + v) * S
                                last = mm(out[:, o:o + S], qz3[h][g, k, b, 2 * v:2 * v + 2, :].rearrange("p v s -> p (v s)"),
                                          kT3[h][g, b, :], start=True, stop=True)
                last.then_inc(s_ps[h], 1)

            def chunk_turn(it, h, layer, c):
                at = layer * NCH + c
                pe.wait_ge(s_exp[h], it * 16 + at + 1)
                if c >= 1:
                    pe.wait_ge(t_sb[h], it * 16 + at)
                for i in range(4):
                    last = nc.tensor.transpose(ps[h][2][:, i * P:(i + 1) * P], sc[h][c % 2][:, i * P:(i + 1) * P], ident)
                last.then_inc(t_ps[h], 1)

            def chunk_values(it, h, layer, c):
                at, pair, r = layer * NCH + c, c // 4, c % 4
                pe.wait_ge(t_sb[h], it * 16 + at + 1)
                if c >= 1:
                    pe.wait_ge(o_sb[h], it * 16 + at)
                for i in range(4):
                    b, k = 2 * pair + i // 2, i % 2
                    if layer == 0:
                        last = mm(ps[h][3][:, 33 * i:33 * i + 33], pt[h][:, i * P:(i + 1) * P],
                                  v0[h][:, b, 4 * k + r, :], start=True, stop=True)
                    else:
                        last = mm(ps[h][3][:, 48 * i:48 * i + 48], pt[h][:, i * P:(i + 1) * P],
                                  v3[h][:, b, r % 2, :], start=True, stop=True)
                last.then_inc(o_ps[h], 1)

            def attend(it, layer):
                for c in range(NCH + 2):
                    if c < NCH:
                        for h in halves:
                            chunk_scores(it, h, layer, c)
                    if 1 <= c <= NCH:
                        for h in halves:
                            chunk_turn(it, h, layer, c - 1)
                    if c >= 2:
                        for h in halves:
                            chunk_values(it, h, layer, c - 2)
                for h in halves:
                    pe.wait_ge(set_pool, 2)
                    pe.wait_ge(o_sb[h], it * 16 + layer * NCH + NCH)
                    out = ps[h][0][:, :].rearrange("p (k b s) -> p k b s", k=2, b=NB)
                    for e in range(2):
                        g = slice(64 * e, 64 * e + 64)
                        for b in range(NB):
                            for k in range(2):
                                last = mm(out[g, k, b, :], ao[h][g, b, k, 64 * e:64 * e + 64], ident[g, g], start=True, stop=True)
                    last.then_inc(mg_ps[h], 1)

            def dense_T(out, weight, rhs, tiles=2):
                for m in range(tiles):
                    for k in range(2):
                        last = mm(out[:, m, :], weight(k)[:, m * P:(m + 1) * P], rhs(k), start=(k == 0), stop=(k == 1))
                return last

            def dense_N(out, lhs, weight, ks=2):
                for t in range(TT):
                    for k in range(ks):
                        last = mm(out[:, t, :], lhs(k, t), weight(k), start=(k == 0), stop=(k == ks - 1))
                return last

            def turn_rows(it, h, bank, src, per, n):
                for t in range(TT):
                    for k in range(KT):
                        last = nc.tensor.transpose(kn(ps[h][bank])[:, k, t * P:(t + 1) * P], src[:, t, k * P:(k + 1) * P], ident)
                last.then_inc(xt_ps[h], 1)

            def tok(t):
                return slice(t * P, (t + 1) * P)

            nat = att[0][:, 0:nn].rearrange("p (m k n) -> p m k n", m=4, k=2)
            pe.wait_ge(ld_nat, 16)
            for m in range(2):
                for k in range(2):
                    mm(kn(ps[0][0])[:, m, :], nat[:, 1, k, m * P:(m + 1) * P], nat[:, 0, k, :], start=(k == 0), stop=(k == 1))
                for k in range(2):
                    last = mm(kn(ps[0][1])[:, m, :], nat[:, 2, k, m * P:(m + 1) * P], nat[:, 3, k, :], start=(k == 0), stop=(k == 1))
            last.then_inc(set_pe, 1)
            pe.wait_ge(ld_w, 16)
            pe.wait_ge(set_m, 1)
            pe.wait_ge(set_pool, 2)
            pe.wait_ge(set_dve, 1)

            with pe.Fori(0, STEPS) as it:
                for h in halves:
                    pe.wait_ge(ld_h[h], it * 16 + 16)
                    pe.wait_ge(free_ps[h], it + 1)
                    dense_T(kn(ps[h][0]), lambda k: w("q0", k), lambda k: hT[h][:, k, :, S:2 * S]).then_inc(q0_ps[h], 1)
                    for m in range(2):
                        for k in range(2):
                            last = mm(ps[h][1 + m][:, :], w("k0", k)[:, m * P:(m + 1) * P], hT[h][:, k, :, :], start=(k == 0), stop=(k == 1))
                    last.then_inc(k0_ps[h], 1)
                    for b in range(NB):
                        if b == 2:
                            pe.wait_ge(q0_sb[h], it + 1)
                        for k in range(2):
                            last = mm(kn(ps[h][3 if b < 2 else 0])[:, b % 2, :], hT[h][:, k, b, :], w("v0", k), start=(k == 0), stop=(k == 1))
                        if b % 2:
                            last.then_inc(v0_ps[h], 1)
                for h in halves:
                    pe.wait_ge(k0_sb[h], it * 2 + 1)
                    pe.wait_ge(v0_sb[h], it * 2 + 2)
                attend(it, 0)
                for h in halves:
                    pe.wait_ge(mg_sb[h], it * 2 + 1)
                    dense_N(kn(ps[h][1]), lambda k, t: tA[h][:, k, tok(t)], lambda k: w("o0", k)).then_inc(pr_ps[h], 1)
                for h in halves:
                    pe.wait_ge(xh_ok[h], it * 4 + 1)
                    turn_rows(it, h, 2, n2[h], 5, 0)
                pe.wait_ge(ld_wb, 16)
                for h in halves:
                    pe.wait_ge(xt_sb[h], it * 6 + 1)
                    for i, bank in enumerate((0, 1, 3, 2)):
                        for m in range(2):
                            mt = 2 * i + m
                            for k in range(2):
                                last = mm(kn(ps[h][bank])[:, m, :], w("w1", k)[:, mt * P:(mt + 1) * P], tA[h][:, k, :], start=(k == 0), stop=(k == 1))
                        last.then_inc(h_ps[h], 1)
                for h in halves:
                    pe.wait_ge(h_sb[h], it * 4 + 4)
                    dense_N(kn(ps[h][0]), lambda k, t: hid[h][:, k, tok(t)], lambda k: w2[:, k, :], ks=8).then_inc(pr_ps[h], 1)
                for h in halves:
                    pe.wait_ge(xh_ok[h], it * 4 + 2)
                    turn_rows(it, h, 1, n3[h], 5, 1)
                for h in halves:
                    pe.wait_ge(xin_ok[h], it + 1)
                    for m in range(2):
                        rows_ = P if m == 0 else 32
                        for k in range(2):
                            last = mm(kn(ps[h][2])[0:rows_, m, :], w("m1", k)[:, m * P:m * P + rows_], tA[h][:, k, :], start=(k == 0), stop=(k == 1))
                    last.then_inc(m1_ps[h], 1)
                for h in halves:
                    pe.wait_ge(m1_sb[h], it + 1)
                    for f, bank in enumerate((0, 1, 3, 2, 0)):
                        if f == 4:
                            pe.wait_ge(m2_mx[h], it * 5 + 1)
                        g = slice(32 * (f % 4), 32 * (f % 4) + 32)
                        for m in range(2):
                            last = mm(kn(ps[h][bank])[:, m, :], w("m2", f // 4)[g, m * P:(m + 1) * P], th[h][g, f // 4, :], start=True, stop=True)
                        last.then_inc(m2_ps[h], 1)
                for h in halves:
                    pe.wait_ge(xm_ok[h], it * 5 + 1)
                    pe.wait_ge(m2_mx[h], it * 5 + 2)
                    dense_T(kn(ps[h][1]), lambda k: w("wk", k), lambda k: xm[h][0][:, k, :]).then_inc(pk_ps[h], 1)
                for h in halves:
                    pe.wait_ge(xm_ok[h], it * 5 + 2)
                    pe.wait_ge(m2_mx[h], it * 5 + 3)
                    for k in range(2):
                        last = mm(kn(ps[h][3])[0:64, 0, :], w("td1", k), xm[h][1][:, k, :], start=(k == 0), stop=(k == 1))
                    last.then_inc(pk_ps[h], 1)
                for h in halves:
                    pe.wait_ge(xm_ok[h], it * 5 + 3)
                    pe.wait_ge(m2_mx[h], it * 5 + 4)
                    dense_T(kn(ps[h][2]), lambda k: w("wv", k), lambda k: xm[h][2][:, k, :]).then_inc(pk_ps[h], 1)
                for h in halves:
                    pe.wait_ge(pk_sb[h], it * 6 + 2)
                    for m in range(2):
                        last = mm(kn(ps[h][3])[:, m, :], w("td2")[0:64, m * P:(m + 1) * P], th[h][0:64, 0, :], start=True, stop=True)
                    last.then_inc(pk_ps[h], 1)
                for h in halves:
                    pe.wait_ge(xm_ok[h], it * 5 + 4)
                    pe.wait_ge(m2_mx[h], it * 5 + 5)
                    dense_T(kn(ps[h][0]), lambda k: w("wr", k), lambda k: xm[h][3][:, k, :]).then_inc(pk_ps[h], 1)
                for h in halves:
                    pe.wait_ge(xm_ok[h], it * 5 + 5)
                    pe.wait_ge(pk_sb[h], it * 6 + 1)
                    dense_T(kn(ps[h][1]), lambda k: w("wg", k), lambda k: xm[h][4][:, k, :]).then_inc(pk_ps[h], 1)
                for h in halves:
                    pe.wait_ge(ruk_ok[h], it + 1)
                    pe.wait_ge(pk_sb[h], it * 6 + 3)
                    for m in range(2):
                        last = mm(kn(ps[h][2])[:, m, :], w("blk"), ruk[h][:, m, :], start=True, stop=True)
                    last.then_inc(cb_ps[h], 1)
                def spread(h, q):
                    m, jp = q // 4, q % 4
                    if q == 0:
                        pe.wait_ge(pk_sb[h], it * 6 + 6)
                    if q >= 2:
                        pe.wait_ge(a_ok[h], it * 8 + q - 1)
                    for i in range(2):
                        j = 2 * jp + i
                        last = mm(kn(ps[h][q % 2])[:, i, :], w("spread")[:, j * P:(j + 1) * P], vS[h][:, m, :], start=True, stop=True)
                    last.then_inc(vx_ps[h], 1)

                def gather(h, q):
                    m, jp = q // 4, q % 4
                    out = ps[h][3][:, :].rearrange("p (t m j h) -> p t m j h", t=TT, m=2, j=J)
                    if q == 0:
                        pe.wait_ge(cv_ok[h], it + 1)
                        pe.wait_ge(pk_sb[h], it * 6 + 4)
                        for t in range(TT):
                            for mm_ in range(2):
                                mm(out[:, t, mm_, :, :].rearrange("p j h -> p (j h)"), cv[h][:, mm_, tok(t)], w("perm"),
                                   start=(t == 0 and mm_ == 0), stop=False, skip_group_check=True)
                    pe.wait_ge(pd_ok[h], it * 8 + q + 1)
                    for i in range(2):
                        for t in range(TT):
                            last = mm(out[:, t, m, 2 * jp + i, :], pd[h][q % 2][:, i, tok(t)], w("sumh"), start=False,
                                      stop=(q == 7 and i == 1 and t == TT - 1), skip_group_check=True)
                    last.then_inc(rd_ps[h], 1)

                for q in range(9):
                    for h in halves:
                        if q < 8:
                            spread(h, q)
                    for h in halves:
                        if q >= 1:
                            gather(h, q - 1)
                for h in halves:
                    pe.wait_ge(xh_ok[h], it * 4 + 3)
                    turn_rows(it, h, 0, n3[h], 5, 2)
                for h in halves:
                    pe.wait_ge(og_ok[h], it + 1)
                    dense_N(kn(ps[h][1]), lambda k, t: tA[h][:, k, tok(t)], lambda k: w("wo", k)).then_inc(pr_ps[h], 1)
                for h in halves:
                    pe.wait_ge(xh_ok[h], it * 4 + 4)
                    turn_rows(it, h, 2, n3[h], 5, 3)
                for h in halves:
                    pe.wait_ge(ff_d[h], it * 2 + 1)
                    dense_T(kn(ps[h][0]), lambda k: w("fk", k), lambda k: tA[h][:, k, :]).then_inc(ff_ps[h], 1)
                for h in halves:
                    pe.wait_ge(ff_d[h], it * 2 + 2)
                    dense_N(kn(ps[h][3]), lambda k, t: th[h][:, k, tok(t)], lambda k: w("fr", k)).then_inc(ff_ps[h], 1)
                for h in halves:
                    dense_T(kn(ps[h][2]), lambda k: m_qk[:, k, :], lambda k: hT[h][:, k, :, 0:S]).then_inc(l2_ps[h], 1)
                for h in halves:
                    pe.wait_ge(kk_ok[h], it + 1)
                    dense_N(kn(ps[h][1]), lambda k, t: kS[h][:, k, tok(t)], lambda k: w("fv", k)).then_inc(pr_ps[h], 1)
                for h in halves:
                    pe.wait_ge(ff_a[h], it * 2 + 1)
                    for b in range(NB):
                        g = slice(64 * (b % 2), 64 * (b % 2) + 64)
                        for k in range(2):
                            last = mm(kn(ps[h][0])[g, b // 2, :], hT[h][:, k, b, 0:S], m_vo[:, k, :], start=(k == 0), stop=(k == 1))
                    last.then_inc(l2_ps[h], 1)
                for h in halves:
                    pe.wait_ge(x2_ok[h], it + 1)
                    pe.wait_ge(tg_ok[h], it * 2 + 2)
                    turn_rows(it, h, 3, n2[h], 5, 4)
                for h in halves:
                    pe.wait_ge(xt_sb[h], it * 6 + 5)
                    pe.wait_ge(l2_sb[h], it * 3 + 1)
                    for b in range(NB):
                        g = slice(64 * (b % 2), 64 * (b % 2) + 64)
                        for k in range(2):
                            last = mm(ps[h][1][g, (b // 2) * S:(b // 2) * S + S], tA[h][:, k, b * S:(b + 1) * S], tS[h][:, k, b * S:(b + 1) * S],
                                      start=(k == 0), stop=(k == 1))
                    last.then_inc(l2_ps[h], 1)
                for h in halves:
                    pe.wait_ge(ff_a[h], it * 2 + 2)
                    pe.wait_ge(l2_sb[h], it * 3 + 2)
                    for t in range(TT):
                        last = nc.tensor.transpose(ps[h][0][:, t * P:(t + 1) * P], pbd[h][:, t, :], ident)
                    last.then_inc(l2_ps[h], 1)
                for h in halves:
                    pe.wait_ge(l2_sb[h], it * 3 + 3)
                    for t in range(TT):
                        last = mm(kn(ps[h][2])[:, t, :], ptb[h][:, t, :], uS[h][:, t, :], start=True, stop=True)
                    last.then_inc(pr_ps[h], 1)
                for h in halves:
                    for k in range(2):
                        last = mm(ps[h][1][:, 0:NT], w("k3", k), hT[h][:, k, :, 0:S], start=(k == 0), stop=(k == 1))
                    last.then_inc(kv3_ps[h], 1)
                for h in halves:
                    for b in range(NB):
                        for e in range(2):
                            for k in range(2):
                                last = mm(ps[h][0][64 * e:64 * e + 64, b * 64:(b + 1) * 64], hT[h][:, k, b, 0:S], w("v3", k),
                                          start=(k == 0), stop=(k == 1))
                    last.then_inc(kv3_ps[h], 1)
                for h in halves:
                    pe.wait_ge(pr_sb[h], it * 6 + 5)
                    turn_rows(it, h, 3, n1[h], 5, 5)
                for h in halves:
                    pe.wait_ge(xt_sb[h], it * 6 + 6)
                    dense_T(kn(ps[h][2]), lambda k: w("q3", k), lambda k: tA[h][:, k, :]).then_inc(l2_ps[h], 1)
                for h in halves:
                    pe.wait_ge(kv3_a[h], it * 2 + 2)
                    pe.wait_ge(kv3_d[h], it + 1)
                attend(it, 1)
                for h in halves:
                    pe.wait_ge(mg_sb[h], it * 2 + 2)
                    dense_N(kn(ps[h][1]), lambda k, t: tA[h][:, k, tok(t)], lambda k: w("o3", k)).then_inc(pr_ps[h], 1)

        @block.scalar
        def _(act):
            A = nc.scalar.activation

            def attend(it, layer):
                def soft(h, c):
                    act.wait_ge(s_sub[h], it * 16 + layer * NCH + c + 1)
                    A(sc[h][c % 2], sc[h][c % 2], ACT.Exp).then_inc(s_exp[h], 1)

                def lift(h, c):
                    act.wait_ge(t_ps[h], it * 16 + layer * NCH + c + 1)
                    if c >= 1:
                        act.wait_ge(o_ps[h], it * 16 + layer * NCH + c)
                    A(pt[h], ps[h][2][:, :], ACT.Copy).then_inc(t_sb[h], 1)

                for c in range(NCH + 1):
                    for h in halves:
                        if c < NCH:
                            soft(h, c)
                    for h in halves:
                        if c >= 1:
                            lift(h, c - 1)
                for h in halves:
                    act.wait_ge(mg_ps[h], it * 2 + layer + 1)
                    name = "vb0" if layer == 0 else "vb3"
                    for k in range(2):
                        last = A(tA[h][:, k, :], kn(ps[h][0])[:, k, :], ACT.Identity, bias=vec(name, k))
                    last.then_inc(mg_sb[h], 1)

            def affine(h, bank, name_w, name_b, dst=None):
                for k in range(2):
                    last = A(dst(k), kn(ps[h][bank])[:, k, :].rearrange("p (b s) -> p b s", b=NB), ACT.Identity,
                             bias=vec(name_b, k) if name_b else 0.0, scale=vec(name_w, k))
                return last

            act.wait_ge(ld_w, 16)
            act.wait_ge(set_dve, 1)
            act.wait_ge(set_pool, 2)
            with act.Fori(0, STEPS) as it:
                for h in halves:
                    act.wait_ge(q0_ps[h], it + 1)
                    for k in range(2):
                        for v in range(2):
                            last = A(qz[h][:, k, :, v, :], kn(ps[h][0])[:, k, :].rearrange("p (b s) -> p b s", b=NB), ACT.Identity,
                                     bias=qb0m[:, k, v:v + 1], scale=vec("par", v))
                    last.then_inc(q0_sb[h], 1)
                    for i in range(2):
                        act.wait_ge(v0_ps[h], it * 2 + i + 1)
                        for b in range(2):
                            last = A(v0[h][:, 2 * i + b, :, 0:32], kn(ps[h][0 if i else 3])[:, b, :].rearrange("p (g c) -> p g c", c=32), ACT.Copy)
                        last.then_inc(v0_sb[h], 1)
                attend(it, 0)
                for h in halves:
                    act.wait_ge(pr_sb[h], it * 6 + 1)
                    for t in range(TT):
                        last = A(n3[h][:, t, :], n1[h][:, t, :], ACT.Square, scale=1.0 / C ** 0.5, accum_out=ssq[h][:, t:t + 1])
                    last.then_inc(sq_ok[h], 1)
                for h in halves:
                    act.wait_ge(xt_ps[h], it * 6 + 1)
                    for k in range(2):
                        last = A(tA[h][:, k, :], kn(ps[h][2])[:, k, :], ACT.Identity, scale=vec("pn", k))
                    last.then_inc(xt_sb[h], 1)
                for h in halves:
                    for i, bank in enumerate((0, 1, 3, 2)):
                        act.wait_ge(h_ps[h], it * 4 + i + 1)
                        for m in range(2):
                            last = A(hid[h][:, 2 * i + m, :], kn(ps[h][bank])[:, m, :], ACT.Gelu_apprx_tanh, bias=vec("b1", 2 * i + m))
                        last.then_inc(h_sb[h], 1)
                for h in halves:
                    act.wait_ge(xt_ps[h], it * 6 + 2)
                    affine(h, 1, "ln1w", "ln1b", lambda k: xaT[h][:, k, :, 1:S + 1]).then_inc(xt_sb[h], 1)
                for h in halves:
                    act.wait_ge(m1_ps[h], it + 1)
                    A(th[h][:, 0, :], kn(ps[h][2])[:, 0, :], ACT.Tanh)
                    A(th[h][0:32, 1, :], kn(ps[h][2])[0:32, 1, :], ACT.Tanh).then_inc(m1_sb[h], 1)
                for h in halves:
                    act.wait_ge(pk_ps[h], it * 6 + 1)
                    A(flat(kS[h]), ps[h][1][:, :], ACT.Copy).then_inc(pk_sb[h], 1)
                for h in halves:
                    act.wait_ge(pk_ps[h], it * 6 + 2)
                    A(th[h][0:64, 0, :], kn(ps[h][3])[0:64, 0, :], ACT.Tanh).then_inc(pk_sb[h], 1)
                for h in halves:
                    act.wait_ge(pk_ps[h], it * 6 + 3)
                    A(flat(vS[h]), ps[h][2][:, :], ACT.Copy).then_inc(pk_sb[h], 1)
                for h in halves:
                    act.wait_ge(pk_ps[h], it * 6 + 4)
                    act.wait_ge(m2_mx[h], it * 5 + 5)
                    for k in range(2):
                        last = A(sx[h][:, k, :, :], kn(ps[h][3])[:, k, :].rearrange("p (b s) -> p b s", b=NB), ACT.Exp, bias=vec("td", k))
                    last.then_inc(e1_ok[h], 1)
                    act.wait_ge(e1_ok[h], it + 1)
                    for k in range(2):
                        last = A(wS[h][:, k, :, 1:S + 1], sx[h][:, k, :, :], ACT.Exp, scale=-1.0)
                    last.then_inc(pk_sb[h], 1)
                for h in halves:
                    act.wait_ge(pk_ps[h], it * 6 + 5)
                    A(flat(rS[h]), ps[h][0][:, :], ACT.Copy).then_inc(pk_sb[h], 1)
                for h in halves:
                    act.wait_ge(pk_ps[h], it * 6 + 6)
                    A(flat(gs[h]), ps[h][1][:, :], ACT.Tanh, scale=0.5).then_inc(tg_ok[h], 1)
                for h in halves:
                    act.wait_ge(xt_ps[h], it * 6 + 3)
                    affine(h, 0, "gnw", "gnb", lambda k: tA[h][:, k, :].rearrange("p (b s) -> p b s", b=NB)).then_inc(xt_sb[h], 1)
                for h in halves:
                    act.wait_ge(xt_ps[h], it * 6 + 4)
                    affine(h, 2, "ln2w", "ln2b", lambda k: xaT[h][:, k, :, 1:S + 1]).then_inc(xt_sb[h], 1)
                for h in halves:
                    act.wait_ge(ff_ps[h], it * 2 + 1)
                    A(flat(rS[h]), ps[h][0][:, :], ACT.Relu).then_inc(ff_a[h], 1)
                for h in halves:
                    act.wait_ge(ff_ps[h], it * 2 + 2)
                    A(flat(gs[h]), ps[h][3][:, :], ACT.Tanh, scale=0.5).then_inc(tg_ok[h], 1)
                for h in halves:
                    act.wait_ge(l2_ps[h], it * 5 + 1)
                    A(flat(tS[h]), ps[h][2][:, :], ACT.Copy).then_inc(l2_sb[h], 1)
                for h in halves:
                    act.wait_ge(l2_ps[h], it * 5 + 2)
                    A(flat(uS[h]), ps[h][0][:, :], ACT.Copy).then_inc(l2_sb[h], 1)
                for h in halves:
                    act.wait_ge(xt_ps[h], it * 6 + 5)
                    A(flat(tA[h]), ps[h][3][:, :], ACT.Copy).then_inc(xt_sb[h], 1)
                for h in halves:
                    act.wait_ge(l2_mx[h], it * 3 + 2)
                    for t in range(TT):
                        for e in range(2):
                            g = slice(64 * e, 64 * e + 64)
                            last = A(pbd[h][g, t, 64 * e:64 * e + 64], ps[h][1][g, t * S:(t + 1) * S], ACT.Exp,
                                     bias=vtmp[h][g, t:t + 1], scale=1.0 / 16.0, accum_out=ssq[h][g, t:t + 1])
                    last.then_inc(ff_a[h], 1)
                for h in halves:
                    act.wait_ge(l2_ps[h], it * 5 + 4)
                    A(ptb[h].rearrange("p t n -> p (t n)"), ps[h][0][:, 0:2 * P], ACT.Copy).then_inc(l2_sb[h], 1)
                for h in halves:
                    act.wait_ge(kv3_ps[h], it * 2 + 1)
                    A(kT3[h].rearrange("p b s -> p (b s)"), ps[h][1][:, 0:NT], ACT.Identity, bias=vec("kb3")).then_inc(kv3_a[h], 1)
                for h in halves:
                    act.wait_ge(xt_ps[h], it * 6 + 6)
                    A(flat(tA[h]), ps[h][3][:, :], ACT.Copy).then_inc(xt_sb[h], 1)
                for h in halves:
                    act.wait_ge(l2_ps[h], it * 5 + 5)
                    for k in range(2):
                        for v in range(4):
                            last = A(qz3[h][:, k, :, v, :], kn(ps[h][2])[:, k, :].rearrange("p (b s) -> p b s", b=NB), ACT.Identity,
                                     bias=qb3m[:, k, v:v + 1], scale=vec("sub", v))
                    last.then_inc(kv3_a[h], 1)
                attend(it, 1)

        @block.gpsimd
        def _(pool):
            G = nc.gpsimd
            for h in halves:
                G.memset(wS[h][:, :, :, :], 0.0)
                G.memset(v3[h][:, :, :, :], 0.0)
                G.memset(v0[h][:, :, :, 32:33], 1.0)
                G.memset(m0[h][:, :, S:2 * S], 0.0)
            G.memset(eps[:, 0:2], 1e-6)
            G.memset(eps[:, 2:4], 1e-5)
            G.memset(eps[:, 4:68], J * 1e-5)
            for h in halves:
                G.memset(n5[h][:, 0, 0:1], 0.0).then_inc(st_out[h], 16)
            G.memset(power[:, :], -0.5).then_inc(set_pool, 1)
            pool.wait_ge(set_pool, 1)
            for h in halves:
                G.memset(v3[h][0:64, :, :, 32:40], 1.0)
                last = G.memset(v3[h][64:128, :, :, 40:48], 1.0)
            last.then_inc(set_pool, 1)

            def inverse_root(it, h, n, src, at):
                G.tensor_tensor(vtmp[h][:, :], src, eps[:, at:at + TT], ALU.add).then_inc(rs_a[h], 1)
                pool.wait_ge(rs_a[h], it * 4 + n + 1)
                G.tensor_tensor(rstd[h][:, :], vtmp[h][:, :], power[:, 0:TT], ALU.pow).then_inc(rs_b[h], 1)

            def attend(it, layer):
                groups = 4 if layer == 0 else 8
                for c in range(NCH):
                    for h in halves:
                        at = layer * NCH + c
                        pool.wait_ge(s_mx[h], it * 16 + at + 1)
                        v = sc[h][c % 2].rearrange("p (g k) -> p g k", g=groups)
                        m = mx[h][:, c % 2, 0:groups].unsqueeze(2).broadcast_to([P, groups, 512 // groups])
                        G.tensor_tensor(v, v, m, ALU.subtract).then_inc(s_sub[h], 1)

            with pool.Fori(0, STEPS) as it:
                attend(it, 0)
                pool.wait_ge(ld_rows, 16)
                for h in halves:
                    pool.wait_ge(ld_x[h], it * 16 + 16)
                    G.tensor_tensor(n1[h][:, :, :], xN[h][:, :, :], row("out_b", TT), ALU.add).then_inc(res[h], 1)
                for h in halves:
                    pool.wait_ge(sq_ok[h], it + 1)
                    inverse_root(it, h, 0, ssq[h][:, :], 0)
                for h in halves:
                    G.tensor_tensor(n4[h][:, :, :], xN[h][:, :, :], row("mlp_b2", TT), ALU.add).then_inc(res[h], 1)
                for h in halves:
                    pool.wait_ge(bn_b[h], it * 3 + 1)
                    inverse_root(it, h, 1, mv[h][:, :, 1], 2)
                    G.tensor_copy(xaT[h][:, :, :, 0:1], hT[h][:, :, :, 1:2]).then_inc(sh_ok[h], 1)
                for h in halves:
                    pool.wait_ge(xt_sb[h], it * 6 + 2)
                    pool.wait_ge(sh_ok[h], it * 2 + 1)
                    G.tensor_tensor(sx[h][:, :, :, :].rearrange("p k b s -> p (k b) s"),
                                    xaT[h][:, :, :, 0:S].rearrange("p k b s -> p (k b) s"),
                                    xaT[h][:, :, :, 1:S + 1].rearrange("p k b s -> p (k b) s"), ALU.subtract).then_inc(sx_ok[h], 1)
                for f in range(5):
                    for h in halves:
                        pool.wait_ge(m2_mx[h], it * 5 + f + 1)
                        v = flat(xm[h][f]).rearrange("p (k s) -> p k s", s=S)
                        G.tensor_tensor(v, v, xaT[h][:, :, :, 1:S + 1].rearrange("p k b s -> p (k b) s"), ALU.add).then_inc(xm_ok[h], 1)
                for q in range(9):
                    for h in halves:
                        if q < 8:
                            m, jp = q // 4, q % 4
                            pool.wait_ge(set_pool, 2)
                            if q == 0:
                                pool.wait_ge(ld_s[h], it * 16 + 16)
                            if q >= 2:
                                pool.wait_ge(sc_ok[h], it * 8 + q - 1)
                            G.tensor_copy(aB[h][q % 2][:, :, :, 0], s0[h][:, m, :, 2 * jp:2 * jp + 2].rearrange("p b j -> p j b")).then_inc(a0_ok[h], 1)
                    for h in halves:
                        if q >= 1:
                            n = q - 1
                            pool.wait_ge(sc_ok[h], it * 8 + n + 1)
                            if n == 0:
                                pool.wait_ge(pk_sb[h], it * 6 + 5)
                            if n >= 2:
                                pool.wait_ge(rd_ps[h], it * 8 + n - 1)
                            r = rS[h][:, n // 4, :].rearrange("p (b s) -> p b s", b=NB)
                            for i in range(2):
                                last = G.tensor_tensor(pd[h][n % 2][:, i, :].rearrange("p (b s) -> p b s", b=NB),
                                                       st[h][n % 2][:, i, :, 0:S], r, ALU.mult)
                            last.then_inc(pd_ok[h], 1)
                for h in halves:
                    pool.wait_ge(gn_d[h], it * 4 + 3)
                    G.tensor_tensor(n3[h][:, :, :], n2[h][:, :, :], n2[h][:, :, :], ALU.mult).then_inc(gn_p[h], 1)
                for h in halves:
                    pool.wait_ge(gn_d[h], it * 4 + 4)
                    G.tensor_tensor(g2[h][:, :], g3[h][:, :], eps[:, 4:68], ALU.add).then_inc(gn_p[h], 1)
                    pool.wait_ge(gn_p[h], it * 3 + 2)
                    G.tensor_tensor(g1[h][:, :], g2[h][:, :], power[:, :], ALU.pow).then_inc(gn_p[h], 1)
                for h in halves:
                    pool.wait_ge(xt_sb[h], it * 6 + 3)
                    pool.wait_ge(pk_sb[h], it * 6 + 6)
                    G.tensor_tensor(tA[h][:, :, :], tA[h][:, :, :], gs[h][:, :, :], ALU.mult).then_inc(og_ok[h], 1)
                for h in halves:
                    pool.wait_ge(bn_b[h], it * 3 + 2)
                    inverse_root(it, h, 2, mv[h][:, :, 1], 2)
                    G.tensor_copy(xaT[h][:, :, :, 0:1], hT[h][:, :, :, 0:1]).then_inc(sh_ok[h], 1)
                for h in halves:
                    pool.wait_ge(xt_sb[h], it * 6 + 4)
                    pool.wait_ge(sh_ok[h], it * 2 + 2)
                    G.tensor_tensor(sx[h][:, :, :, :].rearrange("p k b s -> p (k b) s"),
                                    xaT[h][:, :, :, 0:S].rearrange("p k b s -> p (k b) s"),
                                    xaT[h][:, :, :, 1:S + 1].rearrange("p k b s -> p (k b) s"), ALU.subtract).then_inc(sx_ok[h], 1)
                for h in halves:
                    pool.wait_ge(ff_a[h], it * 2 + 1)
                    G.tensor_tensor(kS[h][:, :, :], rS[h][:, :, :], rS[h][:, :, :], ALU.mult).then_inc(kk_ok[h], 1)
                for h in halves:
                    pool.wait_ge(pr_sb[h], it * 6 + 4)
                    G.tensor_tensor(n2[h][:, :, :], n3[h][:, :, :], n4[h][:, :, :], ALU.add).then_inc(x2_ok[h], 1)
                for h in halves:
                    pool.wait_ge(pr_sb[h], it * 6 + 5)
                    G.tensor_tensor(n2[h][:, :, :], n1[h][:, :, :], row("bo", TT), ALU.add).then_inc(res[h], 1)
                attend(it, 1)
                for h in halves:
                    pool.wait_ge(bn_b[h], it * 3 + 3)
                    inverse_root(it, h, 3, mv[h][:, :, 1], 0)
                for h in halves:
                    pool.wait_ge(fin_ok[h], it * 4 + 1)
                    pool.wait_ge(st_out[h], it * 16 + 16)
                    G.tensor_tensor(n4[h][:, :, :], n3[h][:, :, :], row("gamma", TT), ALU.mult).then_inc(fin_ok[h], 1)
                    pool.wait_ge(fin_ok[h], it * 4 + 2)
                    G.tensor_tensor(n5[h][:, :, :], n4[h][:, :, :], row("beta", TT), ALU.add).then_inc(fin_ok[h], 2)

        @block.vector
        def _(dve):
            V = nc.vector
            dve.wait_ge(set_pool, 2)
            dve.wait_ge(ld_w, 16)
            for k in range(2):
                V.tensor_scalar(qb0m[:, k, :], wa[:, vec0 + VEC["par"][0]:vec0 + VEC["par"][0] + 2], vec("qb0", k), None, ALU.mult)
                V.tensor_scalar(qb3m[:, k, :], wa[:, vec0 + VEC["sub"][0]:vec0 + VEC["sub"][0] + 4], vec("qb3", k), None, ALU.mult)
            for name, factor in (("gnw", 0.5 * J ** 0.5), ("gnb", 0.5)):
                c = vec0 + VEC[name][0]
                V.tensor_scalar(wa[:, c:c + 2], wa[:, c:c + 2], factor, None, ALU.mult)
            V.tensor_scalar(w("fv"), w("fv"), 0.5, None, ALU.mult).then_inc(set_dve, 1)
            for h in halves:
                V.tensor_copy(g1[h][:, 0:1], vec("alpha")).then_inc(free_ps[h], 1)
            dve.wait_ge(set_pe, 1)
            V.tensor_copy(flat(m_qk[:, :, :]), ps[0][0][:, :])
            V.tensor_scalar(flat(m_vo[:, :, :]), ps[0][1][:, :], vec("alpha"), None, ALU.mult).then_inc(set_m, 1)

            def attend(it, layer):
                groups = 4 if layer == 0 else 8

                def masked(h, c):
                    at, pair = layer * NCH + c, c // 4
                    dve.wait_ge(s_ps[h], it * 16 + at + 1)
                    if c >= 2:
                        dve.wait_ge(t_ps[h], it * 16 + at - 1)
                    if layer == 0:
                        o = sc[h][c % 2].rearrange("p (b k s) -> p b k s", b=2, k=2)
                        i = ps[h][c % 2][:, :].rearrange("p (b k s) -> p b k s", b=2, k=2)
                        m = m0[h][:, 2 * pair:2 * pair + 2, :].unsqueeze(2).broadcast_to([P, 2, 2, 2 * S])
                    else:
                        o = sc[h][c % 2].rearrange("p (b k s) -> p b k s", b=2, k=4)
                        i = ps[h][c % 2][:, :].rearrange("p (b k s) -> p b k s", b=2, k=4)
                        m = m3[h][:, 2 * pair:2 * pair + 2, :].unsqueeze(2).broadcast_to([P, 2, 4, S])
                    V.tensor_tensor(o, i, m, ALU.add).then_inc(s_sb[h], 1)

                def peak(h, c):
                    at = layer * NCH + c
                    dve.wait_ge(s_sb[h], it * 16 + at + 1)
                    V.tensor_reduce(mx[h][:, c % 2, 0:groups], sc[h][c % 2].rearrange("p (g k) -> p g k", g=groups), AXX, ALU.max).then_inc(s_mx[h], 1)

                def norm(h, c):
                    at, pair, r = layer * NCH + c, c // 4, c % 4
                    dve.wait_ge(o_ps[h], it * 16 + at + 1)
                    dst = ao[h][:, 2 * pair:2 * pair + 2, :, :].rearrange("p b k (e r c) -> p (b k) e r c", e=2, r=4)[:, :, :, r, :]
                    if layer == 0:
                        o = ps[h][3][:, 0:132].rearrange("p (g c) -> p g c", c=33)
                        V.reciprocal(rc[h][:, 0:4].unsqueeze(2), o[:, :, 32:33]).then_inc(o_rc[h], 1)
                        dve.wait_ge(o_rc[h], it * 16 + at + 1)
                        V.tensor_tensor(dst, o[:, :, 0:32].rearrange("p g (e c) -> p g e c", e=2),
                                        rc[h][:, 0:4].unsqueeze(2).unsqueeze(3).broadcast_to([P, 4, 2, 16]), ALU.mult).then_inc(o_sb[h], 1)
                    else:
                        o = ps[h][3][:, 0:192].rearrange("p (g c) -> p g c", c=48)
                        V.reciprocal(rc[h][:, :].rearrange("p (g c) -> p g c", c=16), o[:, :, 32:48]).then_inc(o_rc[h], 1)
                        dve.wait_ge(o_rc[h], it * 16 + at + 1)
                        V.tensor_tensor(dst, o[:, :, 0:32].rearrange("p g (e c) -> p g e c", e=2),
                                        rc[h][:, :].rearrange("p (g c) -> p g c", c=16).unsqueeze(2).broadcast_to([P, 4, 2, 16]), ALU.mult).then_inc(o_sb[h], 1)

                for c in range(NCH + 2):
                    if c < NCH:
                        for h in halves:
                            masked(h, c)
                        for h in halves:
                            peak(h, c)
                    if c >= 2:
                        for h in halves:
                            norm(h, c - 2)

            def layer_stats(it, h, n, src):
                for t in range(TT):
                    last = V.bn_stats(bns[h][:, t, :], src[:, t, :])
                last.then_inc(bn_a[h], 1)
                dve.wait_ge(set_pool, 2)
                dve.wait_ge(bn_a[h], it * 3 + n + 1)
                for t in range(TT):
                    last = V.bn_aggr(mv[h][:, t, :], bns[h][:, t, :])
                last.then_inc(bn_b[h], 1)

            def layer_norm(it, h, n, dst, src):
                dve.wait_ge(rs_b[h], it * 4 + n + 1)
                for t in range(TT):
                    last = V.tensor_scalar(dst[:, t, :], src[:, t, :], mv[h][:, t, 0:1], rstd[h][:, t:t + 1], ALU.subtract, ALU.mult)
                return last

            with dve.Fori(0, STEPS) as it:
                for h in halves:
                    dve.wait_ge(k0_ps[h], it + 1)
                    for m in range(2):
                        last = V.tensor_scalar(kT[h][:, m, :, :].rearrange("p b s -> p (b s)"), ps[h][1 + m][:, :], vec("kb0", m), None, ALU.add)
                    last.then_inc(k0_sb[h], 1)
                for h in halves:
                    dve.wait_ge(ld_m[h], it * 16 + 16)
                    V.tensor_scalar(m0[h][:, :, 0:S], mint[h][:, :, :], 0.0, MASKED, ALU.is_equal, ALU.mult).then_inc(k0_sb[h], 1)
                for h in halves:
                    dve.wait_ge(k0_sb[h], it * 2 + 2)
                attend(it, 0)
                for h in halves:
                    dve.wait_ge(pr_ps[h], it * 6 + 1)
                    dve.wait_ge(res[h], it * 3 + 1)
                    V.tensor_tensor(n1[h][:, :, :], kn(ps[h][1]), n1[h][:, :, :], ALU.add).then_inc(pr_sb[h], 1)
                for h in halves:
                    dve.wait_ge(rs_b[h], it * 4 + 1)
                    for t in range(TT):
                        last = V.tensor_scalar(n2[h][:, t, :], n1[h][:, t, :], rstd[h][:, t:t + 1], None, ALU.mult)
                    last.then_inc(xh_ok[h], 1)
                for h in halves:
                    dve.wait_ge(pr_ps[h], it * 6 + 2)
                    dve.wait_ge(res[h], it * 3 + 2)
                    V.tensor_tensor(n4[h][:, :, :], kn(ps[h][0]), n4[h][:, :, :], ALU.add).then_inc(pr_sb[h], 1)
                    dve.wait_ge(pr_sb[h], it * 6 + 2)
                    layer_stats(it, h, 0, n4[h])
                for h in halves:
                    layer_norm(it, h, 1, n3[h], n4[h]).then_inc(xh_ok[h], 1)
                for h in halves:
                    dve.wait_ge(sx_ok[h], it * 2 + 1)
                    for k in range(2):
                        last = V.scalar_tensor_tensor(tA[h][:, k, :].rearrange("p (b s) -> p b s", b=NB), sx[h][:, k, :, :], vec("maax", k),
                                                      xaT[h][:, k, :, 1:S + 1], ALU.mult, ALU.add)
                    last.then_inc(xin_ok[h], 1)
                for f, bank in enumerate((0, 1, 3, 2, 0)):
                    for h in halves:
                        dve.wait_ge(m2_ps[h], it * 5 + f + 1)
                        for k in range(2):
                            last = V.scalar_tensor_tensor(xm[h][f][:, k, :], kn(ps[h][bank])[:, k, :], vec("stack", 2 * f + k),
                                                          sx[h][:, k, :, :].rearrange("p b s -> p (b s)"), ALU.add, ALU.mult)
                        last.then_inc(m2_mx[h], 1)
                for h in halves:
                    dve.wait_ge(pk_sb[h], it * 6 + 5)
                    for k in range(2):
                        last = V.scalar_tensor_tensor(ruk[h][:, k, :], rS[h][:, k, :], vec("u", k), kS[h][:, k, :], ALU.mult, ALU.mult)
                    last.then_inc(ruk_ok[h], 1)
                for h in halves:
                    dve.wait_ge(tg_ok[h], it * 2 + 1)
                    V.scalar_tensor_tensor(flat(gs[h][:, :, :]), flat(gs[h][:, :, :]), 1.0, ps[h][1][:, :], ALU.add, ALU.mult).then_inc(pk_sb[h], 1)
                for h in halves:
                    dve.wait_ge(cb_ps[h], it + 1)
                    V.tensor_tensor(cv[h], kn(ps[h][2]), vS[h][:, :, :], ALU.mult).then_inc(cv_ok[h], 1)
                for q in range(8):
                    for h in halves:
                        dve.wait_ge(vx_ps[h], it * 8 + q + 1)
                        for i in range(2):
                            last = V.tensor_tensor(aB[h][q % 2][:, i, :, 1:S + 1], kn(ps[h][q % 2])[:, i, :].rearrange("p (b s) -> p b s", b=NB),
                                                   kS[h][:, q // 4, :].rearrange("p (b s) -> p b s", b=NB), ALU.mult)
                        last.then_inc(a_ok[h], 1)
                    for h in halves:
                        dve.wait_ge(a_ok[h], it * 8 + q + 1)
                        dve.wait_ge(a0_ok[h], it * 8 + q + 1)
                        if q >= 2:
                            dve.wait_ge(pd_ok[h], it * 8 + q - 1)
                        for i in range(2):
                            last = V.tensor_tensor_scan(st[h][q % 2][:, i, :, :].rearrange("p b s -> p (b s)"),
                                                        wS[h][:, q // 4, :, :].rearrange("p b s -> p (b s)"),
                                                        aB[h][q % 2][:, i, :, :].rearrange("p b s -> p (b s)"), 0.0, ALU.mult, ALU.add)
                        last.then_inc(sc_ok[h], 1)
                for h in halves:
                    o = ps[h][3][:, :].rearrange("p (g j h) -> p g h j", g=4, j=J)
                    dve.wait_ge(rd_ps[h], it * 8 + 8)
                    V.tensor_reduce(g3[h][:, :].rearrange("p (g h) -> p g h", g=4), o, AXX, ALU.add).then_inc(gn_d[h], 1)
                    dve.wait_ge(gn_d[h], it * 4 + 1)
                    V.tensor_scalar(g2[h][:, :], g3[h][:, :], -1.0 / J, None, ALU.mult).then_inc(gn_d[h], 1)
                    dve.wait_ge(gn_d[h], it * 4 + 2)
                    V.tensor_tensor(n2[h][:, :, :].rearrange("p t (m h j) -> p (t m) h j", m=2, j=J), o,
                                    g2[h][:, :].rearrange("p (g h) -> p g h", g=4).unsqueeze(3).broadcast_to([P, 4, HT, J]), ALU.add).then_inc(gn_d[h], 1)
                for h in halves:
                    dve.wait_ge(gn_p[h], it * 3 + 1)
                    V.tensor_reduce(g3[h][:, :], n3[h][:, :, :].rearrange("p t (h j) -> p (t h) j", j=J), AXX, ALU.add).then_inc(gn_d[h], 1)
                for h in halves:
                    dve.wait_ge(gn_p[h], it * 3 + 3)
                    V.tensor_tensor(n3[h][:, :, :].rearrange("p t (h j) -> p (t h) j", j=J), n2[h][:, :, :].rearrange("p t (h j) -> p (t h) j", j=J),
                                    g1[h][:, :].unsqueeze(2).broadcast_to([P, 64, J]), ALU.mult).then_inc(xh_ok[h], 1)
                for h in halves:
                    dve.wait_ge(pr_ps[h], it * 6 + 3)
                    V.tensor_tensor(n4[h][:, :, :], kn(ps[h][1]), n4[h][:, :, :], ALU.add).then_inc(pr_sb[h], 1)
                    dve.wait_ge(pr_sb[h], it * 6 + 3)
                    layer_stats(it, h, 1, n4[h])
                for h in halves:
                    layer_norm(it, h, 2, n3[h], n4[h]).then_inc(xh_ok[h], 1)
                for h in halves:
                    dve.wait_ge(sx_ok[h], it * 2 + 2)
                    for name, dst in (("fmk", tA), ("fmr", th)):
                        for k in range(2):
                            last = V.scalar_tensor_tensor(dst[h][:, k, :].rearrange("p (b s) -> p b s", b=NB), sx[h][:, k, :, :], vec(name, k),
                                                          xaT[h][:, k, :, 1:S + 1], ALU.mult, ALU.add)
                        last.then_inc(ff_d[h], 1)
                    V.memset(pbd[h], 0.0)
                for h in halves:
                    dve.wait_ge(pr_ps[h], it * 6 + 4)
                    dve.wait_ge(tg_ok[h], it * 2 + 2)
                    V.scalar_tensor_tensor(flat(n3[h][:, :, :]), flat(gs[h][:, :, :]), 1.0, ps[h][1][:, :], ALU.add, ALU.mult).then_inc(pr_sb[h], 1)
                for h in halves:
                    dve.wait_ge(l2_ps[h], it * 5 + 3)
                    V.tensor_reduce(rstd[h][:, :], ps[h][1][:, 0:2 * S].rearrange("p (t s) -> p t s", t=2), AXX, ALU.max).then_inc(l2_mx[h], 1)
                    dve.wait_ge(l2_mx[h], it * 3 + 1)
                    V.tensor_scalar(vtmp[h][:, :], rstd[h][:, :], -1.0 / 16.0, None, ALU.mult).then_inc(l2_mx[h], 1)
                for h in halves:
                    dve.wait_ge(ff_a[h], it * 2 + 2)
                    V.reciprocal(rstd[h][:, :], ssq[h][:, :]).then_inc(l2_mx[h], 1)
                for h in halves:
                    dve.wait_ge(pr_ps[h], it * 6 + 5)
                    dve.wait_ge(x2_ok[h], it + 1)
                    dve.wait_ge(l2_mx[h], it * 3 + 3)
                    for t in range(TT):
                        last = V.scalar_tensor_tensor(n1[h][:, t, :], kn(ps[h][2])[:, t, :], rstd[h][:, t:t + 1], n2[h][:, t, :], ALU.mult, ALU.add)
                    last.then_inc(pr_sb[h], 1)
                for h in halves:
                    dve.wait_ge(kv3_ps[h], it * 2 + 2)
                    for e in range(2):
                        g = slice(64 * e, 64 * e + 64)
                        dst = v3[h][g, :, :, 0:32].rearrange("p b r (v e c) -> p (b r) v e c", v=2, e=2)[:, :, :, e, :]
                        last = V.tensor_copy(dst, ps[h][0][g, 0:NT].rearrange("p (b e v c) -> p b e v c", e=2, v=2, c=W3)[:, :, e, :, :])
                    last.then_inc(kv3_d[h], 1)
                for h in halves:
                    dve.wait_ge(ld_3[h], it * 32 + 32)
                attend(it, 1)
                for h in halves:
                    dve.wait_ge(pr_ps[h], it * 6 + 6)
                    dve.wait_ge(res[h], it * 3 + 3)
                    V.tensor_tensor(n1[h][:, :, :], kn(ps[h][1]), n2[h][:, :, :], ALU.add).then_inc(pr_sb[h], 1)
                    dve.wait_ge(pr_sb[h], it * 6 + 6)
                    layer_stats(it, h, 2, n1[h])
                for h in halves:
                    layer_norm(it, h, 3, n3[h], n1[h]).then_inc(fin_ok[h], 1)
                for h in halves:
                    V.tensor_copy(g1[h][:, 0:1], vec("alpha")).then_inc(free_ps[h], 1)


def pack(weights, table):
    return np.concatenate([weights[name] for name, _ in table], axis=1)


def kernel(**inputs):
    import concourse.bacc as bacc
    from concourse.bass_utils import run_bass_kernel_spmd

    a = {k: np.asarray(v) for k, v in inputs.items()}
    f = np.float32
    ctx, x = a["ctx_2048"], a["x"]
    L0, L1, L2, L3 = ({k[len(p):]: v for k, v in a.items() if k.startswith(p)}
                      for p in ("L0_xattn_", "L1_xattn_", "L2_xattn_", "L3_xattn_"))

    def fold(m):
        tiles = -(-m.shape[0] // P)
        m = np.concatenate([m, np.zeros((tiles * P - m.shape[0], m.shape[1]), f)])
        return m.reshape(tiles, P, -1).transpose(1, 0, 2).reshape(P, -1)

    def cols(v):
        return v.reshape(-1, P).T

    p = np.arange(P)
    tile = np.arange(2)[:, None]
    o0 = (tile * P + (p % 64 // 16) * 32 + p // 64 * 16 + p % 16).reshape(-1)
    q3 = ((p % 64 // 8 * 4 + tile * 2 + p // 64) * 8 + p % 8).reshape(-1)
    r = p % 64 // 16
    kv = r % 2 * 4 + p % 16 // 8 * 2 + p // 64
    o3 = ((kv * 4 + tile * 2 + r // 2) * 8 + p % 8).reshape(-1)
    v3 = np.broadcast_to(kv * 8 + p % 8, (2, P)).reshape(-1)

    kvw = L0["kv_w"].reshape(C, C, 2)
    kvb = L0["kv_b"].reshape(C, 2)
    head = p // J
    same = (head[:, None] == head[None, :]).astype(f)
    weights = {
        "ident": np.eye(P, dtype=f), "q0": fold(L0["q_w"]), "k0": fold(kvw[:, :, 0]), "v0": fold(kvw[:, :, 1]),
        "o0": fold(L0["out_w"][o0]), "w1": fold(L0["mlp_w1"]), "w2": fold(L0["mlp_w2"]),
        "m1": fold(L1["maa_w1"]), "m2": fold(L1["maa_w2"].reshape(5 * 32, C)),
        "td1": fold(L1["td_w1"]), "td2": fold(L1["td_w2"]),
        "wk": fold(L1["Wk"].T), "wv": fold(L1["Wv"].T), "wr": fold(L1["Wr"].T), "wg": fold(L1["Wg"].T),
        "wo": fold(L1["Wo"].T), "fk": fold(L1["Wfk"].T), "fr": fold(L1["Wfr"].T), "fv": fold(L1["Wfv"].T),
        "q3": fold(L3["Wq"][:, q3]), "k3": fold(np.concatenate([L3["Wk"], L3["Wk"]], axis=1)), "v3": fold(L3["Wv"]),
        "o3": fold(L3["Wo"][o3]),
        "l2q": fold(L2["w_q"]), "l2k": fold(L2["w_k"]), "l2v": fold(L2["w_v"]), "l2o": fold(L2["w_o"].T),
        "sumh": (head[:, None] == np.arange(HT)).astype(f), "blk": same,
        "spread": np.concatenate([same * (p % J == j).astype(f)[:, None] for j in range(J)], axis=1),
        "perm": (p[:, None] == (p % HT * J + p // HT)[None, :]).astype(f),
    }
    vectors = {
        "qb0": cols(L0["q_b"]), "kb0": cols(kvb[:, 0]), "vb0": cols(kvb[:, 1][o0]), "pn": cols(L0["postnorm_w"]),
        "b1": cols(L0["mlp_b1"]), "ln1w": cols(L1["ln1_w"]), "ln1b": cols(L1["ln1_b"]), "ln2w": cols(L1["ln2_w"]),
        "ln2b": cols(L1["ln2_b"]), "maax": cols(L1["maa_x"]), "stack": cols(L1["maa_stack"]),
        "td": cols(L1["time_decay"]), "u": cols(L1["u"]), "gnw": cols(L1["gn_w"]), "gnb": cols(L1["gn_b"]),
        "fmk": cols(L1["ffn_maa_k"]), "fmr": cols(L1["ffn_maa_r"]), "qb3": cols(L3["bq"][q3]),
        "kb3": cols(np.concatenate([L3["bk"], L3["bk"]])), "vb3": cols(L3["bv"][v3]),
        "par": (p[:, None] % 32 // 16 == np.arange(2)).astype(f) / W0,
        "sub": (p[:, None] % 32 // 8 == np.arange(4)).astype(f) / f(W3 ** 0.5),
        "alpha": np.broadcast_to(L2["alpha"].reshape(1, 1), (P, 1)),
    }
    vec = np.concatenate([vectors[n] for n in VEC], axis=1)
    weights["vec"] = np.concatenate([vec, np.zeros((P, 64 - vec.shape[1]), f)], axis=1)

    h = np.concatenate([ctx, x], axis=1).transpose(2, 0, 1).reshape(KT, P, B, 2 * S).transpose(1, 0, 2, 3)
    arrays = {
        "h": h, "x": x.reshape(-1, P, C).transpose(1, 0, 2), "mask": a["mask_BxS2_ik0"],
        "amask": a["mask_Bx1xSxS2_ff0"].reshape(B, S, S),
        "s0": ctx[:, 2:2 + J].reshape(B, KT, P, J).transpose(2, 1, 0, 3),
        "wa": pack(weights, WEIGHTS_A), "wb": pack(weights, WEIGHTS_B), "nat": pack(weights, NAT),
        "rows": np.stack([L0["out_b"], L0["mlp_b2"], L3["bo"], L3["gamma"], L3["beta"]]),
    }
    arrays = {k: np.ascontiguousarray(v) for k, v in arrays.items()}

    nc = bacc.Bacc("TRN2", target_bir_lowering=False, num_devices=1)
    args = [nc.dram_tensor(f"in_{k}", v.shape, mybir.dt.from_np(v.dtype), kind="ExternalInput").ap() for k, v in arrays.items()]
    out = nc.dram_tensor("result", (P, B * S // P, C), F32, kind="ExternalOutput").ap()
    build(nc, *args, out)
    got = run_bass_kernel_spmd(nc, [{f"in_{k}": v for k, v in arrays.items()}], core_ids=[0]).results[0]["result"]
    return np.asarray(got).transpose(1, 0, 2).reshape(B, S, C)
```

```python
import numpy as np
import concourse.bass as bass
from concourse import mybir
from concourse.alu_op_type import AluOpType as ALU
from contextlib import ExitStack

F32 = mybir.dt.float32
I32 = mybir.dt.int32
ACT = mybir.ActivationFunctionType
AXX = mybir.AxisListType.X

B, S, C = 64, 64, 256
P = 128
KT = C // P
NB = 4
NT = NB * S
TT = NT // P
STEPS = B // (2 * NB)
NCH = 8
J = 8
HT = P // J
HID = 4 * C
W0 = 16
W3 = 8
MASKED = -1.0e30
NEWTON = 4
GN = 3 + 2 + 2 + 3 * NEWTON

WEIGHTS_A = [("ident", P), ("q0", 2 * C), ("k0", 2 * C), ("v0", 2 * C), ("o0", 2 * C), ("vec", 64), ("fv", 2 * C), ("ones3", 64), ("bv3", 64)]
WEIGHTS_B = [("w1", 2 * HID), ("w2", 8 * C),
             ("m1", 2 * 160), ("m2", 2 * C), ("td1", 2 * 64), ("td2", C),
             ("wk", 2 * C), ("wv", 2 * C), ("wr", 2 * C), ("wg", 2 * C), ("wo", 2 * C),
             ("fk", 2 * C), ("fr", 2 * C),
             ("q3", 2 * C), ("k3", 2 * P), ("v3", 2 * 64), ("o3", 2 * C),
             ("sumh", HT), ("blk", P), ("perm", P)]
NAT = [("l2q", 2 * C), ("l2k", 2 * C), ("l2v", 2 * C), ("l2o", 2 * C)]
VEC = {}
for _n, _w in [("qb0", 2), ("kb0", 2), ("vb0", 2), ("pn", 2), ("b1", 8), ("ln1w", 2), ("ln1b", 2),
               ("ln2w", 2), ("ln2b", 2), ("maax", 2), ("stack", 10), ("td", 2), ("u", 2),
               ("gnw", 2), ("gnb", 2), ("fmk", 2), ("fmr", 2), ("qb3", 2), ("kb3", 1),
               ("par", 2), ("sub", 4), ("alpha", 1)]:
    VEC[_n] = (sum(w for _, w in VEC.values()), _w)
ROWS = ["out_b", "mlp_b2", "bo", "gamma", "beta"]

FIRST = [("q0", 0, 2), ("k0", 0, 3.5), ("v0", 0, 3.5)] \
    + [("att0", c, 3.2) for c in range(NCH + 2)] + [("merge0", 0, 2), ("out0", 0, 3), ("zturn", 0, 4)] \
    + [("up", i, 1.8) for i in range(4)] + [("down", 0, 3.5), ("down", 1, 4), ("xturn", 0, 5)] \
    + [("mix1", 0, 4)] + [("mix2", f, 1.5) for f in range(5)] \
    + [(n, 0, 2) for n in ("pk", "pw1", "pv", "pw2", "pr", "pg")]
SECOND = [("ruk", 0, 1)] + [("scan", q, 3) for q in range(9)] \
    + [("gturn", 0, 9), ("outg", 0, 6), ("cturn", 0, 6)] \
    + [(n, 0, 2.2) for n in ("fk", "l2k", "fr", "l2v", "fv", "x2turn", "l2s", "l2p", "l2o", "k3", "v3")] \
    + [("x3turn", 0, 2), ("q3", 0, 3)] + [("att1", c, 3.2) for c in range(NCH + 2)] + [("out3", 0, 6)]


def weave(a, b):
    rows = []
    for half, ahead, stages in (a, b):
        whole, at = sum(s[2] for s in stages), 0.0
        for name, i, length in stages:
            rows.append((at / whole, half, ahead, name, i))
            at += length
    return [r[1:] for r in sorted(rows, key=lambda r: r[0])]


HEAD = [(0, 0, name, i) for name, i, _ in FIRST]
BODY = weave((0, 0, SECOND), (1, 0, FIRST)) + weave((0, 1, FIRST), (1, 0, SECOND))
TAIL = weave((0, 0, SECOND), (1, 0, FIRST)) + [(1, 0, name, i) for name, i, _ in SECOND]


class Step:

    def __init__(self, count, ahead):
        self.count, self.ahead = count, ahead

    def __mul__(self, k):
        return Step(self.count * k, self.ahead * k)

    def __add__(self, c):
        return self.count + (self.ahead + c) if self.ahead + c else self.count


def run(engine, stage):
    for half, ahead, name, i in HEAD:
        stage(name, i, half, ahead)
    with engine.Fori(0, STEPS - 1) as it:
        for half, ahead, name, i in BODY:
            stage(name, i, half, Step(it + half, ahead - half))
    for half, ahead, name, i in TAIL:
        stage(name, i, half, STEPS - 1)


def columns(table):
    at, out = 0, {}
    for name, width in table:
        out[name] = (at, width)
        at += width
    return out, at


def build(nc, h_d, x_d, mask_d, amask_d, s0_d, wa_d, wb_d, nat_d, rows_d, out_d):
    ca, na = columns(WEIGHTS_A)
    cb, nb = columns(WEIGHTS_B)
    cn, nn = columns(NAT)


    with ExitStack() as ctx:
        def sb(name, shape, dt=F32):
            return ctx.enter_context(nc.sbuf_tensor(name, shape, dt))

        def sem(name):
            return ctx.enter_context(nc.semaphore(name))

        def sems(name):
            return [sem(f"{name}_{h}") for h in range(2)]

        def sbs(name, shape, dt=F32):
            return [sb(f"{name}_{h}", shape, dt) for h in range(2)]

        wa = sb("wa", [P, na])
        wb = sb("wb", [P, nb])

        def w(name, k=None):
            t, (at, n) = (wa, ca[name]) if name in ca else (wb, cb[name])
            v = t[:, at:at + n]
            return v if k is None else v.rearrange("p (k n) -> p k n", k=2)[:, k, :]

        ident = w("ident")
        vec0 = ca["vec"][0]

        def vec(name, k=0):
            c = vec0 + VEC[name][0] + k
            return wa[:, c:c + 1]

        w2 = w("w2").rearrange("p (m n) -> p m n", m=8)
        rows = sb("rows", [P, len(ROWS), C])

        def row(name, n):
            return rows[:, ROWS.index(name), :].unsqueeze(1).broadcast_to([P, n, C])

        m_qk = sb("m_qk", [P, 2, C])
        m_vo = sb("m_vo", [P, 2, C])
        qb0m = sb("qb0m", [P, 2, 2])
        qb3s = sb("qb3s", [P, 2])
        kb3m = sb("kb3m", [P, 4])
        eps = sb("eps", [P, 4])
        power = sb("power", [P, TT])

        hT = sbs("hT", [P, KT, NB, 2 * S])
        xN = sbs("xN", [P, TT, C])
        mint = sbs("mint", [P, NB, S], I32)
        m0 = sbs("m0", [P, NB, 2 * S])
        m3 = sbs("m3", [P, NB, S])
        s0 = sbs("s0", [P, KT, NB, J])
        big = sbs("big", [P, 2560])
        att = sbs("att", [P, 3584])
        v0 = sbs("v0s", [P, NB, 8, 33])
        v3 = sbs("v3s", [P, NB, 2, 2, 32])
        xaT = sbs("xaT", [P, KT, NB, S + 1])
        sx = sbs("sx", [P, KT, NB, S])
        tA = sbs("tA", [P, KT, NT])
        th = sbs("th", [P, 2, NT])
        kS = sbs("kS", [P, KT, NT])
        vS = sbs("vS", [P, KT, NT])
        rS = sbs("rS", [P, KT, NT])
        gs = sbs("gs", [P, KT, NT])
        wS = sbs("wS", [P, KT, NB, S + 1])
        n1 = sbs("n1", [P, TT, C])
        n2 = sbs("n2", [P, TT, C])
        n3 = sbs("n3", [P, TT, C])
        n4 = sbs("n4", [P, TT, C])
        n5 = sbs("n5", [P, TT, C])
        bns = sbs("bns", [P, TT, 6])
        mv = sbs("mv", [P, TT, 2])
        rstd = sbs("rstd", [P, TT])
        vtmp = sbs("vtmp", [P, TT])
        ssq = sbs("ssq", [P, TT])
        mx = sbs("mx", [P, 2, 8])
        rc = sbs("rc", [P, 2 * P])
        g1 = sbs("g1", [P, 64])
        g2 = sbs("g2", [P, 64])
        g3 = sbs("g3", [P, 64])
        ps = [[ctx.enter_context(nc.psum_tensor(f"ps{h}{k}", [P, 512], F32)) for k in range(4)] for h in range(2)]

        sc = [[a[:, 512 * i:512 * (i + 1)] for i in range(2)] for a in att]
        pt = [a[:, 1024:1536] for a in att]
        ao = [a[:, 1536:2560].rearrange("p (b k c) -> p b k c", b=NB, k=2) for a in att]
        kT = [a[:, 2560:3584].rearrange("p (k b s) -> p k b s", k=2, b=NB) for a in att]
        kz3 = [a[:, 2560:3584].rearrange("p (b v s) -> p b v s", b=NB, v=4) for a in att]
        aB = [[a[:, 520 * i:520 * (i + 1)].rearrange("p (j b s) -> p j b s", j=2, b=NB) for i in range(2)] for a in att]
        st = [[a[:, 1040 + 520 * i:1560 + 520 * i].rearrange("p (j b s) -> p j b s", j=2, b=NB) for i in range(2)] for a in att]
        pd = [[a[:, 2080 + 512 * i:2592 + 512 * i].rearrange("p (j n) -> p j n", j=2) for i in range(2)] for a in att]
        qz = [a[:, 0:1024].rearrange("p (k b v s) -> p k b v s", k=2, v=2, b=NB) for a in big]
        q3T = [a[:, 0:512].rearrange("p (k n) -> p k n", k=2) for a in big]
        hid = [a[:, 0:2048].rearrange("p (m n) -> p m n", m=8) for a in big]
        xm = [[a[:, 512 * j:512 * (j + 1)].rearrange("p (k n) -> p k n", k=2) for j in range(5)] for a in big]
        ruk = [x[0] for x in xm]
        vx = [x[2:5] for x in xm]
        cv = [x[1] for x in xm]
        tS = [x[0] for x in xm]
        uS = [x[1] for x in xm]
        pbd = [x[2].rearrange("p k n -> p (k n)")[:, 0:256].rearrange("p (t n) -> p t n", t=2) for x in xm]
        ptb = [x[3].rearrange("p k n -> p (k n)")[:, 0:256].rearrange("p (t n) -> p t n", t=2) for x in xm]

        def flat(t):
            return t.rearrange("p k n -> p (k n)")

        def kn(bank):
            return bank[:, :].rearrange("p (k n) -> p k n", k=2)

        ld_w, ld_wb, ld_nat, ld_rows = sem("ld_w"), sem("ld_wb"), sem("ld_nat"), sem("ld_rows")
        set_pool, set_dve, set_pe, set_m = sem("set_pool"), sem("set_dve"), sem("set_pe"), sem("set_m")
        ld_h, ld_x, ld_m, ld_3, ld_s = sems("ld_h"), sems("ld_x"), sems("ld_m"), sems("ld_3"), sems("ld_s")
        st_out = sems("st_out")
        free_ps = sems("free_ps")
        qkv_ps = sems("qkv_ps")
        qv_sb, k0_sb = sems("qv_sb"), sems("k0_sb")
        s_ps, s_sb, s_mx, s_sub, s_exp = sems("s_ps"), sems("s_sb"), sems("s_mx"), sems("s_sub"), sems("s_exp")
        t_ps, t_sb, o_ps, o_rc, o_sb = sems("t_ps"), sems("t_sb"), sems("o_ps"), sems("o_rc"), sems("o_sb")
        mg_ps, mg_sb = sems("mg_ps"), sems("mg_sb")
        rc_ok = sems("rc_ok")
        res = sems("res")
        pr_ps, pr_sb = sems("pr_ps"), sems("pr_sb")
        sq_ok, rs_a, rs_b = sems("sq_ok"), sems("rs_a"), sems("rs_b")
        bn_a, bn_b = sems("bn_a"), sems("bn_b")
        xh_ok = sems("xh_ok")
        xt_ps, xt_sb = sems("xt_ps"), sems("xt_sb")
        h_ps, h_sb = sems("h_ps"), sems("h_sb")
        sx_ok, xin_ok = sems("sx_ok"), sems("xin_ok")
        m1_ps, m1_sb, m2_ps, m2_mx, xm_ok = sems("m1_ps"), sems("m1_sb"), sems("m2_ps"), sems("m2_mx"), sems("xm_ok")
        pk_ps, pk_sb = sems("pk_ps"), sems("pk_sb")
        e1_ok, tg_ok = sems("e1_ok"), sems("tg_ok")
        ruk_ok, cb_ps, cv_ok = sems("ruk_ok"), sems("cb_ps"), sems("cv_ok")
        a0_ok, a_ok, sc_ok, pd_ok, rd_ps = sems("a0_ok"), sems("a_ok"), sems("sc_ok"), sems("pd_ok"), sems("rd_ps")
        vx_ok = [[sem(f"vx_ok_{h}{i}") for i in range(3)] for h in range(2)]
        gn_d, gn_p, og_ok = sems("gn_d"), sems("gn_p"), sems("og_ok")
        ff_ps, ff_a, kk_ok, ff_d = sems("ff_ps"), sems("ff_a"), sems("kk_ok"), sems("ff_d")
        x2_ok = sems("x2_ok")
        l2_ps, l2_sb = sems("l2_ps"), sems("l2_sb")
        l2_mx = sems("l2_mx")
        kv3_ps, kv3_a, kv3_d = sems("kv3_ps"), sems("kv3_a"), sems("kv3_d")
        fin_ok = sems("fin_ok")

        block = ctx.enter_context(nc.Block())
        halves = range(2)

        @block.sync
        def _(sp):
            def load(n, h):
                b0 = n * (2 * NB) + h * NB
                sp.dma_start(hT[h][:, :, :, :], h_d[:, :, bass.ds(b0, NB), :]).then_inc(ld_h[h], 16)
                sp.dma_start(xN[h][:, :, :], x_d[:, bass.ds(n * (2 * TT) + h * TT, TT), :]).then_inc(ld_x[h], 16)
                sp.dma_start(mint[h][:, :, :], mask_d[bass.ds(b0, NB), :].unsqueeze(0).broadcast_to([P, NB, S])).then_inc(ld_m[h], 16)
                sp.dma_start(s0[h][:, :, :, :], s0_d[:, :, bass.ds(b0, NB), :]).then_inc(ld_s[h], 16)

            def load_mask(n, h):
                b0 = n * (2 * NB) + h * NB
                for d in range(2):
                    sp.dma_start(m3[h][64 * d:64 * d + 64, :, :],
                                 amask_d[bass.ds(b0, NB), :, :].rearrange("b q k -> q b k")).then_inc(ld_3[h], 16)

            def copy_v(h, q):
                m, jp = q // 4, q % 4
                for i in range(2):
                    src = vS[h][2 * jp + i::J, m, :].unsqueeze(1).broadcast_to([HT, J, NT])
                    sp.dma_start(vx[h][q % 3][:, i, :], src).then_inc(vx_ok[h][q % 3], 16)

            def stage(name, i, h, n):
                if name == "ruk":
                    sp.wait_ge(pk_sb[h], n * 6 + 3)
                    copy_v(h, 0)
                    sp.wait_ge(pk_ps[h], n * 6 + 5)
                    copy_v(h, 1)
                    sp.wait_ge(pk_ps[h], n * 6 + 6)
                    copy_v(h, 2)
                if name == "scan" and i + 3 < 8:
                    sp.wait_ge(a_ok[h], n * 8 + i + 1)
                    copy_v(h, i + 3)
                last = isinstance(n, int) and n == STEPS - 1
                if name == "q3" and not last:
                    sp.wait_ge(kv3_ps[h], n * 2 + 2)
                    load(n + 1, h)
                if name == "out3":
                    if not last:
                        sp.wait_ge(s_sb[h], n * 16 + 16)
                        load_mask(n + 1, h)
                    sp.wait_ge(fin_ok[h], n * 4 + 4)
                    sp.dma_start(out_d[:, bass.ds(n * (2 * TT) + h * TT, TT), :], n5[h][:, :, :]).then_inc(st_out[h], 16)

            sp.dma_start(wa[:, :], wa_d).then_inc(ld_w, 16)
            load(0, 0)
            sp.dma_start(att[1][:, 0:nn], nat_d).then_inc(ld_nat, 16)
            sp.dma_start(rows[:, :, :], rows_d.unsqueeze(0).broadcast_to([P, len(ROWS), C])).then_inc(ld_rows, 16)
            sp.dma_start(wb[:, :], wb_d).then_inc(ld_wb, 16)
            load(0, 1)
            for h in halves:
                load_mask(0, h)
            run(sp, stage)
            for h in halves:
                sp.wait_ge(st_out[h], 16 * STEPS + 16)

        @block.tensor
        def _(pe):
            mm = nc.tensor.matmul

            def dense_T(out, weight, rhs):
                for m in range(2):
                    for k in range(2):
                        last = mm(out[:, m, :], weight(k)[:, m * P:(m + 1) * P], rhs(k), start=(k == 0), stop=(k == 1))
                return last

            def dense_N(out, lhs, weight, ks=2, tiles=range(TT)):
                for t in tiles:
                    for k in range(ks):
                        last = mm(out[:, t, :], lhs(k, t), weight(k), start=(k == 0), stop=(k == ks - 1))
                return last

            def turn_rows(h, bank, src):
                for t in range(TT):
                    for k in range(KT):
                        last = nc.tensor.transpose(kn(ps[h][bank])[:, k, t * P:(t + 1) * P], src[:, t, k * P:(k + 1) * P], ident)
                last.then_inc(xt_ps[h], 1)

            def tok(t):
                return slice(t * P, (t + 1) * P)

            def chunk_scores(n, h, layer, c):
                at, pair, r = layer * NCH + c, c // 4, c % 4
                g = slice(32 * r, 32 * r + 32)
                out = ps[h][c % 2]
                if c >= 2:
                    pe.wait_ge(s_sb[h], n * 16 + at - 1)
                for i in range(2):
                    b = 2 * pair + i
                    for k in range(2):
                        if layer == 0:
                            last = mm(out[:, (2 * i + k) * P:(2 * i + k + 1) * P], qz[h][g, k, b, :, :].rearrange("p v s -> p (v s)"),
                                      kT[h][g, k, b, :], start=True, stop=True)
                        else:
                            last = mm(out[k * S:(k + 1) * S, i * 4 * S:(i + 1) * 4 * S], q3T[h][g, k, b * S:(b + 1) * S],
                                      kz3[h][g, b, :, :].rearrange("p v s -> p (v s)"), start=True, stop=True)
                last.then_inc(s_ps[h], 1)

            def chunk_turn(n, h, layer, c):
                at = layer * NCH + c
                pe.wait_ge(s_exp[h], n * 16 + at + 1)
                if c >= 1:
                    pe.wait_ge(t_sb[h], n * 16 + at)
                for i in range(4):
                    last = nc.tensor.transpose(ps[h][2][:, i * P:(i + 1) * P], sc[h][c % 2][:, i * P:(i + 1) * P], ident)
                last.then_inc(t_ps[h], 1)

            def chunk_values(n, h, layer, c):
                at, pair, r = layer * NCH + c, c // 4, c % 4
                pe.wait_ge(t_sb[h], n * 16 + at + 1)
                if layer == 0:
                    if c >= 1:
                        pe.wait_ge(o_sb[h], n * 16 + c)
                    for i in range(4):
                        b, k = 2 * pair + i // 2, i % 2
                        last = mm(ps[h][3][:, 33 * i:33 * i + 33], pt[h][:, i * P:(i + 1) * P],
                                  v0[h][:, b, 4 * k + r, :], start=True, stop=True)
                else:
                    if c == 4:
                        pe.wait_ge(o_sb[h], n * 16 + at)
                    g = slice(32 * r, 32 * r + 32)
                    for i in range(2):
                        for v in range(2):
                            mm(ps[h][3][g, i * P:(i + 1) * P], v3[h][:, 2 * pair + i, r % 2, v, :],
                               pt[h][:, (2 * i + v) * P:(2 * i + v + 1) * P], start=(v == 0), stop=(v == 1))
                    for v in range(2):
                        last = mm(ps[h][3][g, 2 * P:4 * P], w("ones3")[:, 32 * v:32 * v + 32],
                                  pt[h].rearrange("p (i v n) -> p v i n", i=2, v=2)[:, v, :, :], start=(v == 0), stop=(v == 1))
                last.then_inc(o_ps[h], 1)

            def merge(n, h):
                all_out = n * 16 + NCH
                pe.wait_ge(set_pool, 2)
                pe.wait_ge(o_sb[h], all_out)
                out = ps[h][0][:, :].rearrange("p (k b s) -> p k b s", k=2, b=NB)
                for e in range(2):
                    g = slice(64 * e, 64 * e + 64)
                    for b in range(NB):
                        for k in range(2):
                            last = mm(out[g, k, b, :], ao[h][g, b, k, 64 * e:64 * e + 64], ident[g, g], start=True, stop=True)
                last.then_inc(mg_ps[h], 1)

            def gather(n, h, q):
                m, jp = q // 4, q % 4
                out = ps[h][3][:, :].rearrange("p (t m j h) -> p t m j h", t=TT, m=2, j=J)
                if q == 0:
                    pe.wait_ge(cv_ok[h], n + 1)
                    pe.wait_ge(pk_sb[h], n * 6 + 4)
                    for t in range(TT):
                        for k in range(KT):
                            mm(out[:, t, k, :, :].rearrange("p j h -> p (j h)"), cv[h][:, k, tok(t)], w("perm"),
                               start=(t == 0 and k == 0), stop=False, skip_group_check=True)
                pe.wait_ge(pd_ok[h], n * 8 + q + 1)
                for i in range(2):
                    for t in range(TT):
                        last = mm(out[:, t, m, 2 * jp + i, :], pd[h][q % 2][:, i, tok(t)], w("sumh"), start=False,
                                  stop=(q == 7 and i == 1 and t == TT - 1), skip_group_check=True)
                last.then_inc(rd_ps[h], 1)

            MIX_BANK = (0, 1, 3, 2, 0)
            UP_BANK = (0, 1, 3, 2)

            def stage(name, i, h, n):
                if name == "q0":
                    pe.wait_ge(ld_h[h], n * 16 + 16)
                    pe.wait_ge(free_ps[h], n + 1)
                    dense_T(kn(ps[h][0]), lambda k: w("q0", k), lambda k: hT[h][:, k, :, S:2 * S]).then_inc(qkv_ps[h], 1)
                elif name == "k0":
                    for m in range(2):
                        for k in range(2):
                            last = mm(ps[h][1 + m][:, :], w("k0", k)[:, m * P:(m + 1) * P], hT[h][:, k, :, :], start=(k == 0), stop=(k == 1))
                    last.then_inc(qkv_ps[h], 1)
                elif name == "v0":
                    for b in range(NB):
                        if b == 2:
                            pe.wait_ge(qv_sb[h], n * 3 + 1)
                        for k in range(2):
                            last = mm(kn(ps[h][3 if b < 2 else 0])[:, b % 2, :], hT[h][:, k, b, :], w("v0", k), start=(k == 0), stop=(k == 1))
                        if b % 2:
                            last.then_inc(qkv_ps[h], 1)
                elif name in ("att0", "att1"):
                    layer = 0 if name == "att0" else 1
                    if i == 0:
                        if layer == 0:
                            pe.wait_ge(k0_sb[h], n * 2 + 1)
                            pe.wait_ge(qv_sb[h], n * 3 + 3)
                        else:
                            pe.wait_ge(kv3_a[h], n * 2 + 2)
                            pe.wait_ge(kv3_d[h], n + 1)
                    if i < NCH:
                        chunk_scores(n, h, layer, i)
                    if 1 <= i <= NCH:
                        chunk_turn(n, h, layer, i - 1)
                    if i >= 2:
                        chunk_values(n, h, layer, i - 2)
                elif name == "merge0":
                    merge(n, h)
                elif name == "out0":
                    pe.wait_ge(mg_sb[h], n + 1)
                    dense_N(kn(ps[h][1]), lambda k, t: tA[h][:, k, tok(t)], lambda k: w("o0", k)).then_inc(pr_ps[h], 1)
                elif name == "zturn":
                    pe.wait_ge(xh_ok[h], n * 4 + 1)
                    turn_rows(h, 2, n2[h])
                elif name == "up":
                    if i == 0:
                        pe.wait_ge(ld_wb, 16)
                        pe.wait_ge(xt_sb[h], n * 6 + 1)
                    for m in range(2):
                        mt = 2 * i + m
                        for k in range(2):
                            last = mm(kn(ps[h][UP_BANK[i]])[:, m, :], w("w1", k)[:, mt * P:(mt + 1) * P], tA[h][:, k, :], start=(k == 0), stop=(k == 1))
                    last.then_inc(h_ps[h], 1)
                elif name == "down":
                    pe.wait_ge(h_sb[h], n * 4 + 4)
                    last = dense_N(kn(ps[h][0]), lambda k, t: hid[h][:, k, tok(t)], lambda k: w2[:, k, :], ks=8, tiles=[i])
                    if i == 1:
                        last.then_inc(pr_ps[h], 1)
                elif name == "xturn":
                    pe.wait_ge(xh_ok[h], n * 4 + 2)
                    turn_rows(h, 1, n3[h])
                elif name == "mix1":
                    pe.wait_ge(xin_ok[h], n + 1)
                    for m in range(2):
                        wide = P if m == 0 else 32
                        for k in range(2):
                            last = mm(kn(ps[h][2])[0:wide, m, :], w("m1", k)[:, m * P:m * P + wide], tA[h][:, k, :], start=(k == 0), stop=(k == 1))
                    last.then_inc(m1_ps[h], 1)
                elif name == "mix2":
                    if i == 0:
                        pe.wait_ge(m1_sb[h], n + 1)
                    if i == 4:
                        pe.wait_ge(m2_mx[h], n * 5 + 1)
                    g = slice(32 * (i % 4), 32 * (i % 4) + 32)
                    for m in range(2):
                        last = mm(kn(ps[h][MIX_BANK[i]])[:, m, :], w("m2", i // 4)[g, m * P:(m + 1) * P], th[h][g, i // 4, :], start=True, stop=True)
                    last.then_inc(m2_ps[h], 1)
                elif name == "pk":
                    pe.wait_ge(xm_ok[h], n * 5 + 1)
                    pe.wait_ge(m2_mx[h], n * 5 + 2)
                    dense_T(kn(ps[h][1]), lambda k: w("wk", k), lambda k: xm[h][0][:, k, :]).then_inc(pk_ps[h], 1)
                elif name == "pw1":
                    pe.wait_ge(xm_ok[h], n * 5 + 2)
                    pe.wait_ge(m2_mx[h], n * 5 + 3)
                    for k in range(2):
                        last = mm(kn(ps[h][3])[0:64, 0, :], w("td1", k), xm[h][1][:, k, :], start=(k == 0), stop=(k == 1))
                    last.then_inc(pk_ps[h], 1)
                elif name == "pv":
                    pe.wait_ge(xm_ok[h], n * 5 + 3)
                    pe.wait_ge(m2_mx[h], n * 5 + 4)
                    dense_T(kn(ps[h][2]), lambda k: w("wv", k), lambda k: xm[h][2][:, k, :]).then_inc(pk_ps[h], 1)
                elif name == "pw2":
                    pe.wait_ge(pk_sb[h], n * 6 + 2)
                    for m in range(2):
                        last = mm(kn(ps[h][3])[:, m, :], w("td2")[0:64, m * P:(m + 1) * P], th[h][0:64, 0, :], start=True, stop=True)
                    last.then_inc(pk_ps[h], 1)
                elif name == "pr":
                    pe.wait_ge(xm_ok[h], n * 5 + 4)
                    pe.wait_ge(m2_mx[h], n * 5 + 5)
                    dense_T(kn(ps[h][0]), lambda k: w("wr", k), lambda k: xm[h][3][:, k, :]).then_inc(pk_ps[h], 1)
                elif name == "pg":
                    pe.wait_ge(xm_ok[h], n * 5 + 5)
                    pe.wait_ge(pk_sb[h], n * 6 + 1)
                    dense_T(kn(ps[h][1]), lambda k: w("wg", k), lambda k: xm[h][4][:, k, :]).then_inc(pk_ps[h], 1)
                elif name == "ruk":
                    pe.wait_ge(ruk_ok[h], n + 1)
                    for m in range(2):
                        last = mm(kn(ps[h][2])[:, m, :], w("blk"), ruk[h][:, m, :], start=True, stop=True)
                    last.then_inc(cb_ps[h], 1)
                elif name == "scan":
                    if i >= 1:
                        gather(n, h, i - 1)
                elif name == "gturn":
                    pe.wait_ge(xh_ok[h], n * 4 + 3)
                    turn_rows(h, 0, n3[h])
                elif name == "outg":
                    pe.wait_ge(og_ok[h], n + 1)
                    dense_N(kn(ps[h][1]), lambda k, t: tA[h][:, k, tok(t)], lambda k: w("wo", k)).then_inc(pr_ps[h], 1)
                elif name == "cturn":
                    pe.wait_ge(xh_ok[h], n * 4 + 4)
                    turn_rows(h, 2, n3[h])
                elif name == "fk":
                    pe.wait_ge(ff_d[h], n * 2 + 1)
                    dense_T(kn(ps[h][0]), lambda k: w("fk", k), lambda k: tA[h][:, k, :]).then_inc(ff_ps[h], 1)
                elif name == "l2k":
                    dense_T(kn(ps[h][2]), lambda k: m_qk[:, k, :], lambda k: hT[h][:, k, :, 0:S]).then_inc(l2_ps[h], 1)
                elif name == "fr":
                    pe.wait_ge(ff_d[h], n * 2 + 2)
                    dense_N(kn(ps[h][3]), lambda k, t: th[h][:, k, tok(t)], lambda k: w("fr", k)).then_inc(ff_ps[h], 1)
                elif name == "l2v":
                    pe.wait_ge(ff_a[h], n * 2 + 1)
                    for b in range(NB):
                        g = slice(64 * (b % 2), 64 * (b % 2) + 64)
                        for k in range(2):
                            last = mm(kn(ps[h][0])[g, b // 2, :], hT[h][:, k, b, 0:S], m_vo[:, k, :], start=(k == 0), stop=(k == 1))
                    last.then_inc(l2_ps[h], 1)
                elif name == "fv":
                    pe.wait_ge(kk_ok[h], n + 1)
                    dense_N(kn(ps[h][1]), lambda k, t: kS[h][:, k, tok(t)], lambda k: w("fv", k)).then_inc(pr_ps[h], 1)
                elif name == "x2turn":
                    pe.wait_ge(x2_ok[h], n + 1)
                    pe.wait_ge(tg_ok[h], n * 2 + 2)
                    turn_rows(h, 3, n2[h])
                elif name == "l2s":
                    pe.wait_ge(xt_sb[h], n * 6 + 5)
                    pe.wait_ge(l2_sb[h], n * 3 + 1)
                    for b in range(NB):
                        g = slice(64 * (b % 2), 64 * (b % 2) + 64)
                        for k in range(2):
                            last = mm(ps[h][1][g, (b // 2) * S:(b // 2) * S + S], tA[h][:, k, b * S:(b + 1) * S], tS[h][:, k, b * S:(b + 1) * S],
                                      start=(k == 0), stop=(k == 1))
                    last.then_inc(l2_ps[h], 1)
                elif name == "l2p":
                    pe.wait_ge(ff_a[h], n * 2 + 2)
                    pe.wait_ge(l2_sb[h], n * 3 + 2)
                    for t in range(TT):
                        last = nc.tensor.transpose(ps[h][0][:, t * P:(t + 1) * P], pbd[h][:, t, :], ident)
                    last.then_inc(l2_ps[h], 1)
                elif name == "l2o":
                    pe.wait_ge(l2_sb[h], n * 3 + 3)
                    for t in range(TT):
                        last = mm(kn(ps[h][2])[:, t, :], ptb[h][:, t, :], uS[h][:, t, :], start=True, stop=True)
                    last.then_inc(pr_ps[h], 1)
                elif name == "k3":
                    for k in range(2):
                        last = mm(ps[h][1][:, 0:NT], w("k3", k), hT[h][:, k, :, 0:S], start=(k == 0), stop=(k == 1))
                    last.then_inc(kv3_ps[h], 1)
                elif name == "v3":
                    for b in range(NB):
                        for e in range(2):
                            for k in range(2):
                                last = mm(ps[h][0][64 * e:64 * e + 64, b * 64:(b + 1) * 64], hT[h][:, k, b, 0:S], w("v3", k),
                                          start=(k == 0), stop=(k == 1))
                    last.then_inc(kv3_ps[h], 1)
                elif name == "x3turn":
                    pe.wait_ge(pr_sb[h], n * 6 + 5)
                    turn_rows(h, 3, n1[h])
                elif name == "q3":
                    pe.wait_ge(xt_sb[h], n * 6 + 6)
                    dense_T(kn(ps[h][2]), lambda k: w("q3", k), lambda k: tA[h][:, k, :]).then_inc(l2_ps[h], 1)
                elif name == "out3":
                    pe.wait_ge(o_sb[h], n * 16 + 2 * NCH)
                    dense_N(kn(ps[h][1]), lambda k, t: tA[h][:, k, tok(t)], lambda k: w("o3", k)).then_inc(pr_ps[h], 1)

            nat = att[1][:, 0:nn].rearrange("p (m k n) -> p m k n", m=4, k=2)
            pe.wait_ge(ld_nat, 16)
            for m in range(2):
                for k in range(2):
                    mm(kn(ps[1][0])[:, m, :], nat[:, 1, k, m * P:(m + 1) * P], nat[:, 0, k, :], start=(k == 0), stop=(k == 1))
                for k in range(2):
                    last = mm(kn(ps[1][1])[:, m, :], nat[:, 2, k, m * P:(m + 1) * P], nat[:, 3, k, :], start=(k == 0), stop=(k == 1))
            last.then_inc(set_pe, 1)
            pe.wait_ge(ld_w, 16)
            pe.wait_ge(set_m, 1)
            pe.wait_ge(set_pool, 2)
            pe.wait_ge(set_dve, 1)
            run(pe, stage)

        @block.scalar
        def _(act):
            A = nc.scalar.activation

            def attend(n, h, layer, c):
                at = n * 16 + layer * NCH
                if c < NCH:
                    act.wait_ge(s_sub[h], at + c + 1)
                    A(sc[h][c % 2], sc[h][c % 2], ACT.Exp).then_inc(s_exp[h], 1)
                if 1 <= c <= NCH:
                    act.wait_ge(t_ps[h], at + c)
                    if c >= 2:
                        act.wait_ge(o_ps[h], at + c - 1)
                    A(pt[h], ps[h][2][:, :], ACT.Copy).then_inc(t_sb[h], 1)

            def seqs(v):
                return v.rearrange("p (b s) -> p b s", b=NB)

            def affine(h, bank, name_w, name_b, dst):
                for k in range(2):
                    last = A(dst(k), seqs(kn(ps[h][bank])[:, k, :]), ACT.Identity, bias=vec(name_b, k), scale=vec(name_w, k))
                last.then_inc(xt_sb[h], 1)

            def stage(name, i, h, n):
                if name == "q0":
                    act.wait_ge(qkv_ps[h], n * 4 + 1)
                    for k in range(2):
                        for v in range(2):
                            last = A(qz[h][:, k, :, v, :], seqs(kn(ps[h][0])[:, k, :]), ACT.Identity, bias=qb0m[:, k, v:v + 1], scale=vec("par", v))
                    last.then_inc(qv_sb[h], 1)
                elif name == "v0":
                    for j in range(2):
                        act.wait_ge(qkv_ps[h], n * 4 + 3 + j)
                        for b in range(2):
                            last = A(v0[h][:, 2 * j + b, :, 0:32], kn(ps[h][0 if j else 3])[:, b, :].rearrange("p (g c) -> p g c", c=32), ACT.Copy)
                        last.then_inc(qv_sb[h], 1)
                elif name in ("att0", "att1"):
                    attend(n, h, int(name[-1]), i)
                elif name == "merge0":
                    act.wait_ge(mg_ps[h], n + 1)
                    for k in range(2):
                        last = A(tA[h][:, k, :], kn(ps[h][0])[:, k, :], ACT.Identity, bias=vec("vb0", k))
                    last.then_inc(mg_sb[h], 1)
                elif name == "out0":
                    act.wait_ge(pr_sb[h], n * 6 + 1)
                    for t in range(TT):
                        last = A(n3[h][:, t, :], n1[h][:, t, :], ACT.Square, scale=1.0 / C ** 0.5, accum_out=ssq[h][:, t:t + 1])
                    last.then_inc(sq_ok[h], 1)
                elif name == "zturn":
                    act.wait_ge(xt_ps[h], n * 6 + 1)
                    for k in range(2):
                        last = A(tA[h][:, k, :], kn(ps[h][2])[:, k, :], ACT.Identity, scale=vec("pn", k))
                    last.then_inc(xt_sb[h], 1)
                elif name == "up":
                    act.wait_ge(h_ps[h], n * 4 + i + 1)
                    for m in range(2):
                        last = A(hid[h][:, 2 * i + m, :], kn(ps[h][(0, 1, 3, 2)[i]])[:, m, :], ACT.Gelu_apprx_tanh, bias=vec("b1", 2 * i + m))
                    last.then_inc(h_sb[h], 1)
                elif name == "xturn":
                    act.wait_ge(xt_ps[h], n * 6 + 2)
                    A(xaT[h][:, :, :, 0:1], hT[h][:, :, :, 1:2], ACT.Copy)
                    affine(h, 1, "ln1w", "ln1b", lambda k: xaT[h][:, k, :, 1:S + 1])
                elif name == "mix1":
                    act.wait_ge(m1_ps[h], n + 1)
                    A(th[h][:, 0, :], kn(ps[h][2])[:, 0, :], ACT.Tanh)
                    A(th[h][0:32, 1, :], kn(ps[h][2])[0:32, 1, :], ACT.Tanh).then_inc(m1_sb[h], 1)
                elif name == "pk":
                    act.wait_ge(pk_ps[h], n * 6 + 1)
                    A(flat(kS[h]), ps[h][1][:, :], ACT.Copy).then_inc(pk_sb[h], 1)
                elif name == "pw1":
                    act.wait_ge(pk_ps[h], n * 6 + 2)
                    A(th[h][0:64, 0, :], kn(ps[h][3])[0:64, 0, :], ACT.Tanh).then_inc(pk_sb[h], 1)
                elif name == "pv":
                    act.wait_ge(pk_ps[h], n * 6 + 3)
                    A(flat(vS[h]), ps[h][2][:, :], ACT.Copy).then_inc(pk_sb[h], 1)
                elif name == "pw2":
                    act.wait_ge(pk_ps[h], n * 6 + 4)
                    act.wait_ge(m2_mx[h], n * 5 + 5)
                    for k in range(2):
                        last = A(sx[h][:, k, :, :], seqs(kn(ps[h][3])[:, k, :]), ACT.Exp, bias=vec("td", k))
                    last.then_inc(e1_ok[h], 1)
                    act.wait_ge(e1_ok[h], n + 1)
                    for k in range(2):
                        last = A(wS[h][:, k, :, 1:S + 1], sx[h][:, k, :, :], ACT.Exp, scale=-1.0)
                    last.then_inc(pk_sb[h], 1)
                elif name == "pr":
                    act.wait_ge(pk_ps[h], n * 6 + 5)
                    A(flat(rS[h]), ps[h][0][:, :], ACT.Copy).then_inc(pk_sb[h], 1)
                elif name == "pg":
                    act.wait_ge(pk_ps[h], n * 6 + 6)
                    A(flat(gs[h]), ps[h][1][:, :], ACT.Tanh, scale=0.5).then_inc(tg_ok[h], 1)
                elif name == "scan" and i < 8:
                    m, jp = i // 4, i % 4
                    if i == 0:
                        act.wait_ge(ld_s[h], n * 16 + 16)
                    if i >= 2:
                        act.wait_ge(sc_ok[h], n * 8 + i - 1)
                    A(aB[h][i % 2][:, :, :, 0], s0[h][:, m, :, 2 * jp:2 * jp + 2].rearrange("p b j -> p j b"), ACT.Copy).then_inc(a0_ok[h], 1)
                elif name == "gturn":
                    act.wait_ge(xt_ps[h], n * 6 + 3)
                    affine(h, 0, "gnw", "gnb", lambda k: seqs(tA[h][:, k, :]))
                elif name == "cturn":
                    act.wait_ge(xt_ps[h], n * 6 + 4)
                    A(xaT[h][:, :, :, 0:1], hT[h][:, :, :, 0:1], ACT.Copy)
                    affine(h, 2, "ln2w", "ln2b", lambda k: xaT[h][:, k, :, 1:S + 1])
                elif name == "fk":
                    act.wait_ge(ff_ps[h], n * 2 + 1)
                    A(flat(rS[h]), ps[h][0][:, :], ACT.Relu).then_inc(ff_a[h], 1)
                elif name == "fr":
                    act.wait_ge(ff_ps[h], n * 2 + 2)
                    A(flat(gs[h]), ps[h][3][:, :], ACT.Tanh, scale=0.5).then_inc(tg_ok[h], 1)
                elif name == "l2k":
                    act.wait_ge(l2_ps[h], n * 5 + 1)
                    A(flat(tS[h]), ps[h][2][:, :], ACT.Copy).then_inc(l2_sb[h], 1)
                elif name == "l2v":
                    act.wait_ge(l2_ps[h], n * 5 + 2)
                    A(flat(uS[h]), ps[h][0][:, :], ACT.Copy).then_inc(l2_sb[h], 1)
                elif name == "x2turn":
                    act.wait_ge(xt_ps[h], n * 6 + 5)
                    A(flat(tA[h]), ps[h][3][:, :], ACT.Copy).then_inc(xt_sb[h], 1)
                elif name == "l2s":
                    act.wait_ge(l2_mx[h], n * 3 + 2)
                    for t in range(TT):
                        for e in range(2):
                            g = slice(64 * e, 64 * e + 64)
                            last = A(pbd[h][g, t, 64 * e:64 * e + 64], ps[h][1][g, t * S:(t + 1) * S], ACT.Exp,
                                     bias=vtmp[h][g, t:t + 1], scale=1.0 / 16.0, accum_out=ssq[h][g, t:t + 1])
                    last.then_inc(ff_a[h], 1)
                elif name == "l2p":
                    act.wait_ge(l2_ps[h], n * 5 + 4)
                    A(ptb[h].rearrange("p t n -> p (t n)"), ps[h][0][:, 0:2 * P], ACT.Copy).then_inc(l2_sb[h], 1)
                elif name == "k3":
                    act.wait_ge(kv3_ps[h], n * 2 + 1)
                    for v in range(4):
                        last = A(kz3[h][:, :, v, :], seqs(ps[h][1][:, 0:NT]), ACT.Identity, bias=kb3m[:, v:v + 1], scale=vec("sub", v))
                    last.then_inc(kv3_a[h], 1)
                elif name == "x3turn":
                    act.wait_ge(xt_ps[h], n * 6 + 6)
                    A(flat(tA[h]), ps[h][3][:, :], ACT.Copy).then_inc(xt_sb[h], 1)
                elif name == "q3":
                    act.wait_ge(l2_ps[h], n * 5 + 5)
                    for k in range(2):
                        last = A(q3T[h][:, k, :], kn(ps[h][2])[:, k, :], ACT.Identity, bias=qb3s[:, k:k + 1], scale=W3 ** -0.5)
                    last.then_inc(kv3_a[h], 1)

            act.wait_ge(ld_w, 16)
            act.wait_ge(set_dve, 1)
            act.wait_ge(set_pool, 2)
            run(act, stage)

        @block.gpsimd
        def _(pool):
            G = nc.gpsimd

            def inverse_root(n, h, m, src, at):
                G.tensor_tensor(vtmp[h][:, :], src, eps[:, at:at + TT], ALU.add).then_inc(rs_a[h], 1)
                pool.wait_ge(rs_a[h], n * 4 + m + 1)
                G.tensor_tensor(rstd[h][:, :], vtmp[h][:, :], power[:, 0:TT], ALU.pow).then_inc(rs_b[h], 1)

            def shift(n, h, m):
                pool.wait_ge(xt_sb[h], n * 6 + 2 * (m + 1))
                G.tensor_tensor(sx[h][:, :, :, :].rearrange("p k b s -> p (k b) s"),
                                xaT[h][:, :, :, 0:S].rearrange("p k b s -> p (k b) s"),
                                xaT[h][:, :, :, 1:S + 1].rearrange("p k b s -> p (k b) s"), ALU.subtract).then_inc(sx_ok[h], 1)

            def stage(name, i, h, n):
                if name in ("att0", "att1"):
                    if i < NCH:
                        layer = int(name[-1])
                        groups = 4 if layer == 0 else 8
                        pool.wait_ge(s_mx[h], n * 16 + layer * NCH + i + 1)
                        v = sc[h][i % 2].rearrange("p (g k) -> p g k", g=groups)
                        m = mx[h][:, i % 2, 0:groups].unsqueeze(2).broadcast_to([P, groups, 512 // groups])
                        G.tensor_tensor(v, v, m, ALU.subtract).then_inc(s_sub[h], 1)
                elif name == "merge0":
                    pool.wait_ge(ld_rows, 16)
                    pool.wait_ge(ld_x[h], n * 16 + 16)
                    G.tensor_tensor(n1[h][:, :, :], xN[h][:, :, :], row("out_b", TT), ALU.add).then_inc(res[h], 1)
                elif name == "out0":
                    pool.wait_ge(sq_ok[h], n + 1)
                    inverse_root(n, h, 0, ssq[h][:, :], 0)
                elif name == "zturn":
                    G.tensor_tensor(n4[h][:, :, :], xN[h][:, :, :], row("mlp_b2", TT), ALU.add).then_inc(res[h], 1)
                elif name == "down" and i == 1:
                    pool.wait_ge(bn_b[h], n * 3 + 1)
                    inverse_root(n, h, 1, mv[h][:, :, 1], 2)
                elif name == "xturn":
                    shift(n, h, 0)
                elif name == "mix2":
                    pool.wait_ge(m2_mx[h], n * 5 + i + 1)
                    v = flat(xm[h][i]).rearrange("p (k s) -> p k s", s=S)
                    G.tensor_tensor(v, v, xaT[h][:, :, :, 1:S + 1].rearrange("p k b s -> p (k b) s"), ALU.add).then_inc(xm_ok[h], 1)
                elif name == "scan" and i < 8:
                    m = i // 4
                    pool.wait_ge(sc_ok[h], n * 8 + i + 1)
                    if i == 0:
                        pool.wait_ge(pk_sb[h], n * 6 + 5)
                    if i >= 2:
                        pool.wait_ge(rd_ps[h], n * 8 + i - 1)
                    r = rS[h][:, m, :].rearrange("p (b s) -> p b s", b=NB).unsqueeze(1).broadcast_to([P, 2, NB, S])
                    G.tensor_tensor(pd[h][i % 2].rearrange("p j (b s) -> p j b s", b=NB), st[h][i % 2][:, :, :, 0:S], r, ALU.mult).then_inc(pd_ok[h], 1)
                elif name == "gturn":
                    pool.wait_ge(gn_d[h], n * GN + 3)
                    G.tensor_tensor(n3[h][:, :, :], n2[h][:, :, :], n2[h][:, :, :], ALU.mult).then_inc(gn_p[h], 1)
                    pool.wait_ge(xt_sb[h], n * 6 + 3)
                    pool.wait_ge(pk_sb[h], n * 6 + 6)
                    G.tensor_tensor(tA[h][:, :, :], tA[h][:, :, :], gs[h][:, :, :], ALU.mult).then_inc(og_ok[h], 1)
                elif name == "outg":
                    pool.wait_ge(bn_b[h], n * 3 + 2)
                    inverse_root(n, h, 2, mv[h][:, :, 1], 2)
                elif name == "cturn":
                    shift(n, h, 1)
                elif name == "fk":
                    pool.wait_ge(ff_a[h], n * 2 + 1)
                    G.tensor_tensor(kS[h][:, :, :], rS[h][:, :, :], rS[h][:, :, :], ALU.mult).then_inc(kk_ok[h], 1)
                elif name == "fv":
                    pool.wait_ge(pr_sb[h], n * 6 + 4)
                    G.tensor_tensor(n2[h][:, :, :], n3[h][:, :, :], n4[h][:, :, :], ALU.add).then_inc(x2_ok[h], 1)
                elif name == "l2o":
                    pool.wait_ge(pr_sb[h], n * 6 + 5)
                    G.tensor_tensor(n2[h][:, :, :], n1[h][:, :, :], row("bo", TT), ALU.add).then_inc(res[h], 1)
                elif name == "out3":
                    pool.wait_ge(bn_b[h], n * 3 + 3)
                    inverse_root(n, h, 3, mv[h][:, :, 1], 0)
                    pool.wait_ge(fin_ok[h], n * 4 + 1)
                    pool.wait_ge(st_out[h], n * 16 + 16)
                    G.tensor_tensor(n4[h][:, :, :], n3[h][:, :, :], row("gamma", TT), ALU.mult).then_inc(fin_ok[h], 1)
                    pool.wait_ge(fin_ok[h], n * 4 + 2)
                    G.tensor_tensor(n5[h][:, :, :], n4[h][:, :, :], row("beta", TT), ALU.add).then_inc(fin_ok[h], 2)

            for h in halves:
                G.memset(wS[h][:, :, :, :], 0.0)
                G.memset(v3[h][:, :, :, :, :], 0.0)
                G.memset(v0[h][:, :, :, 32:33], 1.0)
                G.memset(m0[h][:, :, S:2 * S], 0.0)
            G.memset(eps[:, 0:2], 1e-6)
            G.memset(eps[:, 2:4], 1e-5)
            for h in halves:
                G.memset(n5[h][:, 0, 0:1], 0.0).then_inc(st_out[h], 16)
            G.memset(power[:, :], -0.5).then_inc(set_pool, 2)
            run(pool, stage)

        @block.vector
        def _(dve):
            V = nc.vector

            def attend(n, h, layer, c):
                groups = 4 if layer == 0 else 8
                at = n * 16 + layer * NCH
                if c < NCH:
                    pair = c // 4
                    dve.wait_ge(s_ps[h], at + c + 1)
                    if c >= 2:
                        dve.wait_ge(t_ps[h], at + c - 1)
                    if layer == 0:
                        m = m0[h][:, 2 * pair:2 * pair + 2, :].unsqueeze(2).broadcast_to([P, 2, 2, 2 * S])
                    else:
                        m = m3[h][:, 2 * pair:2 * pair + 2, :].unsqueeze(2).broadcast_to([P, 2, 4, S])
                    k = groups // 2
                    V.tensor_tensor(sc[h][c % 2].rearrange("p (b k s) -> p b k s", b=2, k=k),
                                    ps[h][c % 2][:, :].rearrange("p (b k s) -> p b k s", b=2, k=k), m, ALU.add).then_inc(s_sb[h], 1)
                    dve.wait_ge(s_sb[h], at + c + 1)
                    V.tensor_reduce(mx[h][:, c % 2, 0:groups], sc[h][c % 2].rearrange("p (g k) -> p g k", g=groups), AXX, ALU.max).then_inc(s_mx[h], 1)
                if c >= 2:
                    pair, r = (c - 2) // 4, (c - 2) % 4
                    dst = ao[h][:, 2 * pair:2 * pair + 2, :, :].rearrange("p b k (e r c) -> p (b k) e r c", e=2, r=4)[:, :, :, r, :]
                    if layer == 0:
                        dve.wait_ge(o_ps[h], at + c - 1)
                        o = ps[h][3][:, 0:132].rearrange("p (g c) -> p g c", c=33)
                        V.reciprocal(rc[h][:, 0:4].unsqueeze(2), o[:, :, 32:33]).then_inc(o_rc[h], 1)
                        dve.wait_ge(o_rc[h], n * 8 + c - 1)
                        V.tensor_tensor(dst, o[:, :, 0:32].rearrange("p g (e c) -> p g e c", e=2),
                                        rc[h][:, 0:4].unsqueeze(2).unsqueeze(3).broadcast_to([P, 4, 2, 16]), ALU.mult).then_inc(o_sb[h], 1)
                    elif r == 3:
                        dve.wait_ge(o_ps[h], at + c - 1)
                        V.reciprocal(rc[h][:, :], ps[h][3][:, 2 * P:4 * P]).then_inc(rc_ok[h], 1)
                        dve.wait_ge(rc_ok[h], n * 2 + pair + 1)
                        V.tensor_tensor(tA[h][:, :, pair * P:(pair + 1) * P].rearrange("p k (b s) -> p b k s", b=2),
                                        ps[h][3][:, 0:2 * P].rearrange("p (b k s) -> p b k s", b=2, k=2),
                                        rc[h][:, :].rearrange("p (b k s) -> p b k s", b=2, k=2), ALU.mult).then_inc(o_sb[h], 4)

            def layer_stats(n, h, m, src):
                for t in range(TT):
                    last = V.bn_stats(bns[h][:, t, :], src[:, t, :])
                last.then_inc(bn_a[h], 1)
                stats = n * 3 + m + 1
                dve.wait_ge(set_pool, 2)
                dve.wait_ge(bn_a[h], stats)
                for t in range(TT):
                    last = V.bn_aggr(mv[h][:, t, :], bns[h][:, t, :])
                last.then_inc(bn_b[h], 1)

            def layer_norm(n, h, m, dst, src):
                dve.wait_ge(rs_b[h], n * 4 + m + 1)
                for t in range(TT):
                    last = V.tensor_scalar(dst[:, t, :], src[:, t, :], mv[h][:, t, 0:1], rstd[h][:, t:t + 1], ALU.subtract, ALU.mult)
                return last

            def chain(n, h, k, ins):
                ins.then_inc(gn_d[h], 1)
                dve.wait_ge(gn_d[h], n * GN + k)

            def inverse_root(n, h, k, y, v, t):
                chain(n, h, k, V.tensor_scalar(t.bitcast(I32), v.bitcast(I32), 1, None, ALU.logical_shift_right))
                chain(n, h, k + 1, V.tensor_scalar(y.bitcast(I32), t.bitcast(I32), -1.0, float(0x5F3759DF), ALU.mult, ALU.add))
                for s in range(NEWTON):
                    chain(n, h, k + 2 + 3 * s, V.tensor_tensor(t, y, y, ALU.mult))
                    chain(n, h, k + 3 + 3 * s, V.scalar_tensor_tensor(t, t, -0.5, v, ALU.mult, ALU.mult))
                    chain(n, h, k + 4 + 3 * s, V.scalar_tensor_tensor(y, t, 1.5, y, ALU.add, ALU.mult))

            def stage(name, i, h, n):
                if name == "k0":
                    dve.wait_ge(qkv_ps[h], n * 4 + 2)
                    for m in range(2):
                        last = V.tensor_scalar(kT[h][:, m, :, :].rearrange("p b s -> p (b s)"), ps[h][1 + m][:, :], vec("kb0", m), None, ALU.add)
                    last.then_inc(k0_sb[h], 1)
                    dve.wait_ge(ld_m[h], n * 16 + 16)
                    V.tensor_scalar(m0[h][:, :, 0:S], mint[h][:, :, :], 0.0, MASKED, ALU.is_equal, ALU.mult).then_inc(k0_sb[h], 1)
                elif name == "v0":
                    dve.wait_ge(k0_sb[h], n * 2 + 2)
                elif name in ("att0", "att1"):
                    if name == "att1" and i == 0:
                        dve.wait_ge(ld_3[h], n * 32 + 32)
                    attend(n, h, int(name[-1]), i)
                elif name == "out0":
                    dve.wait_ge(pr_ps[h], n * 6 + 1)
                    dve.wait_ge(res[h], n * 3 + 1)
                    V.tensor_tensor(n1[h][:, :, :], kn(ps[h][1]), n1[h][:, :, :], ALU.add).then_inc(pr_sb[h], 1)
                    dve.wait_ge(rs_b[h], n * 4 + 1)
                    for t in range(TT):
                        last = V.tensor_scalar(n2[h][:, t, :], n1[h][:, t, :], rstd[h][:, t:t + 1], None, ALU.mult)
                    last.then_inc(xh_ok[h], 1)
                elif name == "down" and i == 1:
                    dve.wait_ge(pr_ps[h], n * 6 + 2)
                    dve.wait_ge(res[h], n * 3 + 2)
                    V.tensor_tensor(n4[h][:, :, :], kn(ps[h][0]), n4[h][:, :, :], ALU.add).then_inc(pr_sb[h], 1)
                    dve.wait_ge(pr_sb[h], n * 6 + 2)
                    layer_stats(n, h, 0, n4[h])
                    layer_norm(n, h, 1, n3[h], n4[h]).then_inc(xh_ok[h], 1)
                elif name == "xturn":
                    dve.wait_ge(sx_ok[h], n * 2 + 1)
                    for k in range(2):
                        last = V.scalar_tensor_tensor(tA[h][:, k, :].rearrange("p (b s) -> p b s", b=NB), sx[h][:, k, :, :], vec("maax", k),
                                                      xaT[h][:, k, :, 1:S + 1], ALU.mult, ALU.add)
                    last.then_inc(xin_ok[h], 1)
                elif name == "mix2":
                    dve.wait_ge(m2_ps[h], n * 5 + i + 1)
                    for k in range(2):
                        last = V.scalar_tensor_tensor(xm[h][i][:, k, :], kn(ps[h][(0, 1, 3, 2, 0)[i]])[:, k, :], vec("stack", 2 * i + k),
                                                      sx[h][:, k, :, :].rearrange("p b s -> p (b s)"), ALU.add, ALU.mult)
                    last.then_inc(m2_mx[h], 1)
                elif name == "pr":
                    dve.wait_ge(pk_sb[h], n * 6 + 5)
                    for k in range(2):
                        last = V.scalar_tensor_tensor(ruk[h][:, k, :], rS[h][:, k, :], vec("u", k), kS[h][:, k, :], ALU.mult, ALU.mult)
                    last.then_inc(ruk_ok[h], 1)
                elif name == "pg":
                    dve.wait_ge(tg_ok[h], n * 2 + 1)
                    V.scalar_tensor_tensor(flat(gs[h][:, :, :]), flat(gs[h][:, :, :]), 1.0, ps[h][1][:, :], ALU.add, ALU.mult).then_inc(pk_sb[h], 1)
                elif name == "ruk":
                    dve.wait_ge(cb_ps[h], n + 1)
                    V.tensor_tensor(cv[h], kn(ps[h][2]), vS[h][:, :, :], ALU.mult).then_inc(cv_ok[h], 1)
                elif name == "scan" and i < 8:
                    dve.wait_ge(vx_ok[h][i % 3], (n * (3, 3, 2)[i % 3] + i // 3 + 1) * 32)
                    if i >= 2:
                        dve.wait_ge(pd_ok[h], n * 8 + i - 1)
                    k = kS[h][:, i // 4, :].rearrange("p (b s) -> p b s", b=NB).unsqueeze(1).broadcast_to([P, 2, NB, S])
                    V.tensor_tensor(aB[h][i % 2][:, :, :, 1:S + 1], vx[h][i % 3].rearrange("p j (b s) -> p j b s", b=NB), k, ALU.mult).then_inc(a_ok[h], 1)
                    dve.wait_ge(a_ok[h], n * 8 + i + 1)
                    dve.wait_ge(a0_ok[h], n * 8 + i + 1)
                    for j in range(2):
                        last = V.tensor_tensor_scan(st[h][i % 2][:, j, :, :].rearrange("p b s -> p (b s)"),
                                                    wS[h][:, i // 4, :, :].rearrange("p b s -> p (b s)"),
                                                    aB[h][i % 2][:, j, :, :].rearrange("p b s -> p (b s)"), 0.0, ALU.mult, ALU.add)
                    last.then_inc(sc_ok[h], 1)
                elif name == "gturn":
                    o = ps[h][3][:, :].rearrange("p (g j h) -> p g h j", g=4, j=J)
                    dve.wait_ge(rd_ps[h], n * 8 + 8)
                    chain(n, h, 1, V.tensor_reduce(g3[h][:, :].rearrange("p (g h) -> p g h", g=4), o, AXX, ALU.add))
                    chain(n, h, 2, V.tensor_scalar(g2[h][:, :], g3[h][:, :], -1.0 / J, None, ALU.mult))
                    V.tensor_tensor(n2[h][:, :, :].rearrange("p t (m h j) -> p (t m) h j", m=2, j=J), o,
                                    g2[h][:, :].rearrange("p (g h) -> p g h", g=4).unsqueeze(3).broadcast_to([P, 4, HT, J]), ALU.add).then_inc(gn_d[h], 1)
                    dve.wait_ge(gn_p[h], n + 1)
                    chain(n, h, 4, V.tensor_reduce(g3[h][:, :], n3[h][:, :, :].rearrange("p t (h j) -> p (t h) j", j=J), AXX, ALU.add))
                    chain(n, h, 5, V.tensor_scalar(g2[h][:, :], g3[h][:, :], 1.0 / J, 1e-5, ALU.mult, ALU.add))
                    inverse_root(n, h, 6, g1[h][:, :], g2[h][:, :], g3[h][:, :])
                    V.tensor_tensor(n3[h][:, :, :].rearrange("p t (h j) -> p (t h) j", j=J), n2[h][:, :, :].rearrange("p t (h j) -> p (t h) j", j=J),
                                    g1[h][:, :].unsqueeze(2).broadcast_to([P, 64, J]), ALU.mult).then_inc(xh_ok[h], 1)
                elif name == "outg":
                    dve.wait_ge(pr_ps[h], n * 6 + 3)
                    V.tensor_tensor(n4[h][:, :, :], kn(ps[h][1]), n4[h][:, :, :], ALU.add).then_inc(pr_sb[h], 1)
                    dve.wait_ge(pr_sb[h], n * 6 + 3)
                    layer_stats(n, h, 1, n4[h])
                    layer_norm(n, h, 2, n3[h], n4[h]).then_inc(xh_ok[h], 1)
                elif name == "cturn":
                    dve.wait_ge(sx_ok[h], n * 2 + 2)
                    for name_, dst in (("fmk", tA), ("fmr", th)):
                        for k in range(2):
                            last = V.scalar_tensor_tensor(dst[h][:, k, :].rearrange("p (b s) -> p b s", b=NB), sx[h][:, k, :, :], vec(name_, k),
                                                          xaT[h][:, k, :, 1:S + 1], ALU.mult, ALU.add)
                        last.then_inc(ff_d[h], 1)
                    V.memset(pbd[h], 0.0)
                elif name == "fv":
                    dve.wait_ge(pr_ps[h], n * 6 + 4)
                    dve.wait_ge(tg_ok[h], n * 2 + 2)
                    V.scalar_tensor_tensor(flat(n3[h][:, :, :]), flat(gs[h][:, :, :]), 1.0, ps[h][1][:, :], ALU.add, ALU.mult).then_inc(pr_sb[h], 1)
                elif name == "l2s":
                    dve.wait_ge(l2_ps[h], n * 5 + 3)
                    V.tensor_reduce(rstd[h][:, :], ps[h][1][:, 0:2 * S].rearrange("p (t s) -> p t s", t=2), AXX, ALU.max).then_inc(l2_mx[h], 1)
                    dve.wait_ge(l2_mx[h], n * 3 + 1)
                    V.tensor_scalar(vtmp[h][:, :], rstd[h][:, :], -1.0 / 16.0, None, ALU.mult).then_inc(l2_mx[h], 1)
                elif name == "l2p":
                    dve.wait_ge(ff_a[h], n * 2 + 2)
                    V.reciprocal(rstd[h][:, :], ssq[h][:, :]).then_inc(l2_mx[h], 1)
                elif name == "l2o":
                    dve.wait_ge(pr_ps[h], n * 6 + 5)
                    dve.wait_ge(x2_ok[h], n + 1)
                    dve.wait_ge(l2_mx[h], n * 3 + 3)
                    for t in range(TT):
                        last = V.scalar_tensor_tensor(n1[h][:, t, :], kn(ps[h][2])[:, t, :], rstd[h][:, t:t + 1], n2[h][:, t, :], ALU.mult, ALU.add)
                    last.then_inc(pr_sb[h], 1)
                elif name == "v3":
                    dve.wait_ge(kv3_ps[h], n * 2 + 2)
                    for e in range(2):
                        g = slice(64 * e, 64 * e + 64)
                        for v in range(2):
                            o = (2 * v + e) * W3
                            last = V.tensor_tensor(v3[h][g, :, :, v, o:o + W3],
                                                   ps[h][0][g, 0:NT].rearrange("p (b r x) -> p b r x", b=NB, r=2)[:, :, :, o:o + W3],
                                                   w("bv3")[g, :].rearrange("p (r x) -> p r x", r=2)[:, :, o:o + W3].unsqueeze(1).broadcast_to([64, NB, 2, W3]), ALU.add)
                    last.then_inc(kv3_d[h], 1)
                elif name == "out3":
                    dve.wait_ge(pr_ps[h], n * 6 + 6)
                    dve.wait_ge(res[h], n * 3 + 3)
                    V.tensor_tensor(n1[h][:, :, :], kn(ps[h][1]), n2[h][:, :, :], ALU.add).then_inc(pr_sb[h], 1)
                    dve.wait_ge(pr_sb[h], n * 6 + 6)
                    layer_stats(n, h, 2, n1[h])
                    layer_norm(n, h, 3, n3[h], n1[h]).then_inc(fin_ok[h], 1)
                    V.tensor_copy(g1[h][:, 0:1], vec("alpha")).then_inc(free_ps[h], 1)

            dve.wait_ge(set_pool, 2)
            dve.wait_ge(ld_w, 16)
            for k in range(2):
                V.tensor_scalar(qb0m[:, k, :], wa[:, vec0 + VEC["par"][0]:vec0 + VEC["par"][0] + 2], vec("qb0", k), None, ALU.mult)
            V.tensor_scalar(qb3s[:, :], wa[:, vec0 + VEC["qb3"][0]:vec0 + VEC["qb3"][0] + 2], W3 ** -0.5, None, ALU.mult)
            V.tensor_scalar(kb3m[:, :], wa[:, vec0 + VEC["sub"][0]:vec0 + VEC["sub"][0] + 4], vec("kb3"), None, ALU.mult)
            for name in ("gnw", "gnb"):
                c = vec0 + VEC[name][0]
                V.tensor_scalar(wa[:, c:c + 2], wa[:, c:c + 2], 0.5, None, ALU.mult)
            V.tensor_scalar(w("fv"), w("fv"), 0.5, None, ALU.mult).then_inc(set_dve, 1)
            for h in halves:
                V.tensor_copy(g1[h][:, 0:1], vec("alpha")).then_inc(free_ps[h], 1)
            dve.wait_ge(set_pe, 1)
            V.tensor_copy(flat(m_qk[:, :, :]), ps[1][0][:, :])
            V.tensor_scalar(flat(m_vo[:, :, :]), ps[1][1][:, :], vec("alpha"), None, ALU.mult).then_inc(set_m, 1)
            run(dve, stage)


def pack(weights, table):
    return np.concatenate([weights[name] for name, _ in table], axis=1)


def kernel(**inputs):
    import concourse.bacc as bacc
    from concourse.bass_utils import run_bass_kernel_spmd

    a = {k: np.asarray(v) for k, v in inputs.items()}
    f = np.float32
    ctx, x = a["ctx_2048"], a["x"]
    L0, L1, L2, L3 = ({k[len(p):]: v for k, v in a.items() if k.startswith(p)}
                      for p in ("L0_xattn_", "L1_xattn_", "L2_xattn_", "L3_xattn_"))

    def fold(m):
        tiles = -(-m.shape[0] // P)
        m = np.concatenate([m, np.zeros((tiles * P - m.shape[0], m.shape[1]), f)])
        return m.reshape(tiles, P, -1).transpose(1, 0, 2).reshape(P, -1)

    def cols(v):
        return v.reshape(-1, P).T

    p = np.arange(P)
    tile = np.arange(2)[:, None]
    o0 = (tile * P + (p % 64 // 16) * 32 + p // 64 * 16 + p % 16).reshape(-1)
    q3 = ((p % 64 // 8 * 4 + tile * 2 + p // 64) * 8 + p % 8).reshape(-1)

    kvw = L0["kv_w"].reshape(C, C, 2)
    kvb = L0["kv_b"].reshape(C, 2)
    head = p // J
    same = (head[:, None] == head[None, :]).astype(f)
    weights = {
        "ident": np.eye(P, dtype=f), "q0": fold(L0["q_w"]), "k0": fold(kvw[:, :, 0]), "v0": fold(kvw[:, :, 1]),
        "o0": fold(L0["out_w"][o0]), "w1": fold(L0["mlp_w1"]), "w2": fold(L0["mlp_w2"]),
        "m1": fold(L1["maa_w1"]), "m2": fold(L1["maa_w2"].reshape(5 * 32, C)),
        "td1": fold(L1["td_w1"]), "td2": fold(L1["td_w2"]),
        "wk": fold(L1["Wk"].T), "wv": fold(L1["Wv"].T), "wr": fold(L1["Wr"].T), "wg": fold(L1["Wg"].T),
        "wo": fold(L1["Wo"].T), "fk": fold(L1["Wfk"].T), "fr": fold(L1["Wfr"].T), "fv": fold(L1["Wfv"].T),
        "q3": fold(L3["Wq"][:, q3]), "k3": fold(np.concatenate([L3["Wk"], L3["Wk"]], axis=1)), "v3": fold(L3["Wv"]),
        "o3": fold(L3["Wo"][q3]),
        "l2q": fold(L2["w_q"]), "l2k": fold(L2["w_k"]), "l2v": fold(L2["w_v"]), "l2o": fold(L2["w_o"].T),
        "ones3": (2 * np.arange(2)[None, :, None] + p[:, None, None] // S == (np.arange(32) // W3)[None, None, :]).astype(f).reshape(P, -1),
        "bv3": np.broadcast_to(L3["bv"], (P, 64)),
        "sumh": (head[:, None] == np.arange(HT)).astype(f), "blk": same,
        "perm": (p[:, None] == (p % HT * J + p // HT)[None, :]).astype(f),
    }
    vectors = {
        "qb0": cols(L0["q_b"]), "kb0": cols(kvb[:, 0]), "vb0": cols(kvb[:, 1][o0]), "pn": cols(L0["postnorm_w"]),
        "b1": cols(L0["mlp_b1"]), "ln1w": cols(L1["ln1_w"]), "ln1b": cols(L1["ln1_b"]), "ln2w": cols(L1["ln2_w"]),
        "ln2b": cols(L1["ln2_b"]), "maax": cols(L1["maa_x"]), "stack": cols(L1["maa_stack"]),
        "td": cols(L1["time_decay"]), "u": cols(L1["u"]), "gnw": cols(L1["gn_w"]), "gnb": cols(L1["gn_b"]),
        "fmk": cols(L1["ffn_maa_k"]), "fmr": cols(L1["ffn_maa_r"]), "qb3": cols(L3["bq"][q3]),
        "kb3": cols(np.concatenate([L3["bk"], L3["bk"]])), 
        "par": (p[:, None] % 32 // 16 == np.arange(2)).astype(f) / W0,
        "sub": (p[:, None] % 32 // 8 == np.arange(4)).astype(f),
        "alpha": np.broadcast_to(L2["alpha"].reshape(1, 1), (P, 1)),
    }
    vec = np.concatenate([vectors[n] for n in VEC], axis=1)
    weights["vec"] = np.concatenate([vec, np.zeros((P, 64 - vec.shape[1]), f)], axis=1)

    h = np.concatenate([ctx, x], axis=1).transpose(2, 0, 1).reshape(KT, P, B, 2 * S).transpose(1, 0, 2, 3)
    arrays = {
        "h": h, "x": x.reshape(-1, P, C).transpose(1, 0, 2), "mask": a["mask_BxS2_ik0"],
        "amask": a["mask_Bx1xSxS2_ff0"].reshape(B, S, S),
        "s0": ctx[:, 2:2 + J].reshape(B, KT, P, J).transpose(2, 1, 0, 3),
        "wa": pack(weights, WEIGHTS_A), "wb": pack(weights, WEIGHTS_B), "nat": pack(weights, NAT),
        "rows": np.stack([L0["out_b"], L0["mlp_b2"], L3["bo"], L3["gamma"], L3["beta"]]),
    }
    arrays = {k: np.ascontiguousarray(v) for k, v in arrays.items()}

    nc = bacc.Bacc("TRN2", target_bir_lowering=False, num_devices=1)
    args = [nc.dram_tensor(f"in_{k}", v.shape, mybir.dt.from_np(v.dtype), kind="ExternalInput").ap() for k, v in arrays.items()]
    out = nc.dram_tensor("result", (P, B * S // P, C), F32, kind="ExternalOutput").ap()
    build(nc, *args, out)
    got = run_bass_kernel_spmd(nc, [{f"in_{k}": v for k, v in arrays.items()}], core_ids=[0]).results[0]["result"]
    return np.asarray(got).transpose(1, 0, 2).reshape(B, S, C)
```

```python
import numpy as np
import concourse.bass as bass
from concourse import mybir
from concourse.alu_op_type import AluOpType as ALU
from contextlib import ExitStack

F32 = mybir.dt.float32
I32 = mybir.dt.int32
ACT = mybir.ActivationFunctionType
AXX = mybir.AxisListType.X

B, S, C = 64, 64, 256
P = 128
KT = C // P
NB = 4
NT = NB * S
TT = NT // P
STEPS = B // (2 * NB)
NCH = 8
J = 8
HT = P // J
HID = 4 * C
W0 = 16
W3 = 8
MASKED = -1.0e30
NEWTON = 3
GN = 3 + 2 + 2 + 3 * NEWTON

WEIGHTS_A = [("ident", P), ("q0", 2 * C), ("k0", 2 * C), ("v0", 2 * C), ("o0", 2 * C), ("vec", 64), ("fv", 2 * C), ("ones0", 48), ("ones3", 64), ("bv3", 64)]
WEIGHTS_B = [("w1", 2 * HID), ("w2", 8 * C),
             ("m1", 2 * 160), ("m2", 2 * C), ("td1", 2 * 64), ("td2", C),
             ("wk", 2 * C), ("wv", 2 * C), ("wr", 2 * C), ("wg", 2 * C), ("wo", 2 * C),
             ("fk", 2 * C), ("fr", 2 * C),
             ("q3", 2 * C), ("k3", 2 * P), ("v3", 2 * 64), ("o3", 2 * C),
             ("sumh", 2 * 2 * HT), ("blk", P), ("perm", P)]
NAT = [("l2q", 2 * C), ("l2k", 2 * C), ("l2v", 2 * C), ("l2o", 2 * C)]
VEC = {}
for _n, _w in [("qb0", 2), ("kb0", 2), ("pn", 2), ("b1", 8), ("ln1w", 2), ("ln1b", 2),
               ("ln2w", 2), ("ln2b", 2), ("maax", 2), ("stack", 10), ("td", 2), ("u", 2),
               ("gnw", 2), ("gnb", 2), ("fmk", 2), ("fmr", 2), ("qb3", 2), ("kb3", 1),
               ("par", 2), ("sub", 4), ("alpha", 1)]:
    VEC[_n] = (sum(w for _, w in VEC.values()), _w)
ROWS = ["kv_b", "out_b", "mlp_b2", "bo", "gamma", "beta"]

def chunks(layer):
    out = []
    for c in range(NCH + 2):
        out += [(f"score{layer}", c)] if c < NCH else []
        out += [(f"turn{layer}", c - 1)] if 1 <= c <= NCH else []
        out += [(f"value{layer}", c - 2)] if c >= 2 else []
    return out


def scans():
    out = []
    for q in range(9):
        out += [("scan", q)] if q < 8 else []
        out += [("sum", q - 1)] if q >= 1 else []
    return out


FIRST = [("q0", 0), ("k0", 0), ("v0", 0)] + chunks(0) + [("out0", 0), ("norm0", 0), ("zturn", 0)] \
    + [("up", i) for i in range(4)] + [("down", 0), ("down", 1), ("norm1", 0), ("xturn", 0)] \
    + [("mix1", 0)] + [("mix2", f) for f in range(5)] \
    + [(n, 0) for n in ("pk", "pw1", "pv", "pw2", "pr", "pg")]
SECOND = [("ruk", 0)] + scans() \
    + [("oturn", 0), ("gnorm", 0), ("gnorm", 1), ("gnorm", 2), ("gnorm", 3), ("gturn", 0), ("outg", 0), ("norm2", 0), ("cturn", 0)] \
    + [(n, 0) for n in ("fk", "l2k", "fr", "l2v", "fv", "x2turn", "l2s", "l2p", "l2o", "k3", "v3")] \
    + [("x3turn", 0), ("q3", 0)] + chunks(1) + [("out3", 0), ("norm3", 0)]


ORDER = ("001101000000100110010110111110100000011011111011110101010010101101010100000110010010001100001001"
         "001000001000011001101110011111101100101001100000110111110001000010010001001101101010010101111100"
         "11011011100111010111011111110111010100")


def body():
    stages = [iter([(0, 0, *s) for s in SECOND] + [(0, 1, *s) for s in FIRST]),
              iter([(1, 0, *s) for s in FIRST + SECOND])]
    return [next(stages[int(half)]) for half in ORDER]


BODY = body()
HEAD = [(half, 0, name, i) for half, ahead, name, i in BODY if ahead == 1]
TAIL = [stage for stage in BODY if stage[1] == 0]


class Step:

    def __init__(self, count, ahead):
        self.count, self.ahead = count, ahead

    def __mul__(self, k):
        return Step(self.count * k, self.ahead * k)

    def __add__(self, c):
        return self.count + (self.ahead + c) if self.ahead + c else self.count


def run(engine, stage):
    for half, ahead, name, i in HEAD:
        stage(name, i, half, ahead)
    with engine.Fori(0, STEPS - 1) as it:
        for half, ahead, name, i in BODY:
            stage(name, i, half, Step(it + half, ahead - half))
    for half, ahead, name, i in TAIL:
        stage(name, i, half, STEPS - 1)


def columns(table):
    at, out = 0, {}
    for name, width in table:
        out[name] = (at, width)
        at += width
    return out, at


def build(nc, h_d, x_d, mask_d, amask_d, s0_d, wa_d, wb_d, nat_d, rows_d, out_d):
    ca, na = columns(WEIGHTS_A)
    cb, nb = columns(WEIGHTS_B)
    cn, nn = columns(NAT)


    with ExitStack() as ctx:
        def sb(name, shape, dt=F32):
            return ctx.enter_context(nc.sbuf_tensor(name, shape, dt))

        def sem(name):
            return ctx.enter_context(nc.semaphore(name))

        def sems(name):
            return [sem(f"{name}_{h}") for h in range(2)]

        def sbs(name, shape, dt=F32):
            return [sb(f"{name}_{h}", shape, dt) for h in range(2)]

        wa = sb("wa", [P, na])
        wb = sb("wb", [P, nb])

        def w(name, k=None):
            t, (at, n) = (wa, ca[name]) if name in ca else (wb, cb[name])
            v = t[:, at:at + n]
            return v if k is None else v.rearrange("p (k n) -> p k n", k=2)[:, k, :]

        ident = w("ident")
        vec0 = ca["vec"][0]

        def vec(name, k=0):
            c = vec0 + VEC[name][0] + k
            return wa[:, c:c + 1]

        w2 = w("w2").rearrange("p (m n) -> p m n", m=8)
        rows = sb("rows", [P, len(ROWS), C])

        def row(name, n):
            return rows[:, ROWS.index(name), :].unsqueeze(1).broadcast_to([P, n, C])

        m_qk = sb("m_qk", [P, 2, C])
        m_vo = sb("m_vo", [P, 2, C])
        qb0m = sb("qb0m", [P, 2, 2])
        qb3s = sb("qb3s", [P, 2])
        kb3m = sb("kb3m", [P, 4])
        eps = sb("eps", [P, 4])
        power = sb("power", [P, TT])

        hT = sbs("hT", [P, KT, NB, 2 * S])
        xN = sbs("xN", [P, TT, C])
        mint = sbs("mint", [P, NB, S], I32)
        m0 = sbs("m0", [P, NB, 2 * S])
        m3 = sbs("m3", [P, NB, S])
        s0 = sbs("s0", [P, KT, NB, J])
        big = sbs("big", [P, 2560])
        att = sbs("att", [P, 3104])
        v0 = sbs("v0s", [P, NB, 8, 48])
        v3 = sbs("v3s", [P, NB, 2, 2, 32])
        xaT = sbs("xaT", [P, KT, NB, S + 1])
        sx = sbs("sx", [P, KT, NB, S])
        tA = sbs("tA", [P, KT, NT])
        th = sbs("th", [P, 2, NT])
        kS = sbs("kS", [P, KT, NT])
        vS = sbs("vS", [P, KT, NT])
        rS = sbs("rS", [P, KT, NT])
        gs = sbs("gs", [P, KT, NT])
        wS = sbs("wS", [P, KT, NB, S + 1])
        n1 = sbs("n1", [P, TT, C])
        n2 = sbs("n2", [P, TT, C])
        n3 = sbs("n3", [P, TT, C])
        n4 = sbs("n4", [P, TT, C])
        n5 = sbs("n5", [P, TT, C])
        bns = sbs("bns", [P, TT, 6])
        mv = sbs("mv", [P, TT, 2])
        rstd = sbs("rstd", [P, TT])
        vtmp = sbs("vtmp", [P, TT])
        ssq = sbs("ssq", [P, TT])
        mx = sbs("mx", [P, 2, 8])
        rc = sbs("rc", [P, 2 * P])
        g1 = sbs("g1", [P, 64])
        g2 = sbs("g2", [P, 64])
        g3 = sbs("g3", [P, 64])
        ps = [[ctx.enter_context(nc.psum_tensor(f"ps{h}{k}", [P, 512], F32)) for k in range(4)] for h in range(2)]

        sc = [[a[:, 512 * i:512 * (i + 1)] for i in range(2)] for a in att]
        pt = [a[:, 1024:1536] for a in att]
        kT = [a[:, 1536:2560].rearrange("p (k b s) -> p k b s", k=2, b=NB) for a in att]
        kz3 = [a[:, 1536:2560].rearrange("p (b v s) -> p b v s", b=NB, v=4) for a in att]
        aB = [[a[:, 520 * i:520 * (i + 1)].rearrange("p (j b s) -> p j b s", j=2, b=NB) for i in range(2)] for a in att]
        st = [[a[:, 1040 + 520 * i:1560 + 520 * i].rearrange("p (j b s) -> p j b s", j=2, b=NB) for i in range(2)] for a in att]
        pd = [[a[:, 2080 + 512 * i:2592 + 512 * i].rearrange("p (j n) -> p j n", j=2) for i in range(2)] for a in att]
        qz = [a[:, 0:1024].rearrange("p (k b v s) -> p k b v s", k=2, v=2, b=NB) for a in big]
        q3T = [a[:, 0:512].rearrange("p (k n) -> p k n", k=2) for a in big]
        hid = [a[:, 0:2048].rearrange("p (m n) -> p m n", m=8) for a in big]
        xm = [[a[:, 512 * j:512 * (j + 1)].rearrange("p (k n) -> p k n", k=2) for j in range(5)] for a in big]
        ruk = [x[0] for x in xm]
        vx = [x[2:5] for x in xm]
        cv = [x[1] for x in xm]
        oT = [x[0] for x in xm]
        tS = [x[0] for x in xm]
        uS = [x[1] for x in xm]
        pbd = [x[2].rearrange("p k n -> p (k n)")[:, 0:256].rearrange("p (t n) -> p t n", t=2) for x in xm]
        ptb = [x[3].rearrange("p k n -> p (k n)")[:, 0:256].rearrange("p (t n) -> p t n", t=2) for x in xm]

        def flat(t):
            return t.rearrange("p k n -> p (k n)")

        def kn(bank):
            return bank[:, :].rearrange("p (k n) -> p k n", k=2)

        ld_w, ld_wb, ld_nat, ld_rows = sem("ld_w"), sem("ld_wb"), sem("ld_nat"), sem("ld_rows")
        set_pool, set_dve, set_pe, set_m = sem("set_pool"), sem("set_dve"), sem("set_pe"), sem("set_m")
        ld_h, ld_x, ld_m, ld_3, ld_s = sems("ld_h"), sems("ld_x"), sems("ld_m"), sems("ld_3"), sems("ld_s")
        st_out = sems("st_out")
        free_ps = sems("free_ps")
        qkv_ps = sems("qkv_ps")
        q0_sb, v0_sb, k0_sb = sems("q0_sb"), sems("v0_sb"), sems("k0_sb")
        s_ps, s_sb, s_mx, s_sub, s_exp = sems("s_ps"), sems("s_sb"), sems("s_mx"), sems("s_sub"), sems("s_exp")
        t_ps, t_sb, o_ps, o_rc, o_sb = sems("t_ps"), sems("t_sb"), sems("o_ps"), sems("o_rc"), sems("o_sb")
        m0_ok = sems("m0_ok")
        res = sems("res")
        pr_ps, pr_sb = sems("pr_ps"), sems("pr_sb")
        sq_ok, rs_a, rs_b = sems("sq_ok"), sems("rs_a"), sems("rs_b")
        bn_a, bn_b = sems("bn_a"), sems("bn_b")
        xh_ok = sems("xh_ok")
        xt_ps, xt_sb = sems("xt_ps"), sems("xt_sb")
        h_ps, h_sb = sems("h_ps"), sems("h_sb")
        sx_ok, xin_ok = sems("sx_ok"), sems("xin_ok")
        m1_ps, m1_sb, m2_ps, m2_mx, xm_ok = sems("m1_ps"), sems("m1_sb"), sems("m2_ps"), sems("m2_mx"), sems("xm_ok")
        pk_ps, pk_sb = sems("pk_ps"), sems("pk_sb")
        e1_ok, tg_ok = sems("e1_ok"), sems("tg_ok")
        ruk_ok, cb_ps, cv_ok = sems("ruk_ok"), sems("cb_ps"), sems("cv_ok")
        a0_ok, a_ok, sc_ok, pd_ok, rd_ps = sems("a0_ok"), sems("a_ok"), sems("sc_ok"), sems("pd_ok"), sems("rd_ps")
        vx_ok = [[sem(f"vx_ok_{h}{i}") for i in range(3)] for h in range(2)]
        ot_sb = sems("ot_sb")
        gn_d, gn_p, og_ok = sems("gn_d"), sems("gn_p"), sems("og_ok")
        ff_ps, ff_a, kk_ok, ff_d = sems("ff_ps"), sems("ff_a"), sems("kk_ok"), sems("ff_d")
        x2_ok = sems("x2_ok")
        l2_ps, l2_sb = sems("l2_ps"), sems("l2_sb")
        l2_mx = sems("l2_mx")
        kv3_ps, kv3_a, kv3_d = sems("kv3_ps"), sems("kv3_a"), sems("kv3_d")
        fin_ok = sems("fin_ok")

        block = ctx.enter_context(nc.Block())
        halves = range(2)

        @block.sync
        def _(sp):
            def load(n, h):
                b0 = n * (2 * NB) + h * NB
                sp.dma_start(hT[h][:, :, :, :], h_d[:, :, bass.ds(b0, NB), :]).then_inc(ld_h[h], 16)
                sp.dma_start(xN[h][:, :, :], x_d[:, bass.ds(n * (2 * TT) + h * TT, TT), :]).then_inc(ld_x[h], 16)
                sp.dma_start(mint[h][:, :, :], mask_d[bass.ds(b0, NB), :].unsqueeze(0).broadcast_to([P, NB, S])).then_inc(ld_m[h], 16)
                sp.dma_start(s0[h][:, :, :, :], s0_d[:, :, bass.ds(b0, NB), :]).then_inc(ld_s[h], 16)

            def load_mask(n, h):
                b0 = n * (2 * NB) + h * NB
                for d in range(2):
                    sp.dma_start(m3[h][64 * d:64 * d + 64, :, :],
                                 amask_d[bass.ds(b0, NB), :, :].rearrange("b q k -> q b k")).then_inc(ld_3[h], 16)

            def copy_v(h, q):
                m, jp = q // 4, q % 4
                for i in range(2):
                    src = vS[h][2 * jp + i::J, m, :].unsqueeze(1).broadcast_to([HT, J, NT])
                    sp.dma_start(vx[h][q % 3][:, i, :], src).then_inc(vx_ok[h][q % 3], 16)

            def stage(name, i, h, n):
                if name == "ruk":
                    sp.wait_ge(pk_sb[h], n * 6 + 3)
                    copy_v(h, 0)
                    sp.wait_ge(pk_ps[h], n * 6 + 5)
                    copy_v(h, 1)
                    sp.wait_ge(pk_ps[h], n * 6 + 6)
                    copy_v(h, 2)
                if name == "scan" and i + 3 < 8:
                    sp.wait_ge(a_ok[h], n * 8 + i + 1)
                    copy_v(h, i + 3)
                last = isinstance(n, int) and n == STEPS - 1
                if name == "q3" and not last:
                    sp.wait_ge(kv3_ps[h], n * 2 + 2)
                    load(n + 1, h)
                if name == "norm3":
                    if not last:
                        sp.wait_ge(s_sb[h], n * 16 + 16)
                        load_mask(n + 1, h)
                    sp.wait_ge(fin_ok[h], n * 4 + 4)
                    sp.dma_start(out_d[:, bass.ds(n * (2 * TT) + h * TT, TT), :], n5[h][:, :, :]).then_inc(st_out[h], 16)

            sp.dma_start(wa[:, :], wa_d).then_inc(ld_w, 16)
            load(0, 0)
            sp.dma_start(att[1][:, 0:nn], nat_d).then_inc(ld_nat, 16)
            sp.dma_start(rows[:, :, :], rows_d.unsqueeze(0).broadcast_to([P, len(ROWS), C])).then_inc(ld_rows, 16)
            sp.dma_start(wb[:, :], wb_d).then_inc(ld_wb, 16)
            load(0, 1)
            for h in halves:
                load_mask(0, h)
            run(sp, stage)
            for h in halves:
                sp.wait_ge(st_out[h], 16 * STEPS + 16)

        @block.tensor
        def _(pe):
            mm = nc.tensor.matmul

            def dense_T(out, weight, rhs):
                for m in range(2):
                    for k in range(2):
                        last = mm(out[:, m, :], weight(k)[:, m * P:(m + 1) * P], rhs(k), start=(k == 0), stop=(k == 1))
                return last

            def dense_N(out, lhs, weight, ks=2, tiles=range(TT)):
                for t in tiles:
                    for k in range(ks):
                        last = mm(out[:, t, :], lhs(k, t), weight(k), start=(k == 0), stop=(k == ks - 1))
                return last

            def turn_rows(h, bank, src):
                for t in range(TT):
                    for k in range(KT):
                        last = nc.tensor.transpose(kn(ps[h][bank])[:, k, t * P:(t + 1) * P], src[:, t, k * P:(k + 1) * P], ident)
                last.then_inc(xt_ps[h], 1)

            def tok(t):
                return slice(t * P, (t + 1) * P)

            def chunk_scores(n, h, layer, c):
                at, pair, r = layer * NCH + c, c // 4, c % 4
                g = slice(32 * r, 32 * r + 32)
                out = ps[h][c % 2]
                if c >= 2:
                    pe.wait_ge(s_sb[h], n * 16 + at - 1)
                for i in range(2):
                    b = 2 * pair + i
                    for k in range(2):
                        if layer == 0:
                            last = mm(out[:, (2 * i + k) * P:(2 * i + k + 1) * P], qz[h][g, k, b, :, :].rearrange("p v s -> p (v s)"),
                                      kT[h][g, k, b, :], start=True, stop=True)
                        else:
                            last = mm(out[k * S:(k + 1) * S, i * 4 * S:(i + 1) * 4 * S], q3T[h][g, k, b * S:(b + 1) * S],
                                      kz3[h][g, b, :, :].rearrange("p v s -> p (v s)"), start=True, stop=True)
                last.then_inc(s_ps[h], 1)

            def chunk_turn(n, h, layer, c):
                at = layer * NCH + c
                pe.wait_ge(s_exp[h], n * 16 + at + 1)
                if c >= 1:
                    pe.wait_ge(t_sb[h], n * 16 + at)
                for i in range(4):
                    last = nc.tensor.transpose(ps[h][2][:, i * P:(i + 1) * P], sc[h][c % 2][:, i * P:(i + 1) * P], ident)
                last.then_inc(t_ps[h], 1)

            def chunk_values(n, h, layer, c):
                at, pair, r = layer * NCH + c, c // 4, c % 4
                pe.wait_ge(t_sb[h], n * 16 + at + 1)
                if c == 4:
                    pe.wait_ge(o_sb[h], n * 16 + at)
                g = slice(32 * r, 32 * r + 32)
                for i in range(2):
                    b = 2 * pair + i
                    if layer == 0:
                        for k in range(2):
                            for v in range(2):
                                j = 2 * i + k
                                mm(ps[h][3][g, j * S:(j + 1) * S], v0[h][:, b, 4 * k + r, 16 * v:16 * v + 32],
                                   pt[h][:, (2 * j + v) * S:(2 * j + v + 1) * S], start=(v == 0), stop=(v == 1))
                    else:
                        for v in range(2):
                            mm(ps[h][3][g, i * P:(i + 1) * P], v3[h][:, b, r % 2, v, :],
                               pt[h][:, (2 * i + v) * P:(2 * i + v + 1) * P], start=(v == 0), stop=(v == 1))
                for v in range(2):
                    if layer == 0:
                        ones, p_v = w("ones0")[:, 16 * v:16 * v + 32], pt[h].rearrange("p (j v s) -> p v j s", j=4, v=2)[:, v, :, :]
                    else:
                        ones, p_v = w("ones3")[:, 32 * v:32 * v + 32], pt[h].rearrange("p (i v n) -> p v i n", i=2, v=2)[:, v, :, :]
                    last = mm(ps[h][3][g, 2 * P:4 * P], ones, p_v, start=(v == 0), stop=(v == 1))
                last.then_inc(o_ps[h], 1)

            def gather(n, h, q):
                m, jp = q // 4, q % 4
                out = kn(ps[h][3])
                if q == 0:
                    pe.wait_ge(cv_ok[h], n + 1)
                    pe.wait_ge(pk_sb[h], n * 6 + 4)
                    for k in range(KT):
                        mm(out[:, k, :], w("perm"), cv[h][:, k, :], start=(k == 0), stop=False, skip_group_check=True)
                pe.wait_ge(pd_ok[h], n * 8 + q + 1)
                for i in range(2):
                    last = mm(out[32 * jp:32 * jp + 32, m, :], w("sumh")[:, 32 * i:32 * i + 32], pd[h][q % 2][:, i, :], start=False,
                              stop=(q == 7 and i == 1), skip_group_check=True)
                last.then_inc(rd_ps[h], 1)

            MIX_BANK = (0, 1, 3, 2, 0)
            UP_BANK = (0, 1, 3, 2)

            def stage(name, i, h, n):
                if name == "q0":
                    pe.wait_ge(ld_h[h], n * 16 + 16)
                    pe.wait_ge(free_ps[h], n + 1)
                    dense_T(kn(ps[h][0]), lambda k: w("q0", k), lambda k: hT[h][:, k, :, S:2 * S]).then_inc(qkv_ps[h], 1)
                elif name == "k0":
                    for m in range(2):
                        for k in range(2):
                            last = mm(ps[h][1 + m][:, :], w("k0", k)[:, m * P:(m + 1) * P], hT[h][:, k, :, :], start=(k == 0), stop=(k == 1))
                    last.then_inc(qkv_ps[h], 1)
                elif name == "v0":
                    for b in range(NB):
                        if b == 2:
                            pe.wait_ge(q0_sb[h], n + 1)
                        for k in range(2):
                            last = mm(kn(ps[h][3 if b < 2 else 0])[:, b % 2, :], hT[h][:, k, b, :], w("v0", k), start=(k == 0), stop=(k == 1))
                        if b % 2:
                            last.then_inc(qkv_ps[h], 1)
                elif name in ("score0", "score1"):
                    layer = int(name[-1])
                    if i == 0:
                        if layer == 0:
                            pe.wait_ge(k0_sb[h], n + 1)
                            pe.wait_ge(v0_sb[h], n * 2 + 2)
                        else:
                            pe.wait_ge(kv3_a[h], n * 2 + 2)
                            pe.wait_ge(kv3_d[h], n + 1)
                    chunk_scores(n, h, layer, i)
                elif name in ("turn0", "turn1"):
                    chunk_turn(n, h, int(name[-1]), i)
                elif name in ("value0", "value1"):
                    chunk_values(n, h, int(name[-1]), i)
                elif name == "out0":
                    pe.wait_ge(o_sb[h], n * 16 + NCH)
                    dense_N(kn(ps[h][1]), lambda k, t: tA[h][:, k, tok(t)], lambda k: w("o0", k)).then_inc(pr_ps[h], 1)
                elif name == "zturn":
                    pe.wait_ge(xh_ok[h], n * 4 + 1)
                    turn_rows(h, 2, n2[h])
                elif name == "up":
                    if i == 0:
                        pe.wait_ge(ld_wb, 16)
                        pe.wait_ge(xt_sb[h], n * 6 + 1)
                    for m in range(2):
                        mt = 2 * i + m
                        for k in range(2):
                            last = mm(kn(ps[h][UP_BANK[i]])[:, m, :], w("w1", k)[:, mt * P:(mt + 1) * P], tA[h][:, k, :], start=(k == 0), stop=(k == 1))
                    last.then_inc(h_ps[h], 1)
                elif name == "down":
                    pe.wait_ge(h_sb[h], n * 4 + 4)
                    last = dense_N(kn(ps[h][0]), lambda k, t: hid[h][:, k, tok(t)], lambda k: w2[:, k, :], ks=8, tiles=[i])
                    if i == 1:
                        last.then_inc(pr_ps[h], 1)
                elif name == "xturn":
                    pe.wait_ge(xh_ok[h], n * 4 + 2)
                    turn_rows(h, 1, n3[h])
                elif name == "mix1":
                    pe.wait_ge(xin_ok[h], n + 1)
                    for m in range(2):
                        wide = P if m == 0 else 32
                        for k in range(2):
                            last = mm(kn(ps[h][2])[0:wide, m, :], w("m1", k)[:, m * P:m * P + wide], tA[h][:, k, :], start=(k == 0), stop=(k == 1))
                    last.then_inc(m1_ps[h], 1)
                elif name == "mix2":
                    if i == 0:
                        pe.wait_ge(m1_sb[h], n + 1)
                    if i == 4:
                        pe.wait_ge(m2_mx[h], n * 5 + 1)
                    g = slice(32 * (i % 4), 32 * (i % 4) + 32)
                    for m in range(2):
                        last = mm(kn(ps[h][MIX_BANK[i]])[:, m, :], w("m2", i // 4)[g, m * P:(m + 1) * P], th[h][g, i // 4, :], start=True, stop=True)
                    last.then_inc(m2_ps[h], 1)
                elif name == "pk":
                    pe.wait_ge(xm_ok[h], n * 5 + 1)
                    pe.wait_ge(m2_mx[h], n * 5 + 2)
                    dense_T(kn(ps[h][1]), lambda k: w("wk", k), lambda k: xm[h][0][:, k, :]).then_inc(pk_ps[h], 1)
                elif name == "pw1":
                    pe.wait_ge(xm_ok[h], n * 5 + 2)
                    pe.wait_ge(m2_mx[h], n * 5 + 3)
                    for k in range(2):
                        last = mm(kn(ps[h][3])[0:64, 0, :], w("td1", k), xm[h][1][:, k, :], start=(k == 0), stop=(k == 1))
                    last.then_inc(pk_ps[h], 1)
                elif name == "pv":
                    pe.wait_ge(xm_ok[h], n * 5 + 3)
                    pe.wait_ge(m2_mx[h], n * 5 + 4)
                    dense_T(kn(ps[h][2]), lambda k: w("wv", k), lambda k: xm[h][2][:, k, :]).then_inc(pk_ps[h], 1)
                elif name == "pw2":
                    pe.wait_ge(pk_sb[h], n * 6 + 2)
                    for m in range(2):
                        last = mm(kn(ps[h][3])[:, m, :], w("td2")[0:64, m * P:(m + 1) * P], th[h][0:64, 0, :], start=True, stop=True)
                    last.then_inc(pk_ps[h], 1)
                elif name == "pr":
                    pe.wait_ge(xm_ok[h], n * 5 + 4)
                    pe.wait_ge(m2_mx[h], n * 5 + 5)
                    dense_T(kn(ps[h][0]), lambda k: w("wr", k), lambda k: xm[h][3][:, k, :]).then_inc(pk_ps[h], 1)
                elif name == "pg":
                    pe.wait_ge(xm_ok[h], n * 5 + 5)
                    pe.wait_ge(pk_sb[h], n * 6 + 1)
                    dense_T(kn(ps[h][1]), lambda k: w("wg", k), lambda k: xm[h][4][:, k, :]).then_inc(pk_ps[h], 1)
                elif name == "ruk":
                    pe.wait_ge(ruk_ok[h], n + 1)
                    for m in range(2):
                        last = mm(kn(ps[h][2])[:, m, :], w("blk"), ruk[h][:, m, :], start=True, stop=True)
                    last.then_inc(cb_ps[h], 1)
                elif name == "sum":
                    gather(n, h, i)
                elif name == "oturn":
                    pe.wait_ge(ot_sb[h], n + 1)
                    for t in range(TT):
                        for k in range(KT):
                            last = nc.tensor.transpose(kn(ps[h][2])[:, t, k * P:(k + 1) * P], oT[h][:, k, tok(t)], ident)
                    last.then_inc(cb_ps[h], 1)
                elif name == "gturn":
                    pe.wait_ge(xh_ok[h], n * 4 + 3)
                    turn_rows(h, 0, n3[h])
                elif name == "outg":
                    pe.wait_ge(og_ok[h], n + 1)
                    dense_N(kn(ps[h][1]), lambda k, t: tA[h][:, k, tok(t)], lambda k: w("wo", k)).then_inc(pr_ps[h], 1)
                elif name == "cturn":
                    pe.wait_ge(xh_ok[h], n * 4 + 4)
                    turn_rows(h, 2, n3[h])
                elif name == "fk":
                    pe.wait_ge(ff_d[h], n * 2 + 1)
                    dense_T(kn(ps[h][0]), lambda k: w("fk", k), lambda k: tA[h][:, k, :]).then_inc(ff_ps[h], 1)
                elif name == "l2k":
                    dense_T(kn(ps[h][2]), lambda k: m_qk[:, k, :], lambda k: hT[h][:, k, :, 0:S]).then_inc(l2_ps[h], 1)
                elif name == "fr":
                    pe.wait_ge(ff_d[h], n * 2 + 2)
                    dense_N(kn(ps[h][3]), lambda k, t: th[h][:, k, tok(t)], lambda k: w("fr", k)).then_inc(ff_ps[h], 1)
                elif name == "l2v":
                    pe.wait_ge(ff_a[h], n * 2 + 1)
                    for b in range(NB):
                        g = slice(64 * (b % 2), 64 * (b % 2) + 64)
                        for k in range(2):
                            last = mm(kn(ps[h][0])[g, b // 2, :], hT[h][:, k, b, 0:S], m_vo[:, k, :], start=(k == 0), stop=(k == 1))
                    last.then_inc(l2_ps[h], 1)
                elif name == "fv":
                    pe.wait_ge(kk_ok[h], n + 1)
                    dense_N(kn(ps[h][1]), lambda k, t: kS[h][:, k, tok(t)], lambda k: w("fv", k)).then_inc(pr_ps[h], 1)
                elif name == "x2turn":
                    pe.wait_ge(x2_ok[h], n + 1)
                    pe.wait_ge(tg_ok[h], n * 2 + 2)
                    turn_rows(h, 3, n2[h])
                elif name == "l2s":
                    pe.wait_ge(xt_sb[h], n * 6 + 5)
                    pe.wait_ge(l2_sb[h], n * 3 + 1)
                    for b in range(NB):
                        g = slice(64 * (b % 2), 64 * (b % 2) + 64)
                        for k in range(2):
                            last = mm(ps[h][1][g, (b // 2) * S:(b // 2) * S + S], tA[h][:, k, b * S:(b + 1) * S], tS[h][:, k, b * S:(b + 1) * S],
                                      start=(k == 0), stop=(k == 1))
                    last.then_inc(l2_ps[h], 1)
                elif name == "l2p":
                    pe.wait_ge(ff_a[h], n * 2 + 2)
                    pe.wait_ge(l2_sb[h], n * 3 + 2)
                    for t in range(TT):
                        last = nc.tensor.transpose(ps[h][0][:, t * P:(t + 1) * P], pbd[h][:, t, :], ident)
                    last.then_inc(l2_ps[h], 1)
                elif name == "l2o":
                    pe.wait_ge(l2_sb[h], n * 3 + 3)
                    for t in range(TT):
                        last = mm(kn(ps[h][2])[:, t, :], ptb[h][:, t, :], uS[h][:, t, :], start=True, stop=True)
                    last.then_inc(pr_ps[h], 1)
                elif name == "k3":
                    for k in range(2):
                        last = mm(ps[h][1][:, 0:NT], w("k3", k), hT[h][:, k, :, 0:S], start=(k == 0), stop=(k == 1))
                    last.then_inc(kv3_ps[h], 1)
                elif name == "v3":
                    for b in range(NB):
                        for e in range(2):
                            for k in range(2):
                                last = mm(ps[h][0][64 * e:64 * e + 64, b * 64:(b + 1) * 64], hT[h][:, k, b, 0:S], w("v3", k),
                                          start=(k == 0), stop=(k == 1))
                    last.then_inc(kv3_ps[h], 1)
                elif name == "x3turn":
                    pe.wait_ge(pr_sb[h], n * 6 + 5)
                    turn_rows(h, 3, n1[h])
                elif name == "q3":
                    pe.wait_ge(xt_sb[h], n * 6 + 6)
                    dense_T(kn(ps[h][2]), lambda k: w("q3", k), lambda k: tA[h][:, k, :]).then_inc(l2_ps[h], 1)
                elif name == "out3":
                    pe.wait_ge(o_sb[h], n * 16 + 2 * NCH)
                    dense_N(kn(ps[h][1]), lambda k, t: tA[h][:, k, tok(t)], lambda k: w("o3", k)).then_inc(pr_ps[h], 1)

            nat = att[1][:, 0:nn].rearrange("p (m k n) -> p m k n", m=4, k=2)
            pe.wait_ge(ld_nat, 16)
            for m in range(2):
                for k in range(2):
                    mm(kn(ps[1][0])[:, m, :], nat[:, 1, k, m * P:(m + 1) * P], nat[:, 0, k, :], start=(k == 0), stop=(k == 1))
                for k in range(2):
                    last = mm(kn(ps[1][1])[:, m, :], nat[:, 2, k, m * P:(m + 1) * P], nat[:, 3, k, :], start=(k == 0), stop=(k == 1))
            last.then_inc(set_pe, 1)
            pe.wait_ge(ld_w, 16)
            pe.wait_ge(set_m, 1)
            pe.wait_ge(set_pool, 2)
            pe.wait_ge(set_dve, 1)
            run(pe, stage)

        @block.scalar
        def _(act):
            A = nc.scalar.activation

            def seqs(v):
                return v.rearrange("p (b s) -> p b s", b=NB)

            def affine(h, bank, name_w, name_b, dst):
                for k in range(2):
                    last = A(dst(k), seqs(kn(ps[h][bank])[:, k, :]), ACT.Identity, bias=vec(name_b, k), scale=vec(name_w, k))
                last.then_inc(xt_sb[h], 1)

            def stage(name, i, h, n):
                if name == "q0":
                    act.wait_ge(qkv_ps[h], n * 4 + 1)
                    for k in range(2):
                        for v in range(2):
                            last = A(qz[h][:, k, :, v, :], seqs(kn(ps[h][0])[:, k, :]), ACT.Identity, bias=qb0m[:, k, v:v + 1], scale=vec("par", v))
                    last.then_inc(q0_sb[h], 1)
                elif name == "k0":
                    act.wait_ge(qkv_ps[h], n * 4 + 2)
                    for m in range(2):
                        last = A(kT[h][:, m, :, :].rearrange("p b s -> p (b s)"), ps[h][1 + m][:, :], ACT.Identity, bias=vec("kb0", m))
                    last.then_inc(k0_sb[h], 1)
                elif name in ("score0", "score1"):
                    at = n * 16 + int(name[-1]) * NCH
                    act.wait_ge(s_sub[h], at + i + 1)
                    A(sc[h][i % 2], sc[h][i % 2], ACT.Exp).then_inc(s_exp[h], 1)
                elif name in ("turn0", "turn1"):
                    at = n * 16 + int(name[-1]) * NCH
                    act.wait_ge(t_ps[h], at + i + 1)
                    if i >= 1:
                        act.wait_ge(o_ps[h], at + i)
                    A(pt[h], ps[h][2][:, :], ACT.Copy).then_inc(t_sb[h], 1)
                elif name == "norm0":
                    act.wait_ge(pr_sb[h], n * 6 + 1)
                    for t in range(TT):
                        last = A(n3[h][:, t, :], n1[h][:, t, :], ACT.Square, scale=1.0 / C ** 0.5, accum_out=ssq[h][:, t:t + 1])
                    last.then_inc(sq_ok[h], 1)
                elif name == "zturn":
                    act.wait_ge(xt_ps[h], n * 6 + 1)
                    for k in range(2):
                        last = A(tA[h][:, k, :], kn(ps[h][2])[:, k, :], ACT.Identity, scale=vec("pn", k))
                    last.then_inc(xt_sb[h], 1)
                elif name == "up":
                    act.wait_ge(h_ps[h], n * 4 + i + 1)
                    for m in range(2):
                        last = A(hid[h][:, 2 * i + m, :], kn(ps[h][(0, 1, 3, 2)[i]])[:, m, :], ACT.Gelu_apprx_tanh, bias=vec("b1", 2 * i + m))
                    last.then_inc(h_sb[h], 1)
                elif name == "xturn":
                    act.wait_ge(xt_ps[h], n * 6 + 2)
                    A(xaT[h][:, :, :, 0:1], hT[h][:, :, :, 1:2], ACT.Copy)
                    affine(h, 1, "ln1w", "ln1b", lambda k: xaT[h][:, k, :, 1:S + 1])
                elif name == "mix1":
                    act.wait_ge(m1_ps[h], n + 1)
                    A(th[h][:, 0, :], kn(ps[h][2])[:, 0, :], ACT.Tanh)
                    A(th[h][0:32, 1, :], kn(ps[h][2])[0:32, 1, :], ACT.Tanh).then_inc(m1_sb[h], 1)
                elif name == "pk":
                    act.wait_ge(pk_ps[h], n * 6 + 1)
                    A(flat(kS[h]), ps[h][1][:, :], ACT.Copy).then_inc(pk_sb[h], 1)
                elif name == "pw1":
                    act.wait_ge(pk_ps[h], n * 6 + 2)
                    A(th[h][0:64, 0, :], kn(ps[h][3])[0:64, 0, :], ACT.Tanh).then_inc(pk_sb[h], 1)
                elif name == "pv":
                    act.wait_ge(pk_ps[h], n * 6 + 3)
                    A(flat(vS[h]), ps[h][2][:, :], ACT.Copy).then_inc(pk_sb[h], 1)
                elif name == "pw2":
                    act.wait_ge(pk_ps[h], n * 6 + 4)
                    act.wait_ge(m2_mx[h], n * 5 + 5)
                    for k in range(2):
                        last = A(sx[h][:, k, :, :], seqs(kn(ps[h][3])[:, k, :]), ACT.Exp, bias=vec("td", k))
                    last.then_inc(e1_ok[h], 1)
                    act.wait_ge(e1_ok[h], n + 1)
                    for k in range(2):
                        last = A(wS[h][:, k, :, 1:S + 1], sx[h][:, k, :, :], ACT.Exp, scale=-1.0)
                    last.then_inc(pk_sb[h], 1)
                elif name == "pr":
                    act.wait_ge(pk_ps[h], n * 6 + 5)
                    A(flat(rS[h]), ps[h][0][:, :], ACT.Copy).then_inc(pk_sb[h], 1)
                elif name == "pg":
                    act.wait_ge(pk_ps[h], n * 6 + 6)
                    A(flat(gs[h]), ps[h][1][:, :], ACT.Tanh, scale=0.5).then_inc(tg_ok[h], 1)
                elif name == "scan":
                    m, jp = i // 4, i % 4
                    if i == 0:
                        act.wait_ge(ld_s[h], n * 16 + 16)
                    if i >= 2:
                        act.wait_ge(sc_ok[h], n * 8 + i - 1)
                    A(aB[h][i % 2][:, :, :, 0], s0[h][:, m, :, 2 * jp:2 * jp + 2].rearrange("p b j -> p j b"), ACT.Copy).then_inc(a0_ok[h], 1)
                elif name == "oturn":
                    act.wait_ge(rd_ps[h], n * 8 + 8)
                    A(flat(oT[h]), ps[h][3][:, :], ACT.Copy).then_inc(ot_sb[h], 1)
                elif name == "gnorm" and i == 0:
                    act.wait_ge(gn_d[h], n * GN + 3)
                    A(flat(n3[h]), flat(n2[h]), ACT.Square).then_inc(gn_p[h], 1)
                elif name == "gturn":
                    act.wait_ge(xt_ps[h], n * 6 + 3)
                    affine(h, 0, "gnw", "gnb", lambda k: seqs(tA[h][:, k, :]))
                elif name == "cturn":
                    act.wait_ge(xt_ps[h], n * 6 + 4)
                    A(xaT[h][:, :, :, 0:1], hT[h][:, :, :, 0:1], ACT.Copy)
                    affine(h, 2, "ln2w", "ln2b", lambda k: xaT[h][:, k, :, 1:S + 1])
                elif name == "fk":
                    act.wait_ge(ff_ps[h], n * 2 + 1)
                    A(flat(rS[h]), ps[h][0][:, :], ACT.Relu).then_inc(ff_a[h], 1)
                elif name == "fr":
                    act.wait_ge(ff_ps[h], n * 2 + 2)
                    A(flat(gs[h]), ps[h][3][:, :], ACT.Tanh, scale=0.5).then_inc(tg_ok[h], 1)
                elif name == "l2k":
                    act.wait_ge(l2_ps[h], n * 5 + 1)
                    A(flat(tS[h]), ps[h][2][:, :], ACT.Copy).then_inc(l2_sb[h], 1)
                elif name == "l2v":
                    act.wait_ge(l2_ps[h], n * 5 + 2)
                    A(flat(uS[h]), ps[h][0][:, :], ACT.Copy).then_inc(l2_sb[h], 1)
                elif name == "x2turn":
                    act.wait_ge(xt_ps[h], n * 6 + 5)
                    A(flat(tA[h]), ps[h][3][:, :], ACT.Copy).then_inc(xt_sb[h], 1)
                elif name == "l2s":
                    act.wait_ge(l2_mx[h], n * 3 + 2)
                    for t in range(TT):
                        for e in range(2):
                            g = slice(64 * e, 64 * e + 64)
                            last = A(pbd[h][g, t, 64 * e:64 * e + 64], ps[h][1][g, t * S:(t + 1) * S], ACT.Exp,
                                     bias=vtmp[h][g, t:t + 1], scale=1.0 / 16.0, accum_out=ssq[h][g, t:t + 1])
                    last.then_inc(ff_a[h], 1)
                elif name == "l2p":
                    act.wait_ge(l2_ps[h], n * 5 + 4)
                    A(ptb[h].rearrange("p t n -> p (t n)"), ps[h][0][:, 0:2 * P], ACT.Copy).then_inc(l2_sb[h], 1)
                elif name == "k3":
                    act.wait_ge(kv3_ps[h], n * 2 + 1)
                    for v in range(4):
                        last = A(kz3[h][:, :, v, :], seqs(ps[h][1][:, 0:NT]), ACT.Identity, bias=kb3m[:, v:v + 1], scale=vec("sub", v))
                    last.then_inc(kv3_a[h], 1)
                elif name == "x3turn":
                    act.wait_ge(xt_ps[h], n * 6 + 6)
                    A(flat(tA[h]), ps[h][3][:, :], ACT.Copy).then_inc(xt_sb[h], 1)
                elif name == "q3":
                    act.wait_ge(l2_ps[h], n * 5 + 5)
                    for k in range(2):
                        last = A(q3T[h][:, k, :], kn(ps[h][2])[:, k, :], ACT.Identity, bias=qb3s[:, k:k + 1], scale=W3 ** -0.5)
                    last.then_inc(kv3_a[h], 1)

            act.wait_ge(ld_w, 16)
            act.wait_ge(set_dve, 1)
            act.wait_ge(set_pool, 2)
            run(act, stage)

        @block.gpsimd
        def _(pool):
            G = nc.gpsimd

            def inverse_root(n, h, m, src, at):
                G.tensor_tensor(vtmp[h][:, :], src, eps[:, at:at + TT], ALU.add).then_inc(rs_a[h], 1)
                pool.wait_ge(rs_a[h], n * 4 + m + 1)
                G.tensor_tensor(rstd[h][:, :], vtmp[h][:, :], power[:, 0:TT], ALU.pow).then_inc(rs_b[h], 1)

            def shift(n, h, m):
                pool.wait_ge(xt_sb[h], n * 6 + 2 * (m + 1))
                G.tensor_tensor(sx[h][:, :, :, :].rearrange("p k b s -> p (k b) s"),
                                xaT[h][:, :, :, 0:S].rearrange("p k b s -> p (k b) s"),
                                xaT[h][:, :, :, 1:S + 1].rearrange("p k b s -> p (k b) s"), ALU.subtract).then_inc(sx_ok[h], 1)

            def stage(name, i, h, n):
                if name == "v0":
                    pool.wait_ge(ld_rows, 16)
                    pool.wait_ge(ld_x[h], n * 16 + 16)
                    G.tensor_tensor(n1[h][:, :, :], xN[h][:, :, :], row("out_b", TT), ALU.add).then_inc(res[h], 1)
                elif name == "norm0":
                    pool.wait_ge(sq_ok[h], n + 1)
                    inverse_root(n, h, 0, ssq[h][:, :], 0)
                elif name == "zturn":
                    G.tensor_tensor(n4[h][:, :, :], xN[h][:, :, :], row("mlp_b2", TT), ALU.add).then_inc(res[h], 1)
                elif name == "norm1":
                    pool.wait_ge(bn_b[h], n * 3 + 1)
                    inverse_root(n, h, 1, mv[h][:, :, 1], 2)
                elif name == "xturn":
                    shift(n, h, 0)
                elif name == "mix2":
                    pool.wait_ge(m2_mx[h], n * 5 + i + 1)
                    v = flat(xm[h][i]).rearrange("p (k s) -> p k s", s=S)
                    G.tensor_tensor(v, v, xaT[h][:, :, :, 1:S + 1].rearrange("p k b s -> p (k b) s"), ALU.add).then_inc(xm_ok[h], 1)
                elif name == "scan":
                    m = i // 4
                    pool.wait_ge(sc_ok[h], n * 8 + i + 1)
                    if i == 0:
                        pool.wait_ge(pk_sb[h], n * 6 + 5)
                    if i >= 2:
                        pool.wait_ge(rd_ps[h], n * 8 + i - 1)
                    r = rS[h][:, m, :].rearrange("p (b s) -> p b s", b=NB).unsqueeze(1).broadcast_to([P, 2, NB, S])
                    G.tensor_tensor(pd[h][i % 2].rearrange("p j (b s) -> p j b s", b=NB), st[h][i % 2][:, :, :, 0:S], r, ALU.mult).then_inc(pd_ok[h], 1)
                elif name == "gturn":
                    pool.wait_ge(xt_sb[h], n * 6 + 3)
                    pool.wait_ge(pk_sb[h], n * 6 + 6)
                    G.tensor_tensor(tA[h][:, :, :], tA[h][:, :, :], gs[h][:, :, :], ALU.mult).then_inc(og_ok[h], 1)
                elif name == "norm2":
                    pool.wait_ge(bn_b[h], n * 3 + 2)
                    inverse_root(n, h, 2, mv[h][:, :, 1], 2)
                elif name == "cturn":
                    shift(n, h, 1)
                elif name == "fk":
                    pool.wait_ge(ff_a[h], n * 2 + 1)
                    G.tensor_tensor(kS[h][:, :, :], rS[h][:, :, :], rS[h][:, :, :], ALU.mult).then_inc(kk_ok[h], 1)
                elif name == "fv":
                    pool.wait_ge(pr_sb[h], n * 6 + 4)
                    G.tensor_tensor(n2[h][:, :, :], n3[h][:, :, :], n4[h][:, :, :], ALU.add).then_inc(x2_ok[h], 1)
                elif name == "l2o":
                    pool.wait_ge(pr_sb[h], n * 6 + 5)
                    G.tensor_tensor(n2[h][:, :, :], n1[h][:, :, :], row("bo", TT), ALU.add).then_inc(res[h], 1)
                elif name == "norm3":
                    pool.wait_ge(bn_b[h], n * 3 + 3)
                    inverse_root(n, h, 3, mv[h][:, :, 1], 0)
                    pool.wait_ge(fin_ok[h], n * 4 + 1)
                    pool.wait_ge(st_out[h], n * 16 + 16)
                    G.tensor_tensor(n4[h][:, :, :], n3[h][:, :, :], row("gamma", TT), ALU.mult).then_inc(fin_ok[h], 1)
                    pool.wait_ge(fin_ok[h], n * 4 + 2)
                    G.tensor_tensor(n5[h][:, :, :], n4[h][:, :, :], row("beta", TT), ALU.add).then_inc(fin_ok[h], 2)

            for h in halves:
                G.memset(wS[h][:, :, :, :], 0.0)
                G.memset(v3[h][:, :, :, :, :], 0.0)
                G.memset(v0[h][:, :, :, :], 0.0)
                G.memset(m0[h][:, :, S:2 * S], 0.0)
            G.memset(eps[:, 0:2], 1e-6)
            G.memset(eps[:, 2:4], 1e-5)
            for h in halves:
                G.memset(n5[h][:, 0, 0:1], 0.0).then_inc(st_out[h], 16)
            G.memset(power[:, :], -0.5).then_inc(set_pool, 2)
            run(pool, stage)

        @block.vector
        def _(dve):
            V = nc.vector

            def softmax_scores(n, h, layer, c):
                groups = 4 if layer == 0 else 8
                at = n * 16 + layer * NCH
                pair = c // 4
                dve.wait_ge(s_ps[h], at + c + 1)
                if c >= 2:
                    dve.wait_ge(t_ps[h], at + c - 1)
                if layer == 0:
                    m = m0[h][:, 2 * pair:2 * pair + 2, :].unsqueeze(2).broadcast_to([P, 2, 2, 2 * S])
                else:
                    m = m3[h][:, 2 * pair:2 * pair + 2, :].unsqueeze(2).broadcast_to([P, 2, 4, S])
                k = groups // 2
                V.tensor_tensor(sc[h][c % 2].rearrange("p (b k s) -> p b k s", b=2, k=k),
                                ps[h][c % 2][:, :].rearrange("p (b k s) -> p b k s", b=2, k=k), m, ALU.add).then_inc(s_sb[h], 1)
                dve.wait_ge(s_sb[h], at + c + 1)
                V.tensor_reduce(mx[h][:, c % 2, 0:groups], sc[h][c % 2].rearrange("p (g k) -> p g k", g=groups), AXX, ALU.max).then_inc(s_mx[h], 1)
                dve.wait_ge(s_mx[h], at + c + 1)
                v = sc[h][c % 2].rearrange("p (g k) -> p g k", g=groups)
                V.tensor_tensor(v, v, mx[h][:, c % 2, 0:groups].unsqueeze(2).broadcast_to([P, groups, 512 // groups]), ALU.subtract).then_inc(s_sub[h], 1)

            def divide(n, h, layer, pair):
                at = n * 16 + layer * NCH + 4 * pair + 4
                dve.wait_ge(o_ps[h], at)
                V.reciprocal(rc[h][:, :], ps[h][3][:, 2 * P:4 * P]).then_inc(o_rc[h], 4)
                dve.wait_ge(o_rc[h], at)
                V.tensor_tensor(tA[h][:, :, pair * P:(pair + 1) * P].rearrange("p k (b s) -> p b k s", b=2),
                                ps[h][3][:, 0:2 * P].rearrange("p (b k s) -> p b k s", b=2, k=2),
                                rc[h][:, :].rearrange("p (b k s) -> p b k s", b=2, k=2), ALU.mult).then_inc(o_sb[h], 4)

            def layer_stats(n, h, m, src):
                for t in range(TT):
                    last = V.bn_stats(bns[h][:, t, :], src[:, t, :])
                last.then_inc(bn_a[h], 1)
                stats = n * 3 + m + 1
                dve.wait_ge(set_pool, 2)
                dve.wait_ge(bn_a[h], stats)
                for t in range(TT):
                    last = V.bn_aggr(mv[h][:, t, :], bns[h][:, t, :])
                last.then_inc(bn_b[h], 1)

            def layer_norm(n, h, m, dst, src):
                dve.wait_ge(rs_b[h], n * 4 + m + 1)
                for t in range(TT):
                    last = V.tensor_scalar(dst[:, t, :], src[:, t, :], mv[h][:, t, 0:1], rstd[h][:, t:t + 1], ALU.subtract, ALU.mult)
                return last

            def chain(n, h, k, ins):
                ins.then_inc(gn_d[h], 1)
                dve.wait_ge(gn_d[h], n * GN + k)

            def inverse_root(n, h, k, y, v, t):
                chain(n, h, k, V.tensor_scalar(t.bitcast(I32), v.bitcast(I32), 1, None, ALU.logical_shift_right))
                chain(n, h, k + 1, V.tensor_scalar(y.bitcast(I32), t.bitcast(I32), -1.0, float(0x5F3759DF), ALU.mult, ALU.add))
                for s in range(NEWTON):
                    chain(n, h, k + 2 + 3 * s, V.tensor_tensor(t, y, y, ALU.mult))
                    chain(n, h, k + 3 + 3 * s, V.scalar_tensor_tensor(t, t, -0.5, v, ALU.mult, ALU.mult))
                    chain(n, h, k + 4 + 3 * s, V.scalar_tensor_tensor(y, t, 1.5, y, ALU.add, ALU.mult))

            def stage(name, i, h, n):
                if name == "k0":
                    dve.wait_ge(ld_m[h], n * 16 + 16)
                    V.tensor_scalar(m0[h][:, :, 0:S], mint[h][:, :, :], 0.0, MASKED, ALU.is_equal, ALU.mult).then_inc(m0_ok[h], 1)
                elif name == "v0":
                    for j in range(2):
                        dve.wait_ge(qkv_ps[h], n * 4 + 3 + j)
                        for b in range(2):
                            last = V.tensor_tensor(v0[h][:, 2 * j + b, :, :].rearrange("p g (v c) -> p g v c", c=W0)[:, :, 0:3:2, :],
                                                   kn(ps[h][0 if j else 3])[:, b, :].rearrange("p (g v c) -> p g v c", v=2, c=W0),
                                                   rows[:, ROWS.index("kv_b"), :].rearrange("p (g v c) -> p g v c", v=2, c=W0), ALU.add)
                        last.then_inc(v0_sb[h], 1)
                    dve.wait_ge(m0_ok[h], n + 1)
                elif name in ("score0", "score1"):
                    if name == "score1" and i == 0:
                        dve.wait_ge(ld_3[h], n * 32 + 32)
                    softmax_scores(n, h, int(name[-1]), i)
                elif name in ("value0", "value1") and i % 4 == 3:
                    divide(n, h, int(name[-1]), i // 4)
                elif name == "norm0":
                    dve.wait_ge(pr_ps[h], n * 6 + 1)
                    dve.wait_ge(res[h], n * 3 + 1)
                    V.tensor_tensor(n1[h][:, :, :], kn(ps[h][1]), n1[h][:, :, :], ALU.add).then_inc(pr_sb[h], 1)
                    dve.wait_ge(rs_b[h], n * 4 + 1)
                    for t in range(TT):
                        last = V.tensor_scalar(n2[h][:, t, :], n1[h][:, t, :], rstd[h][:, t:t + 1], None, ALU.mult)
                    last.then_inc(xh_ok[h], 1)
                elif name == "norm1":
                    dve.wait_ge(pr_ps[h], n * 6 + 2)
                    dve.wait_ge(res[h], n * 3 + 2)
                    V.tensor_tensor(n4[h][:, :, :], kn(ps[h][0]), n4[h][:, :, :], ALU.add).then_inc(pr_sb[h], 1)
                    dve.wait_ge(pr_sb[h], n * 6 + 2)
                    layer_stats(n, h, 0, n4[h])
                    layer_norm(n, h, 1, n3[h], n4[h]).then_inc(xh_ok[h], 1)
                elif name == "xturn":
                    dve.wait_ge(sx_ok[h], n * 2 + 1)
                    for k in range(2):
                        last = V.scalar_tensor_tensor(tA[h][:, k, :].rearrange("p (b s) -> p b s", b=NB), sx[h][:, k, :, :], vec("maax", k),
                                                      xaT[h][:, k, :, 1:S + 1], ALU.mult, ALU.add)
                    last.then_inc(xin_ok[h], 1)
                elif name == "mix2":
                    dve.wait_ge(m2_ps[h], n * 5 + i + 1)
                    for k in range(2):
                        last = V.scalar_tensor_tensor(xm[h][i][:, k, :], kn(ps[h][(0, 1, 3, 2, 0)[i]])[:, k, :], vec("stack", 2 * i + k),
                                                      sx[h][:, k, :, :].rearrange("p b s -> p (b s)"), ALU.add, ALU.mult)
                    last.then_inc(m2_mx[h], 1)
                elif name == "pr":
                    dve.wait_ge(pk_sb[h], n * 6 + 5)
                    for k in range(2):
                        last = V.scalar_tensor_tensor(ruk[h][:, k, :], rS[h][:, k, :], vec("u", k), kS[h][:, k, :], ALU.mult, ALU.mult)
                    last.then_inc(ruk_ok[h], 1)
                elif name == "pg":
                    dve.wait_ge(tg_ok[h], n * 2 + 1)
                    V.scalar_tensor_tensor(flat(gs[h][:, :, :]), flat(gs[h][:, :, :]), 1.0, ps[h][1][:, :], ALU.add, ALU.mult).then_inc(pk_sb[h], 1)
                elif name == "ruk":
                    dve.wait_ge(cb_ps[h], n * 2 + 1)
                    V.tensor_tensor(cv[h], kn(ps[h][2]), vS[h][:, :, :], ALU.mult).then_inc(cv_ok[h], 1)
                elif name == "scan":
                    dve.wait_ge(vx_ok[h][i % 3], (n * (3, 3, 2)[i % 3] + i // 3 + 1) * 32)
                    if i >= 2:
                        dve.wait_ge(pd_ok[h], n * 8 + i - 1)
                    k = kS[h][:, i // 4, :].rearrange("p (b s) -> p b s", b=NB).unsqueeze(1).broadcast_to([P, 2, NB, S])
                    V.tensor_tensor(aB[h][i % 2][:, :, :, 1:S + 1], vx[h][i % 3].rearrange("p j (b s) -> p j b s", b=NB), k, ALU.mult).then_inc(a_ok[h], 1)
                    dve.wait_ge(a_ok[h], n * 8 + i + 1)
                    dve.wait_ge(a0_ok[h], n * 8 + i + 1)
                    for j in range(2):
                        last = V.tensor_tensor_scan(st[h][i % 2][:, j, :, :].rearrange("p b s -> p (b s)"),
                                                    wS[h][:, i // 4, :, :].rearrange("p b s -> p (b s)"),
                                                    aB[h][i % 2][:, j, :, :].rearrange("p b s -> p (b s)"), 0.0, ALU.mult, ALU.add)
                    last.then_inc(sc_ok[h], 1)
                elif name == "gnorm" and i == 0:
                    o = ps[h][2][:, :].rearrange("p (g j h) -> p g h j", g=4, j=J)
                    dve.wait_ge(cb_ps[h], n * 2 + 2)
                    chain(n, h, 1, V.tensor_reduce(g3[h][:, :].rearrange("p (g h) -> p g h", g=4), o, AXX, ALU.add))
                    chain(n, h, 2, V.tensor_scalar(g2[h][:, :], g3[h][:, :], -1.0 / J, None, ALU.mult))
                    V.tensor_tensor(n2[h][:, :, :].rearrange("p t (m h j) -> p (t m) h j", m=2, j=J), o,
                                    g2[h][:, :].rearrange("p (g h) -> p g h", g=4).unsqueeze(3).broadcast_to([P, 4, HT, J]), ALU.add).then_inc(gn_d[h], 1)
                elif name == "gnorm" and i == 1:
                    dve.wait_ge(gn_p[h], n + 1)
                    chain(n, h, 4, V.tensor_reduce(g3[h][:, :], n3[h][:, :, :].rearrange("p t (h j) -> p (t h) j", j=J), AXX, ALU.add))
                    chain(n, h, 5, V.tensor_scalar(g2[h][:, :], g3[h][:, :], 1.0 / J, 1e-5, ALU.mult, ALU.add))
                elif name == "gnorm" and i == 2:
                    inverse_root(n, h, 6, g1[h][:, :], g2[h][:, :], g3[h][:, :])
                elif name == "gnorm" and i == 3:
                    V.tensor_tensor(n3[h][:, :, :].rearrange("p t (h j) -> p (t h) j", j=J), n2[h][:, :, :].rearrange("p t (h j) -> p (t h) j", j=J),
                                    g1[h][:, :].unsqueeze(2).broadcast_to([P, 64, J]), ALU.mult).then_inc(xh_ok[h], 1)
                elif name == "norm2":
                    dve.wait_ge(pr_ps[h], n * 6 + 3)
                    V.tensor_tensor(n4[h][:, :, :], kn(ps[h][1]), n4[h][:, :, :], ALU.add).then_inc(pr_sb[h], 1)
                    dve.wait_ge(pr_sb[h], n * 6 + 3)
                    layer_stats(n, h, 1, n4[h])
                    layer_norm(n, h, 2, n3[h], n4[h]).then_inc(xh_ok[h], 1)
                elif name == "cturn":
                    dve.wait_ge(sx_ok[h], n * 2 + 2)
                    for name_, dst in (("fmk", tA), ("fmr", th)):
                        for k in range(2):
                            last = V.scalar_tensor_tensor(dst[h][:, k, :].rearrange("p (b s) -> p b s", b=NB), sx[h][:, k, :, :], vec(name_, k),
                                                          xaT[h][:, k, :, 1:S + 1], ALU.mult, ALU.add)
                        last.then_inc(ff_d[h], 1)
                    V.memset(pbd[h], 0.0)
                elif name == "fv":
                    dve.wait_ge(pr_ps[h], n * 6 + 4)
                    dve.wait_ge(tg_ok[h], n * 2 + 2)
                    V.scalar_tensor_tensor(flat(n3[h][:, :, :]), flat(gs[h][:, :, :]), 1.0, ps[h][1][:, :], ALU.add, ALU.mult).then_inc(pr_sb[h], 1)
                elif name == "l2s":
                    dve.wait_ge(l2_ps[h], n * 5 + 3)
                    V.tensor_reduce(rstd[h][:, :], ps[h][1][:, 0:2 * S].rearrange("p (t s) -> p t s", t=2), AXX, ALU.max).then_inc(l2_mx[h], 1)
                    dve.wait_ge(l2_mx[h], n * 3 + 1)
                    V.tensor_scalar(vtmp[h][:, :], rstd[h][:, :], -1.0 / 16.0, None, ALU.mult).then_inc(l2_mx[h], 1)
                elif name == "l2p":
                    dve.wait_ge(ff_a[h], n * 2 + 2)
                    V.reciprocal(rstd[h][:, :], ssq[h][:, :]).then_inc(l2_mx[h], 1)
                elif name == "l2o":
                    dve.wait_ge(pr_ps[h], n * 6 + 5)
                    dve.wait_ge(x2_ok[h], n + 1)
                    dve.wait_ge(l2_mx[h], n * 3 + 3)
                    for t in range(TT):
                        last = V.scalar_tensor_tensor(n1[h][:, t, :], kn(ps[h][2])[:, t, :], rstd[h][:, t:t + 1], n2[h][:, t, :], ALU.mult, ALU.add)
                    last.then_inc(pr_sb[h], 1)
                elif name == "v3":
                    dve.wait_ge(kv3_ps[h], n * 2 + 2)
                    for e in range(2):
                        g = slice(64 * e, 64 * e + 64)
                        for v in range(2):
                            o = (2 * v + e) * W3
                            last = V.tensor_tensor(v3[h][g, :, :, v, o:o + W3],
                                                   ps[h][0][g, 0:NT].rearrange("p (b r x) -> p b r x", b=NB, r=2)[:, :, :, o:o + W3],
                                                   w("bv3")[g, :].rearrange("p (r x) -> p r x", r=2)[:, :, o:o + W3].unsqueeze(1).broadcast_to([64, NB, 2, W3]), ALU.add)
                    last.then_inc(kv3_d[h], 1)
                elif name == "norm3":
                    dve.wait_ge(pr_ps[h], n * 6 + 6)
                    dve.wait_ge(res[h], n * 3 + 3)
                    V.tensor_tensor(n1[h][:, :, :], kn(ps[h][1]), n2[h][:, :, :], ALU.add).then_inc(pr_sb[h], 1)
                    dve.wait_ge(pr_sb[h], n * 6 + 6)
                    layer_stats(n, h, 2, n1[h])
                    layer_norm(n, h, 3, n3[h], n1[h]).then_inc(fin_ok[h], 1)
                    V.tensor_copy(g1[h][:, 0:1], vec("alpha")).then_inc(free_ps[h], 1)

            dve.wait_ge(set_pool, 2)
            dve.wait_ge(ld_w, 16)
            for k in range(2):
                V.tensor_scalar(qb0m[:, k, :], wa[:, vec0 + VEC["par"][0]:vec0 + VEC["par"][0] + 2], vec("qb0", k), None, ALU.mult)
            V.tensor_scalar(qb3s[:, :], wa[:, vec0 + VEC["qb3"][0]:vec0 + VEC["qb3"][0] + 2], W3 ** -0.5, None, ALU.mult)
            V.tensor_scalar(kb3m[:, :], wa[:, vec0 + VEC["sub"][0]:vec0 + VEC["sub"][0] + 4], vec("kb3"), None, ALU.mult)
            for name in ("gnw", "gnb"):
                c = vec0 + VEC[name][0]
                V.tensor_scalar(wa[:, c:c + 2], wa[:, c:c + 2], 0.5, None, ALU.mult)
            V.tensor_scalar(w("fv"), w("fv"), 0.5, None, ALU.mult).then_inc(set_dve, 1)
            for h in halves:
                V.tensor_copy(g1[h][:, 0:1], vec("alpha")).then_inc(free_ps[h], 1)
            dve.wait_ge(ld_rows, 16)
            dve.wait_ge(set_pe, 1)
            V.tensor_copy(flat(m_qk[:, :, :]), ps[1][0][:, :])
            V.tensor_scalar(flat(m_vo[:, :, :]), ps[1][1][:, :], vec("alpha"), None, ALU.mult).then_inc(set_m, 1)
            run(dve, stage)


def pack(weights, table):
    return np.concatenate([weights[name] for name, _ in table], axis=1)


def kernel(**inputs):
    import concourse.bacc as bacc
    from concourse.bass_utils import run_bass_kernel_spmd

    a = {k: np.asarray(v) for k, v in inputs.items()}
    f = np.float32
    ctx, x = a["ctx_2048"], a["x"]
    L0, L1, L2, L3 = ({k[len(p):]: v for k, v in a.items() if k.startswith(p)}
                      for p in ("L0_xattn_", "L1_xattn_", "L2_xattn_", "L3_xattn_"))

    def fold(m):
        tiles = -(-m.shape[0] // P)
        m = np.concatenate([m, np.zeros((tiles * P - m.shape[0], m.shape[1]), f)])
        return m.reshape(tiles, P, -1).transpose(1, 0, 2).reshape(P, -1)

    def cols(v):
        return v.reshape(-1, P).T

    p = np.arange(P)
    tile = np.arange(2)[:, None]
    q3 = ((p % 64 // 8 * 4 + tile * 2 + p // 64) * 8 + p % 8).reshape(-1)

    kvw = L0["kv_w"].reshape(C, C, 2)
    kvb = L0["kv_b"].reshape(C, 2)
    head = p // J
    same = (head[:, None] == head[None, :]).astype(f)
    weights = {
        "ident": np.eye(P, dtype=f), "q0": fold(L0["q_w"]), "k0": fold(kvw[:, :, 0]), "v0": fold(kvw[:, :, 1]),
        "o0": fold(L0["out_w"]), "w1": fold(L0["mlp_w1"]), "w2": fold(L0["mlp_w2"]),
        "m1": fold(L1["maa_w1"]), "m2": fold(L1["maa_w2"].reshape(5 * 32, C)),
        "td1": fold(L1["td_w1"]), "td2": fold(L1["td_w2"]),
        "wk": fold(L1["Wk"].T), "wv": fold(L1["Wv"].T), "wr": fold(L1["Wr"].T), "wg": fold(L1["Wg"].T),
        "wo": fold(L1["Wo"].T), "fk": fold(L1["Wfk"].T), "fr": fold(L1["Wfr"].T), "fv": fold(L1["Wfv"].T),
        "q3": fold(L3["Wq"][:, q3]), "k3": fold(np.concatenate([L3["Wk"], L3["Wk"]], axis=1)), "v3": fold(L3["Wv"]),
        "o3": fold(L3["Wo"][q3]),
        "l2q": fold(L2["w_q"]), "l2k": fold(L2["w_k"]), "l2v": fold(L2["w_v"]), "l2o": fold(L2["w_o"].T),
        "ones3": (2 * np.arange(2)[None, :, None] + p[:, None, None] // S == (np.arange(32) // W3)[None, None, :]).astype(f).reshape(P, -1),
        "ones0": np.broadcast_to((np.arange(48) // W0 != 1).astype(f), (P, 48)),
        "bv3": np.broadcast_to(L3["bv"], (P, 64)),
        "sumh": np.concatenate([head[:, None] + HT * i == np.arange(2 * HT) for i in range(2)], axis=1).astype(f), "blk": same,
        "perm": (p[:, None] == (p % HT * J + p // HT)[None, :]).astype(f),
    }
    vectors = {
        "qb0": cols(L0["q_b"]), "kb0": cols(kvb[:, 0]), "pn": cols(L0["postnorm_w"]),
        "b1": cols(L0["mlp_b1"]), "ln1w": cols(L1["ln1_w"]), "ln1b": cols(L1["ln1_b"]), "ln2w": cols(L1["ln2_w"]),
        "ln2b": cols(L1["ln2_b"]), "maax": cols(L1["maa_x"]), "stack": cols(L1["maa_stack"]),
        "td": cols(L1["time_decay"]), "u": cols(L1["u"]), "gnw": cols(L1["gn_w"]), "gnb": cols(L1["gn_b"]),
        "fmk": cols(L1["ffn_maa_k"]), "fmr": cols(L1["ffn_maa_r"]), "qb3": cols(L3["bq"][q3]),
        "kb3": cols(np.concatenate([L3["bk"], L3["bk"]])), 
        "par": (p[:, None] % 32 // 16 == np.arange(2)).astype(f) / W0,
        "sub": (p[:, None] % 32 // 8 == np.arange(4)).astype(f),
        "alpha": np.broadcast_to(L2["alpha"].reshape(1, 1), (P, 1)),
    }
    vec = np.concatenate([vectors[n] for n in VEC], axis=1)
    weights["vec"] = np.concatenate([vec, np.zeros((P, 64 - vec.shape[1]), f)], axis=1)

    h = np.concatenate([ctx, x], axis=1).transpose(2, 0, 1).reshape(KT, P, B, 2 * S).transpose(1, 0, 2, 3)
    arrays = {
        "h": h, "x": x.reshape(-1, P, C).transpose(1, 0, 2), "mask": a["mask_BxS2_ik0"],
        "amask": a["mask_Bx1xSxS2_ff0"].reshape(B, S, S),
        "s0": ctx[:, 2:2 + J].reshape(B, KT, P, J).transpose(2, 1, 0, 3),
        "wa": pack(weights, WEIGHTS_A), "wb": pack(weights, WEIGHTS_B), "nat": pack(weights, NAT),
        "rows": np.stack([kvb[:, 1], L0["out_b"], L0["mlp_b2"], L3["bo"], L3["gamma"], L3["beta"]]),
    }
    arrays = {k: np.ascontiguousarray(v) for k, v in arrays.items()}

    nc = bacc.Bacc("TRN2", target_bir_lowering=False, num_devices=1)
    args = [nc.dram_tensor(f"in_{k}", v.shape, mybir.dt.from_np(v.dtype), kind="ExternalInput").ap() for k, v in arrays.items()]
    out = nc.dram_tensor("result", (P, B * S // P, C), F32, kind="ExternalOutput").ap()
    build(nc, *args, out)
    got = run_bass_kernel_spmd(nc, [{f"in_{k}": v for k, v in arrays.items()}], core_ids=[0]).results[0]["result"]
    return np.asarray(got).transpose(1, 0, 2).reshape(B, S, C)
```
